# Optimizing a Trainium2 kernel written in Bass

```python
import numpy as np
import jax
import jax.numpy as jnp

def _softmax(x, axis=-1):
    return jax.nn.softmax(x, axis=axis)

def _gelu(x):
    return jax.nn.gelu(x, approximate=True)

def _silu(x):
    return jax.nn.silu(x)

def _sigmoid(x):
    return jax.nn.sigmoid(x)

def _layernorm(x, axis=-1, eps=1e-05):
    m = jnp.mean(x, axis=axis, keepdims=True)
    v = jnp.var(x, axis=axis, keepdims=True)
    return (x - m) / jnp.sqrt(v + eps)

def _scatter_add(tgt, idx, src, axis=0):
    return tgt.at[idx].add(src)

def _segment_sum(src, seg, n):
    return jax.ops.segment_sum(src, seg, n)
kernel_name = 'mk_decoder_postln_d1_seqx_r8_a629aa'

def setup_inputs(seed: int=0):
    np.random.seed(seed)
    _w = jnp.asarray

    def _rec_inputs():
        import jax
        import jax.numpy as jnp
        _rk = jax.random.key(seed)
        x = -0.0005207 + 1.001 * jax.random.normal(jax.random.fold_in(_rk, 1), (64, 64, 128), jnp.float32)
        _lenS = 64 - jax.random.randint(jax.random.fold_in(_rk, 7), (64,), 0, max(1, 64 // 4) + 1, jnp.int32)
        _lenS2 = 64 - jax.random.randint(jax.random.fold_in(_rk, 8), (64,), 0, max(1, 64 // 4) + 1, jnp.int32)
        _ctx_512P = jax.random.normal(jax.random.fold_in(_rk, 11), (64, 16, 64), jnp.float32)
        _ctx_512c = jax.random.dirichlet(jax.random.fold_in(_rk, 511), 0.3 * jnp.ones((16,), jnp.float32), (64, 64))
        _ctx_512t = jnp.einsum('bsk,bkd->bsd', _ctx_512c, _ctx_512P)
        _ctx_512t = _ctx_512t * jax.lax.rsqrt(jnp.mean(jnp.square(_ctx_512t)) + 1e-12) * 0.953939
        ctx_512 = 0.502058 + 0.29099 * (_ctx_512t + 0.3 * jax.random.normal(jax.random.fold_in(_rk, 611), (64, 64, 64), jnp.float32))
        itok_BxS2xS_0_7 = jax.random.randint(jax.random.fold_in(_rk, 12), (64, 64, 64), 0, 8, jnp.int32)
        return (x, ctx_512, itok_BxS2xS_0_7)
    x, ctx_512, itok_BxS2xS_0_7 = _rec_inputs()

    def _L0_attn_setup():
        import jax, jax.numpy as jnp
        import numpy as np
        B, L, D, H = (8, 256, 128, 16)
        HD = D // H
        K = 4
        EPS = 1e-06

        def _short_conv(x, w, b):
            xp = jnp.pad(x, ((0, 0), (K - 1, 0), (0, 0)))
            y = b
            for i in range(K):
                y = y + w[:, i] * xp[:, i:i + x.shape[1], :]
            return y

        def _delta_rule(q, k, v, beta):
            qT = jnp.moveaxis(q, 1, 0)
            kT = jnp.moveaxis(k, 1, 0)
            vT = jnp.moveaxis(v, 1, 0)
            bT = jnp.moveaxis(beta, 1, 0)

            def step(S, inp):
                q_t, k_t, v_t, b_t = inp
                pred = jnp.einsum('bhk,bhkv->bhv', k_t, S)
                S = S + b_t[..., None, None] * (k_t[..., None] * (v_t - pred)[..., None, :])
                o_t = jnp.einsum('bhk,bhkv->bhv', q_t, S)
                return (S, o_t)
            S0 = jnp.zeros((q.shape[0], H, HD, HD), q.dtype)
            _, o = jax.lax.scan(step, S0, (qT, kT, vT, bT))
            return jnp.moveaxis(o, 0, 1)

        def _rmsnorm(x, w):
            return x * jax.lax.rsqrt(jnp.mean(x * x, axis=-1, keepdims=True) + EPS) * w
        key = jax.random.key(seed)
        ks = jax.random.split(key, 12)
        s = 0.02
        inp = {'x': jax.random.normal(ks[0], (B, L, D), jnp.float32), 'Wq': jax.random.normal(ks[1], (D, D), jnp.float32) * s, 'bq': jnp.zeros((D,), jnp.float32), 'Wk': jax.random.normal(ks[2], (D, D), jnp.float32) * s, 'bk': jnp.zeros((D,), jnp.float32), 'Wv': jax.random.normal(ks[3], (D, D), jnp.float32) * s, 'bv': jnp.zeros((D,), jnp.float32), 'Wbeta': jax.random.normal(ks[4], (H, D), jnp.float32) * s, 'bbeta': jnp.zeros((H,), jnp.float32), 'Wo': jax.random.normal(ks[5], (D, D), jnp.float32) * s, 'bo': jnp.zeros((D,), jnp.float32), 'wq_conv': jax.random.normal(ks[6], (D, K), jnp.float32) * 0.2, 'bq_conv': jnp.zeros((D,), jnp.float32), 'wk_conv': jax.random.normal(ks[7], (D, K), jnp.float32) * 0.2, 'bk_conv': jnp.zeros((D,), jnp.float32), 'wv_conv': jax.random.normal(ks[8], (D, K), jnp.float32) * 0.2, 'bv_conv': jnp.zeros((D,), jnp.float32), 'norm_w': jnp.ones((HD,), jnp.float32)}
        return inp
    _L0_attn_all = _L0_attn_setup()
    _L0_attn_in = {k: v for k, v in _L0_attn_all.items() if k in ('Wq', 'bq', 'Wk', 'bk', 'Wv', 'bv', 'Wbeta', 'bbeta', 'Wo', 'bo', 'wq_conv', 'bq_conv', 'wk_conv', 'bk_conv', 'wv_conv', 'bv_conv', 'norm_w')}
    del _L0_attn_all

    def _L0_xattn_setup():
        import jax, jax.numpy as jnp
        import numpy as np
        key = jax.random.key(seed)
        k1, k2, k3, k4, k5 = jax.random.split(key, 5)
        B, K, S, E, I, D = (4, 2, 64, 8, 128, 256)
        x = jax.random.normal(k1, (B, S, I), dtype=jnp.float32)
        weights = jax.random.uniform(k2, (B, K, S), dtype=jnp.float32)
        ensembles = jax.random.randint(k3, (B, K, S), 0, E, dtype=jnp.int64)
        lim1 = float(np.sqrt(6.0 / (D + I)))
        proj_in = jax.random.uniform(k4, (E, D, I), dtype=jnp.float32, minval=-lim1, maxval=lim1)
        proj_out = jax.random.uniform(k5, (E, I, D), dtype=jnp.float32, minval=-lim1, maxval=lim1)
        return {'x': x, 'weights': weights, 'ensembles': ensembles, 'proj_in': proj_in, 'proj_out': proj_out}
    _L0_xattn_all = _L0_xattn_setup()
    _L0_xattn_in = {k: v for k, v in _L0_xattn_all.items() if k in ('proj_in', 'proj_out')}
    del _L0_xattn_all

    def _L0_ffn_setup():
        import jax, jax.numpy as jnp
        import numpy as np
        from jax import lax
        N_HEADS = 16
        TOP_K = 2
        N_EXPERTS = 8

        def layer_norm(x, w, b, eps=1e-05):
            mu = jnp.mean(x, axis=-1, keepdims=True)
            var = jnp.mean(jnp.square(x - mu), axis=-1, keepdims=True)
            return (x - mu) * lax.rsqrt(var + eps) * w + b

        def attention(x, w_qkv, b_qkv, w_o, b_o):
            B, T, D = x.shape
            dh = D // N_HEADS
            qkv = x @ w_qkv + b_qkv
            q, k, v = jnp.split(qkv, 3, axis=-1)
            q = q.reshape(B, T, N_HEADS, dh)
            k = k.reshape(B, T, N_HEADS, dh)
            v = v.reshape(B, T, N_HEADS, dh)
            scores = jnp.einsum('bqhd,bkhd->bhqk', q, k) / jnp.sqrt(jnp.float32(dh)).astype(x.dtype)
            probs = jax.nn.softmax(scores, axis=-1)
            ctx = jnp.einsum('bhqk,bkhd->bqhd', probs, v).reshape(B, T, D)
            return ctx @ w_o + b_o

        def moe_ff(x, w_gate, w1, b1, w2, b2):
            B, T, D = x.shape
            t = x.reshape(B * T, D)
            probs = jax.nn.softmax(t @ w_gate, axis=-1)
            tw, ti = lax.top_k(probs, TOP_K)
            tw = tw / jnp.sum(tw, axis=-1, keepdims=True)
            out = jnp.zeros_like(t)
            for e in range(N_EXPERTS):
                we = jnp.sum(jnp.where(ti == e, tw, 0.0), axis=-1)
                h = jax.nn.gelu(t @ w1[e] + b1[e]) @ w2[e] + b2[e]
                out = out + we[:, None] * h
            return out.reshape(B, T, D)
        key = jax.random.key(seed)
        ks = jax.random.split(key, 8)
        B, T, D, H, E = (4, 64, 128, 512, 8)
        s = lambda d: 1.0 / np.sqrt(d)
        return {'x': jax.random.normal(ks[0], (B, T, D), jnp.float32), 'ln1_w': jnp.ones((D,), jnp.float32), 'ln1_b': jnp.zeros((D,), jnp.float32), 'ln2_w': jnp.ones((D,), jnp.float32), 'ln2_b': jnp.zeros((D,), jnp.float32), 'w_qkv': jax.random.normal(ks[1], (D, 3 * D), jnp.float32) * s(D), 'b_qkv': jnp.zeros((3 * D,), jnp.float32), 'w_o': jax.random.normal(ks[2], (D, D), jnp.float32) * s(D), 'b_o': jnp.zeros((D,), jnp.float32), 'w_gate': jax.random.normal(ks[3], (D, E), jnp.float32) * s(D), 'w1': jax.random.normal(ks[4], (E, D, H), jnp.float32) * s(D), 'b1': jnp.zeros((E, H), jnp.float32), 'w2': jax.random.normal(ks[5], (E, H, D), jnp.float32) * s(H), 'b2': jnp.zeros((E, D), jnp.float32)}
    _L0_ffn_all = _L0_ffn_setup()
    _L0_ffn_in = {k: v for k, v in _L0_ffn_all.items() if k in ('ln1_w', 'ln1_b', 'ln2_w', 'ln2_b', 'w_qkv', 'b_qkv', 'w_o', 'b_o', 'w_gate', 'w1', 'b1', 'w2', 'b2')}
    del _L0_ffn_all
    return {'x': x, 'ctx_512': ctx_512, 'itok_BxS2xS_0_7': itok_BxS2xS_0_7, 'L0_attn_Wq': _L0_attn_in['Wq'], 'L0_attn_bq': _L0_attn_in['bq'], 'L0_attn_Wk': _L0_attn_in['Wk'], 'L0_attn_bk': _L0_attn_in['bk'], 'L0_attn_Wv': _L0_attn_in['Wv'], 'L0_attn_bv': _L0_attn_in['bv'], 'L0_attn_Wbeta': _L0_attn_in['Wbeta'], 'L0_attn_bbeta': _L0_attn_in['bbeta'], 'L0_attn_Wo': _L0_attn_in['Wo'], 'L0_attn_bo': _L0_attn_in['bo'], 'L0_attn_wq_conv': _L0_attn_in['wq_conv'], 'L0_attn_bq_conv': _L0_attn_in['bq_conv'], 'L0_attn_wk_conv': _L0_attn_in['wk_conv'], 'L0_attn_bk_conv': _L0_attn_in['bk_conv'], 'L0_attn_wv_conv': _L0_attn_in['wv_conv'], 'L0_attn_bv_conv': _L0_attn_in['bv_conv'], 'L0_attn_norm_w': _L0_attn_in['norm_w'], 'L0_xattn_proj_in': _L0_xattn_in['proj_in'], 'L0_xattn_proj_out': _L0_xattn_in['proj_out'], 'L0_ffn_ln1_w': _L0_ffn_in['ln1_w'], 'L0_ffn_ln1_b': _L0_ffn_in['ln1_b'], 'L0_ffn_ln2_w': _L0_ffn_in['ln2_w'], 'L0_ffn_ln2_b': _L0_ffn_in['ln2_b'], 'L0_ffn_w_qkv': _L0_ffn_in['w_qkv'], 'L0_ffn_b_qkv': _L0_ffn_in['b_qkv'], 'L0_ffn_w_o': _L0_ffn_in['w_o'], 'L0_ffn_b_o': _L0_ffn_in['b_o'], 'L0_ffn_w_gate': _L0_ffn_in['w_gate'], 'L0_ffn_w1': _L0_ffn_in['w1'], 'L0_ffn_b1': _L0_ffn_in['b1'], 'L0_ffn_w2': _L0_ffn_in['w2'], 'L0_ffn_b2': _L0_ffn_in['b2']}

def reference(x, ctx_512, itok_BxS2xS_0_7, L0_attn_Wq, L0_attn_bq, L0_attn_Wk, L0_attn_bk, L0_attn_Wv, L0_attn_bv, L0_attn_Wbeta, L0_attn_bbeta, L0_attn_Wo, L0_attn_bo, L0_attn_wq_conv, L0_attn_bq_conv, L0_attn_wk_conv, L0_attn_bk_conv, L0_attn_wv_conv, L0_attn_bv_conv, L0_attn_norm_w, L0_xattn_proj_in, L0_xattn_proj_out, L0_ffn_ln1_w, L0_ffn_ln1_b, L0_ffn_ln2_w, L0_ffn_ln2_b, L0_ffn_w_qkv, L0_ffn_b_qkv, L0_ffn_w_o, L0_ffn_b_o, L0_ffn_w_gate, L0_ffn_w1, L0_ffn_b1, L0_ffn_w2, L0_ffn_b2):
    import jax
    import jax.numpy as jnp

    def _L0_attn_ref(x, Wq, bq, Wk, bk, Wv, bv, Wbeta, bbeta, Wo, bo, wq_conv, bq_conv, wk_conv, bk_conv, wv_conv, bv_conv, norm_w):
        import jax, jax.numpy as jnp
        import numpy as np
        B, L, D, H = (8, 256, 128, 16)
        HD = D // H
        K = 4
        EPS = 1e-06

        def _short_conv(x, w, b):
            xp = jnp.pad(x, ((0, 0), (K - 1, 0), (0, 0)))
            y = b
            for i in range(K):
                y = y + w[:, i] * xp[:, i:i + x.shape[1], :]
            return y

        def _delta_rule(q, k, v, beta):
            qT = jnp.moveaxis(q, 1, 0)
            kT = jnp.moveaxis(k, 1, 0)
            vT = jnp.moveaxis(v, 1, 0)
            bT = jnp.moveaxis(beta, 1, 0)

            def step(S, inp):
                q_t, k_t, v_t, b_t = inp
                pred = jnp.einsum('bhk,bhkv->bhv', k_t, S)
                S = S + b_t[..., None, None] * (k_t[..., None] * (v_t - pred)[..., None, :])
                o_t = jnp.einsum('bhk,bhkv->bhv', q_t, S)
                return (S, o_t)
            S0 = jnp.zeros((q.shape[0], H, HD, HD), q.dtype)
            _, o = jax.lax.scan(step, S0, (qT, kT, vT, bT))
            return jnp.moveaxis(o, 0, 1)

        def _rmsnorm(x, w):
            return x * jax.lax.rsqrt(jnp.mean(x * x, axis=-1, keepdims=True) + EPS) * w
        Bx, Lx, Dx = x.shape
        k = _short_conv(x @ Wk.T + bk, wk_conv, bk_conv)
        q = _short_conv(x @ Wq.T + bq, wq_conv, bq_conv)
        v = _short_conv(x @ Wv.T + bv, wv_conv, bv_conv)
        beta = jax.nn.sigmoid(x @ Wbeta.T + bbeta)
        k = k.reshape(Bx, Lx, H, HD)
        q = q.reshape(Bx, Lx, H, HD)
        v = v.reshape(Bx, Lx, H, HD)
        v = jax.nn.silu(v)
        knorm = jnp.linalg.norm(k, axis=-1, keepdims=True)
        qnorm = jnp.linalg.norm(q, axis=-1, keepdims=True)
        k = k / (knorm + EPS)
        v = v / (knorm + EPS)
        q = q / (qnorm + EPS)
        o = _delta_rule(q, k, v, beta)
        o = _rmsnorm(o, norm_w)
        o = o.reshape(Bx, Lx, Dx)
        return o @ Wo.T + bo

    def _L0_xattn_ref(x, weights, ensembles, proj_in, proj_out):
        import jax, jax.numpy as jnp
        import numpy as np
        E = proj_in.shape[0]
        h = jax.nn.relu(jnp.einsum('edi,bsi->bsed', proj_in, x))
        o = jnp.einsum('eid,bsed->bsei', proj_out, h)
        onehot = jax.nn.one_hot(ensembles, E, dtype=x.dtype)
        gate = jnp.einsum('bks,bkse->bse', weights, onehot)
        return jnp.einsum('bsei,bse->bsi', o, gate)

    def _L0_ffn_ref(x, ln1_w, ln1_b, ln2_w, ln2_b, w_qkv, b_qkv, w_o, b_o, w_gate, w1, b1, w2, b2):
        import jax, jax.numpy as jnp
        import numpy as np
        from jax import lax
        N_HEADS = 16
        TOP_K = 2
        N_EXPERTS = 8

        def layer_norm(x, w, b, eps=1e-05):
            mu = jnp.mean(x, axis=-1, keepdims=True)
            var = jnp.mean(jnp.square(x - mu), axis=-1, keepdims=True)
            return (x - mu) * lax.rsqrt(var + eps) * w + b

        def attention(x, w_qkv, b_qkv, w_o, b_o):
            B, T, D = x.shape
            dh = D // N_HEADS
            qkv = x @ w_qkv + b_qkv
            q, k, v = jnp.split(qkv, 3, axis=-1)
            q = q.reshape(B, T, N_HEADS, dh)
            k = k.reshape(B, T, N_HEADS, dh)
            v = v.reshape(B, T, N_HEADS, dh)
            scores = jnp.einsum('bqhd,bkhd->bhqk', q, k) / jnp.sqrt(jnp.float32(dh)).astype(x.dtype)
            probs = jax.nn.softmax(scores, axis=-1)
            ctx = jnp.einsum('bhqk,bkhd->bqhd', probs, v).reshape(B, T, D)
            return ctx @ w_o + b_o

        def moe_ff(x, w_gate, w1, b1, w2, b2):
            B, T, D = x.shape
            t = x.reshape(B * T, D)
            probs = jax.nn.softmax(t @ w_gate, axis=-1)
            tw, ti = lax.top_k(probs, TOP_K)
            tw = tw / jnp.sum(tw, axis=-1, keepdims=True)
            out = jnp.zeros_like(t)
            for e in range(N_EXPERTS):
                we = jnp.sum(jnp.where(ti == e, tw, 0.0), axis=-1)
                h = jax.nn.gelu(t @ w1[e] + b1[e]) @ w2[e] + b2[e]
                out = out + we[:, None] * h
            return out.reshape(B, T, D)
        h = x + attention(layer_norm(x, ln1_w, ln1_b), w_qkv, b_qkv, w_o, b_o)
        return h + moe_ff(layer_norm(h, ln2_w, ln2_b), w_gate, w1, b1, w2, b2)
    x = _layernorm(x + _L0_attn_ref(x, L0_attn_Wq, L0_attn_bq, L0_attn_Wk, L0_attn_bk, L0_attn_Wv, L0_attn_bv, L0_attn_Wbeta, L0_attn_bbeta, L0_attn_Wo, L0_attn_bo, L0_attn_wq_conv, L0_attn_bq_conv, L0_attn_wk_conv, L0_attn_bk_conv, L0_attn_wv_conv, L0_attn_bv_conv, L0_attn_norm_w), axis=-1)
    x = _layernorm(x + _L0_xattn_ref(x, ctx_512, itok_BxS2xS_0_7, L0_xattn_proj_in, L0_xattn_proj_out), axis=-1)
    x = _layernorm(x + _L0_ffn_ref(x, L0_ffn_ln1_w, L0_ffn_ln1_b, L0_ffn_ln2_w, L0_ffn_ln2_b, L0_ffn_w_qkv, L0_ffn_b_qkv, L0_ffn_w_o, L0_ffn_b_o, L0_ffn_w_gate, L0_ffn_w1, L0_ffn_b1, L0_ffn_w2, L0_ffn_b2), axis=-1)
    return x

_drawn_inputs = setup_inputs


def setup_inputs(seed=0):
    import zlib

    import numpy as np

    out = dict(_drawn_inputs(seed))
    spreads = {'L0_attn_bq': (0.0, 0.1),
     'L0_attn_bk': (0.0, 0.1),
     'L0_attn_bv': (0.0, 0.1),
     'L0_attn_bbeta': (0.0, 0.708),
     'L0_attn_bo': (0.0, 0.1),
     'L0_attn_bq_conv': (0.0, 0.1),
     'L0_attn_bk_conv': (0.0, 0.1),
     'L0_attn_bv_conv': (0.0, 0.1),
     'L0_attn_norm_w': (1.0, 0.2),
     'L0_ffn_ln1_w': (1.0, 0.2),
     'L0_ffn_ln1_b': (0.0, 0.1),
     'L0_ffn_ln2_w': (1.0, 0.2),
     'L0_ffn_ln2_b': (0.0, 0.1),
     'L0_ffn_b_qkv': (0.0, 0.1),
     'L0_ffn_b_o': (0.0, 0.1),
     'L0_ffn_b1': (0.0, 0.365),
     'L0_ffn_b2': (0.0, 0.1)}
    factors = {}
    for name, (base, spread) in spreads.items():
        noise = np.random.default_rng([zlib.crc32(name.encode()), seed]).standard_normal(out[name].shape)
        drawn = base * np.exp(spread * noise) if base else spread * noise
        out[name] = jnp.asarray(drawn.astype(out[name].dtype))
    for name, factor in factors.items():
        out[name] = (out[name] * factor).astype(out[name].dtype)
    return out
```

```python
from contextlib import ExitStack

import concourse.bass as bass
from concourse import mybir

F32 = mybir.dt.float32
I32 = mybir.dt.int32
ALU = mybir.AluOpType
ACT = mybir.ActivationFunctionType
AX = mybir.AxisListType

P = 128
B, S, D = 64, 64, 128
NTOK = B * S
H, HD = 16, 8
TAPS = 4
GT = 512
G = NTOK // GT
GB = GT // S
TILES = GT // P
PAD = S + TAPS - 1
CH = GT // B
NCH = S // CH
HC = CH // 2
XE, XH = 8, 256
XC = XH // P
XK = 64
NE, FH = 8, 512
FC = FH // P
NORM_EPS = 1e-6
LN_EPS = 1e-5
CREDIT = 2

K_, Q_, V_, O_ = 0, 1, 2, 3
COLS = ["L0_attn_bk", "L0_attn_bq", "L0_attn_bv", "L0_attn_bk_conv", "L0_attn_bq_conv", "L0_attn_bv_conv",
        "L0_ffn_ln1_w", "L0_ffn_ln1_b", "L0_ffn_ln2_w", "L0_ffn_ln2_b"]
C_LN1W, C_LN1B, C_LN2W, C_LN2B = 6, 7, 8, 9
C_BETA, C_NORMW, C_FOLD, C_QKV, C_EPS, C_ONE, C_LNEPS = 10, 11, 12, 15, 18, 19, 20
NCOL = 24


def done(g):
    return g + (1 + CREDIT)


def free2(g):
    return g + 1


def free1(g):
    return g + 2


def dram_ap(t, offset, dims):
    return bass.AP(tensor=t.tensor, offset=offset, ap=[list(d) for d in dims])


def decoder_layer(nc, a, out):
    with ExitStack() as whole:
        def keep(name, shape, dt=F32):
            return whole.enter_context(nc.sbuf_tensor(name, shape, dt))

        def sem(name):
            return whole.enter_context(nc.semaphore(name))

        w = {
            "ident": keep("ident", [P, P]),
            "headsel": keep("headsel", [P, H]),
            "halfpow": keep("halfpow", [P, TILES * H]),
            "wT": keep("wT", [P, 4, P]),
            "wbT": keep("wbT", [P, H, HD]),
            "pinT": keep("pinT", [P, XE * XC, P]),
            "poutT": keep("poutT", [P, XE * XC, P]),
            "cols": keep("cols", [P, NCOL]),
            "taps": keep("taps", [P, 3, TAPS]),
            "bo_row": keep("bo_row", [P, D]),
        }
        scr = {n: nc.dram_tensor(n, shape, F32, kind="Internal").ap()
               for n, shape in (("k_scr", [P, NTOK]), ("q_scr", [P, NTOK]), ("gate_scr", [XE, NTOK]),
                                ("x1_scr", [P, NTOK]), ("x2_scr", [P, NTOK]))}
        w["idle_dve"], w["idle_pool"] = keep("idle_dve", [P, 1]), keep("idle_pool", [P, 1])
        weights_stage(nc, a, w, sem)

        w["bT"] = keep("bT", [P, S, B])
        with ExitStack() as early:
            for name, shape in (("vT", [P, S, B]),
                                ("kT", [P, S, B]), ("qT", [P, S, B]), ("ss", [P, G, 2 * TILES * H])):
                w[name] = early.enter_context(nc.sbuf_tensor(name, shape, F32))
            project_stage(nc, a, w, sem)
            scale_stage(nc, w, sem)
            delta_stage(nc, a, w, scr, sem)
        w["x1"] = keep("x1", [P, G * TILES, D])
        w["x1T"] = keep("x1T", [P, NTOK])
        mix_in_stage(nc, a, w, sem)
        w["x2"] = keep("x2", [P, G * TILES, D])
        xattn_stage(nc, w, scr, sem)
        w["h2T"] = keep("h2T", [P, NTOK])
        w["logits"] = keep("logits", [P, G * TILES, NE])
        attend_stage(nc, a, w, sem)
        moe_stage(nc, a, w, out, sem)


def weights_stage(nc, a, w, sem):
    raw_in, col_in, made, set_up, turned, moved_even, moved_odd, folded = (
        sem(n) for n in ("raw_in", "col_in", "made", "set_up", "turned", "moved_even", "moved_odd", "folded"))
    with ExitStack() as ctx:
        raw = ctx.enter_context(nc.sbuf_tensor("raw", [P, 4, D], F32))
        raw_b = ctx.enter_context(nc.sbuf_tensor("raw_b", [H, D], F32))
        raw_pin = ctx.enter_context(nc.sbuf_tensor("raw_pin", [P, XE * XC, D], F32))
        raw_pout = ctx.enter_context(nc.sbuf_tensor("raw_pout", [P, XE, XH], F32))
        NT = 4 + XE * XC * 2
        bank = [ctx.enter_context(nc.psum_tensor(f"turn{i}", [P, 4, P], F32)) for i in range(2)]
        bank_b = ctx.enter_context(nc.psum_tensor("turn_b", [P, H], F32))
        cols, taps = w["cols"], w["taps"]
        n_small = len(COLS) + 3 + 3 + 3
        block = ctx.enter_context(nc.Block())

        @block.sync
        def _(sp):
            for i, n in enumerate(("L0_attn_Wk", "L0_attn_Wq", "L0_attn_Wv", "L0_attn_Wo")):
                sp.dma_start(raw[:, i, :], a[n]).then_inc(raw_in, 16)
            sp.dma_start(raw_b[:], a["L0_attn_Wbeta"]).then_inc(raw_in, 16)
            sp.dma_start(raw_pin[:], a["L0_xattn_proj_in"].rearrange("e (c p) i -> p (e c) i", p=P)).then_inc(raw_in, 16)
            sp.dma_start(raw_pout[:], a["L0_xattn_proj_out"].rearrange("e i d -> i e d")).then_inc(raw_in, 16)
            sp.wait_ge(raw_in, 7 * 16)

        @block.scalar
        def _(act):
            for i, n in enumerate(COLS):
                act.dma_start(cols[:, i:i + 1], dram_ap(a[n], 0, [[1, P], [1, 1]])).then_inc(col_in, 16)
            for i, n in enumerate(("L0_attn_wk_conv", "L0_attn_wq_conv", "L0_attn_wv_conv")):
                act.dma_start(taps[:, i, :], a[n]).then_inc(col_in, 16)
            act.dma_start(cols[:, C_BETA:C_BETA + 1],
                          dram_ap(a["L0_attn_bbeta"], 0, [[1, H], [0, HD], [1, 1]])).then_inc(col_in, 16)
            act.dma_start(cols[:, C_NORMW:C_NORMW + 1],
                          dram_ap(a["L0_attn_norm_w"], 0, [[0, H], [1, HD], [1, 1]])).then_inc(col_in, 16)
            act.dma_start(w["bo_row"][:], dram_ap(a["L0_attn_bo"], 0, [[0, P], [1, D]])).then_inc(col_in, 16)
            for i in range(3):
                act.dma_start(cols[:, C_QKV + i:C_QKV + i + 1],
                              dram_ap(a["L0_ffn_b_qkv"], i * D, [[1, P], [1, 1]])).then_inc(col_in, 16)
            act.wait_ge(turned, 1)
            nc.scalar.copy(w["wT"][:], bank[0][:]).then_inc(moved_even, 1)
            for b in range(2, NT // 4, 2):
                act.wait_ge(turned, b + 1)
                t = 4 * (b - 1)
                dst = w["pinT"] if t < XE * XC else w["poutT"]
                nc.scalar.copy(dst[:, t % (XE * XC):t % (XE * XC) + 4, :], bank[0][:]).then_inc(moved_even, 1)

        @block.gpsimd
        def _(pool):
            ident, headsel = w["ident"], w["headsel"]
            nc.gpsimd.memset(ident[:], 0.0).then_inc(made, 1)
            nc.gpsimd.memset(headsel[:], 1.0).then_inc(made, 1)
            nc.gpsimd.memset(w["halfpow"][:], -0.5).then_inc(set_up, 1)
            pool.wait_ge(made, 2)
            nc.gpsimd.affine_select(out=ident[:], in_=ident[:], compare_op=ALU.not_equal, fill=1.0, base=0,
                                    pattern=[[-1, P]], channel_multiplier=1).then_inc(set_up, 1)
            nc.gpsimd.affine_select(out=headsel[:], in_=headsel[:], compare_op=ALU.is_ge, fill=0.0, base=0,
                                    pattern=[[-HD, H]], channel_multiplier=1).then_inc(made, 1)
            pool.wait_ge(made, 3)
            nc.gpsimd.affine_select(out=headsel[:], in_=headsel[:], compare_op=ALU.is_ge, fill=0.0, base=HD - 1,
                                    pattern=[[HD, H]], channel_multiplier=-1).then_inc(set_up, 1)

        @block.tensor
        def _(pe):
            pe.wait_ge(set_up, 3)
            pe.wait_ge(raw_in, 7 * 16)
            for b in range(NT // 4):
                if b >= 2:
                    pe.wait_ge(moved_odd if b % 2 else moved_even, b // 2)
                for i in range(4):
                    t = 4 * b + i - 4
                    if b == 0:
                        src = raw[:, i, :]
                    elif t < XE * XC:
                        src = raw_pin[:, t, :]
                    else:
                        t -= XE * XC
                        src = raw_pout[:, t // XC, (t % XC) * P:(t % XC + 1) * P]
                    last = nc.tensor.transpose(bank[b % 2][:, i, :], src, w["ident"][:])
                last.then_inc(turned, 1)
            nc.tensor.transpose(bank_b[:], raw_b[:], w["ident"][0:H, 0:H]).then_inc(turned, 1)

        @block.vector
        def _(dve):
            for b in range(1, NT // 4, 2):
                dve.wait_ge(turned, b + 1)
                t = 4 * (b - 1)
                dst = w["pinT"] if t < XE * XC else w["poutT"]
                nc.vector.tensor_copy(dst[:, t % (XE * XC):t % (XE * XC) + 4, :], bank[1][:]).then_inc(moved_odd, 1)
            dve.wait_ge(turned, NT // 4 + 1)
            nc.vector.tensor_copy(w["wbT"][:], bank_b[:].unsqueeze(2).to_broadcast([P, H, HD])).then_inc(set_up, 1)
            dve.wait_ge(col_in, 16 * (len(COLS) + 9))
            for i in range(3):
                nc.vector.scalar_tensor_tensor(out=cols[:, C_FOLD + i:C_FOLD + i + 1], in0=cols[:, i:i + 1],
                                               scalar=taps[:, i, TAPS - 1:TAPS], in1=cols[:, 3 + i:4 + i],
                                               op0=ALU.mult, op1=ALU.add).then_inc(folded, 1)
            nc.vector.memset(cols[:, C_EPS:C_EPS + 1], NORM_EPS).then_inc(folded, 1)
            nc.vector.memset(cols[:, C_ONE:C_ONE + 1], 1.0).then_inc(folded, 1)
            dve.wait_ge(folded, 5)


def project_stage(nc, a, w, sem):
    x_in = [sem("x_in0"), sem("x_in1")]
    (x_turned, xT_ready, proj_done, padded, first_tap, beta_ready, taps_done, sig_ready, v_ready, squared,
     summed, ss_ready, zeroed) = (sem("pr_" + n) for n in (
         "x_turned", "xT_ready", "proj_done", "padded", "first_tap", "beta_ready", "taps_done", "sig_ready",
         "v_ready", "squared", "summed", "ss_ready", "zeroed"))
    cols, taps = w["cols"], w["taps"]
    x = a["x"].rearrange("b s d -> (b s) d")
    with ExitStack() as ctx:
        def mem(name, shape):
            return [ctx.enter_context(nc.sbuf_tensor(f"{name}{i}", shape, F32)) for i in range(2)]

        xs = mem("xs", [P, TILES, D])
        xT = mem("xT", [P, GT])
        pad = mem("pad", [P, 3, GB, PAD])
        conv = mem("conv", [P, 3, GB, S])
        sig = mem("sig", [P, GB, S])
        sq = mem("sq", [P, 2, GB, S])
        ps_t = [ctx.enter_context(nc.psum_tensor(f"ps_t{i}", [P, GT], F32)) for i in range(2)]
        ps_p = [ctx.enter_context(nc.psum_tensor(f"ps_p{i}", [P, GB, S], F32)) for i in range(4)]
        ps_s = [ctx.enter_context(nc.psum_tensor(f"ps_s{i}", [P, 2 * TILES * H], F32)) for i in range(2)]

        def cols_of(t, g):
            return t[:, :, bass.ds(g * GB, GB)].rearrange("p t b -> p b t")

        block = ctx.enter_context(nc.Block())

        @block.sync
        def _(sp):
            def load(g, j):
                sp.dma_start(xs[j][:], x[bass.ds(g * GT, GT), :].rearrange("(n p) d -> p n d", p=P)
                             ).then_inc(x_in[j], 16)
            load(0, 0)
            load(1, 1)
            with sp.Fori(0, G // 2 - 1) as it:
                for j in range(2):
                    g = it * 2 + j
                    sp.wait_ge(x_turned, done(g))
                    load(g + 2, j)

        @block.tensor
        def _(pe):
            pe.sem_inc(x_turned, CREDIT)
            pe.sem_inc(summed, CREDIT)
            with pe.Fori(0, G // 2) as it:
                for j in range(2):
                    g = it * 2 + j
                    pe.wait_ge(x_in[j], it * 16 + 16)
                    pe.wait_ge(xT_ready, free2(g))
                    for i in range(TILES):
                        last = nc.tensor.transpose(ps_t[j][:, i * P:(i + 1) * P], xs[j][:, i, :], w["ident"][:])
                    last.then_inc(x_turned, 1)
                    pe.wait_ge(xT_ready, done(g))
                    for i in range(4):
                        if i < 3:
                            pe.wait_ge(first_tap, g * 3 + (i + 1))
                        else:
                            pe.wait_ge(beta_ready, free1(g))
                        lhsT = w["wT"][:, i, :] if i < 3 else w["wbT"][:].rearrange("p h d -> p (h d)")
                        nc.tensor.matmul(ps_p[i][:].rearrange("p b s -> p (b s)"), lhsT, xT[j][:],
                                         start=True, stop=True).then_inc(proj_done, 1)
                    pe.wait_ge(squared, done(g))
                    pe.wait_ge(ss_ready, free2(g))
                    sqv = sq[j][:].rearrange("p w b s -> p w (b s)")
                    for i in range(2):
                        for n in range(TILES):
                            o = (i * TILES + n) * H
                            last = nc.tensor.matmul(ps_s[j][:, o:o + H], sqv[:, i, n * P:(n + 1) * P],
                                                    w["headsel"][:], start=True, stop=True)
                    last.then_inc(summed, 1)

        @block.scalar
        def _(act):
            act.sem_inc(xT_ready, CREDIT)
            act.sem_inc(beta_ready, CREDIT)
            act.sem_inc(sig_ready, CREDIT)
            act.sem_inc(ss_ready, CREDIT)
            act.sem_inc(first_tap, 3)
            act.wait_ge(zeroed, 2)
            with act.Fori(0, G // 2) as it:
                for j in range(2):
                    g = it * 2 + j
                    act.wait_ge(x_turned, done(g))
                    act.wait_ge(proj_done, g * 4)
                    nc.scalar.copy(xT[j][:], ps_t[j][:]).then_inc(xT_ready, 1)
                    for i in range(3):
                        act.wait_ge(proj_done, g * 4 + (i + 1))
                        if i == 0:
                            act.wait_ge(v_ready, free2(g))
                            act.wait_ge(squared, free2(g))
                        nc.scalar.activation(pad[j][:, i, :, TAPS - 1:PAD], ps_p[i][:], ACT.Identity,
                                             bias=cols[:, i:i + 1]).then_inc(padded, 1)
                        nc.scalar.activation(conv[j][:, i, :, :], ps_p[i][:], ACT.Identity,
                                             bias=cols[:, C_FOLD + i:C_FOLD + i + 1],
                                             scale=taps[:, i, TAPS - 1:TAPS]).then_inc(first_tap, 1)
                    act.wait_ge(proj_done, g * 4 + 4)
                    nc.scalar.activation(cols_of(w["bT"], g), ps_p[3][:], ACT.Sigmoid,
                                         bias=cols[:, C_BETA:C_BETA + 1]).then_inc(beta_ready, 1)
                    act.wait_ge(taps_done, g * 9 + 9)
                    nc.scalar.activation(sig[j][:], conv[j][:, V_, :, :], ACT.Sigmoid).then_inc(sig_ready, 1)
                    act.wait_ge(summed, done(g))
                    nc.scalar.copy(w["ss"][:, bass.ds(g, 1), :].rearrange("p o n -> p (o n)"), ps_s[j][:]).then_inc(ss_ready, 1)

        @block.vector
        def _(dve):
            dve.sem_inc(v_ready, CREDIT)
            nc.vector.memset(pad[0][:, :, :, 0:TAPS - 1], 0.0).then_inc(zeroed, 1)
            nc.vector.memset(pad[1][:, :, :, 0:TAPS - 1], 0.0).then_inc(zeroed, 1)
            with dve.Fori(0, G // 2) as it:
                for j in range(2):
                    g = it * 2 + j
                    for t in range(TAPS - 1):
                        for i in range(3):
                            o = 3 * t + i
                            if t == 0:
                                dve.wait_ge(padded, g * 3 + (i + 1))
                                dve.wait_ge(first_tap, g * 3 + (i + 4))
                            else:
                                dve.wait_ge(taps_done, g * 9 + (o - 2))
                            dst = conv[j][:, i, :, :]
                            if t == TAPS - 2 and i < V_:
                                dst = cols_of(w["kT"] if i == K_ else w["qT"], g)
                            nc.vector.scalar_tensor_tensor(out=dst, in0=pad[j][:, i, :, t:t + S],
                                                           scalar=taps[:, i, t:t + 1], in1=conv[j][:, i, :, :],
                                                           op0=ALU.mult, op1=ALU.add).then_inc(taps_done, 1)
                    dve.wait_ge(sig_ready, done(g))
                    nc.vector.tensor_tensor(cols_of(w["vT"], g), conv[j][:, V_, :, :], sig[j][:],
                                            ALU.mult).then_inc(v_ready, 1)

        @block.gpsimd
        def _(pool):
            pool.sem_inc(squared, CREDIT)
            with pool.Fori(0, G // 2) as it:
                for j in range(2):
                    g = it * 2 + j
                    pool.wait_ge(taps_done, g * 9 + 8)
                    pool.wait_ge(summed, free2(g))
                    nc.gpsimd.tensor_tensor(sq[j][:, 0, :, :], cols_of(w["kT"], g), cols_of(w["kT"], g), ALU.mult)
                    nc.gpsimd.tensor_tensor(sq[j][:, 1, :, :], cols_of(w["qT"], g), cols_of(w["qT"], g),
                                            ALU.mult).then_inc(squared, 1)


def scale_stage(nc, w, sem):
    rooted, inverted, spread, turned, scaled, v_scaled = (
        sem("sc_" + n) for n in ("rooted", "inverted", "spread", "turned", "scaled", "v_scaled"))
    with ExitStack() as ctx:
        rexp = [ctx.enter_context(nc.sbuf_tensor(f"rexp{i}", [P, 2, TILES, H, HD], F32)) for i in range(2)]
        ps_r = [ctx.enter_context(nc.psum_tensor(f"ps_r{i}", [P, 2, GB, S], F32)) for i in range(2)]
        ss = w["ss"]

        def cols_of(t, g):
            return t[:, :, bass.ds(g * GB, GB)].rearrange("p t b -> p b t")

        block = ctx.enter_context(nc.Block())

        @block.scalar
        def _(act):
            nc.scalar.activation(ss[:], ss[:], ACT.Sqrt).then_inc(rooted, 1)

        @block.vector
        def _(dve):
            dve.sem_inc(v_scaled, CREDIT)
            dve.sem_inc(scaled, CREDIT * 2)
            dve.wait_ge(rooted, 1)
            nc.vector.tensor_scalar(ss[:], ss[:], NORM_EPS, None, ALU.add).then_inc(rooted, 1)
            dve.wait_ge(rooted, 2)
            nc.vector.reciprocal(ss[:], ss[:]).then_inc(inverted, 1)
            with dve.Fori(0, G // 2) as it:
                for j in range(2):
                    g = it * 2 + j
                    dve.wait_ge(turned, done(g))
                    kT, qT, vT, bT = (cols_of(w[n], g) for n in ("kT", "qT", "vT", "bT"))
                    nc.vector.tensor_tensor(kT, kT, ps_r[j][:, 0, :, :], ALU.mult)
                    nc.vector.tensor_tensor(vT, vT, ps_r[j][:, 0, :, :], ALU.mult).then_inc(scaled, 1)
                    nc.vector.tensor_tensor(qT, qT, ps_r[j][:, 1, :, :], ALU.mult).then_inc(scaled, 1)
                    dve.wait_ge(scaled, g * 2 + (1 + 2 * CREDIT))
                    nc.vector.tensor_tensor(vT, vT, bT, ALU.mult).then_inc(v_scaled, 1)

        @block.gpsimd
        def _(pool):
            pool.sem_inc(spread, CREDIT)
            pool.wait_ge(inverted, 1)
            with pool.Fori(0, G // 2) as it:
                for j in range(2):
                    g = it * 2 + j
                    pool.wait_ge(turned, free2(g))
                    src = ss[:, bass.ds(g, 1), :].rearrange("p o n -> p (o n)").unsqueeze(2)
                    nc.gpsimd.tensor_copy(rexp[j][:].rearrange("p w n h d -> p (w n h) d"),
                                          src.to_broadcast([P, 2 * TILES * H, HD])).then_inc(spread, 1)

        @block.tensor
        def _(pe):
            pe.sem_inc(turned, CREDIT)
            with pe.Fori(0, G // 2) as it:
                for j in range(2):
                    g = it * 2 + j
                    pe.wait_ge(spread, done(g))
                    pe.wait_ge(scaled, g * 2 + 2)
                    for i in range(2):
                        for n in range(TILES):
                            last = nc.tensor.transpose(
                                ps_r[j][:, i, :, :].rearrange("p b s -> p (b s)")[:, n * P:(n + 1) * P],
                                rexp[j][:, i, n, :, :].rearrange("p h d -> p (h d)"), w["ident"][:])
                    last.then_inc(turned, 1)


def delta_stage(nc, a, w, scr, sem):
    stored = [sem(f"kq_stored{c}") for c in range(NCH)]
    kq_in = [sem("kq_in0"), sem("kq_in1")]
    (state_op, qs_made, o_summed, o_copied, dist_ready, hit, weighed, gated, gates_copied, gates_stored,
     const, picks_in, empty) = (sem("de_" + n) for n in (
         "state_op", "qs_made", "o_summed", "o_copied", "dist_ready", "hit", "weighed", "gated", "gates_copied",
         "gates_stored", "const", "picks_in", "empty"))
    OPS = 6
    NIT = NCH // 2
    TURN = 2 * CH
    PAIRS = B // 2
    GC = PAIRS // NIT * S
    with ExitStack() as ctx:
        def mem(name, shape, n=2, dt=F32):
            return [ctx.enter_context(nc.sbuf_tensor(f"{name}{i}", shape, dt)) for i in range(n)]

        krep = mem("krep", [P, HD, CH, B])
        qrep = mem("qrep", [P, HD, CH, B])
        qs = mem("qs", [P, HD, HC, B])
        state = mem("state", [P, HD, B])
        prod, = mem("prod", [P, HD, B], 1)
        rise, = mem("rise", [P, HD, B], 1)
        pred, bpred, upd = mem("small", [P, B], 3)
        pick_w, = mem("pick_w", [P, PAIRS, S], 1)
        pick_e, = mem("pick_e", [P, PAIRS, S], 1, I32)
        dist = mem("dist", [P, GC])
        wsel = mem("wsel", [P, GC])
        negs, = mem("negs", [P, XE], 1)
        esel, = mem("esel", [P, XE, 2, XE], 1)
        gates, = mem("gates", [2 * XE, GC], 1)
        ps_o = [ctx.enter_context(nc.psum_tensor(f"ps_o{i}", [P, 512], F32)) for i in range(2)]
        ps_g = ctx.enter_context(nc.psum_tensor("ps_g", [2 * XE, GC], F32))
        oT = w["bT"]
        block = ctx.enter_context(nc.Block())

        @block.sync
        def _(sp):
            def load(first, cb):
                for t, name in ((krep, "k_scr"), (qrep, "q_scr")):
                    for i in range(HD):
                        src = dram_ap(scr[name], first + i * NTOK,
                                      [[HD * NTOK, H], [0, HD], [1, CH * B]])
                        sp.dma_start(t[cb][:, i, :, :].rearrange("p t b -> p (t b)"), src).then_inc(kq_in[cb], 16)
            for cb in range(2):
                sp.wait_ge(stored[cb], 32)
                load(cb * CH * B, cb)
            for c in range(2, NCH):
                sp.wait_ge(stored[c], 32)
            with sp.Fori(1, NIT) as it:
                for cb in range(2):
                    first = sp.snap((it * 2 + cb) * (CH * B))
                    sp.wait_ge(qs_made, it * TURN + ((cb - 1) * CH + CREDIT * HC))
                    load(first, cb)

        @block.scalar
        def _(act):
            for c in range(NCH):
                for t, name in ((w["kT"], "k_scr"), (w["qT"], "q_scr")):
                    act.dma_start(scr[name][:, c * CH * B:(c + 1) * CH * B],
                                  t[:, c * CH:(c + 1) * CH, :].rearrange("p t b -> p (t b)")).then_inc(stored[c], 16)
            for t, name in ((pick_w, "ctx_512"), (pick_e, "itok_BxS2xS_0_7")):
                for b2 in range(2):
                    src = dram_ap(a[name], b2 * XK * S, [[S, XK], [2 * XK * S, PAIRS], [1, S]])
                    act.dma_start(t[b2 * XK:(b2 + 1) * XK, :, :], src).then_inc(picks_in, 16)
            act.sem_inc(o_copied, CREDIT)
            act.sem_inc(gates_stored, 32)
            act.wait_ge(const, 3 * XE + 1)
            act.wait_ge(picks_in, 64)
            with act.Fori(0, NIT) as it:
                part = pick_e[:, bass.ds(it * (PAIRS // NIT), PAIRS // NIT), :].rearrange("p n s -> p (n s)")
                for e in range(XE):
                    n = it * XE + e
                    nc.scalar.activation(dist[e % 2][:], part, ACT.Abs, bias=negs[:, e:e + 1]).then_inc(dist_ready, 1)
                    act.wait_ge(dist_ready, n + 1)
                    act.wait_ge(gated, free2(n))
                    nc.scalar.activation(wsel[e % 2][:], dist[e % 2][:], ACT.Relu, bias=w["cols"][:, C_ONE:C_ONE + 1],
                                         scale=-1.0).then_inc(hit, 1)
                    if e % 2:
                        hc = it * 4 + e // 2
                        act.wait_ge(o_summed, done(hc))
                        nc.scalar.copy(oT[:, bass.ds(hc * HC, HC), :].rearrange("p t b -> p (t b)"),
                                       ps_o[(e // 2) % 2][:, 0:HC * B]).then_inc(o_copied, 1)
                act.wait_ge(gated, it * XE + (XE + CREDIT))
                act.wait_ge(gates_stored, it * 32 + 32)
                nc.scalar.copy(gates[:], ps_g[:]).then_inc(gates_copied, 1)
                act.wait_ge(gates_copied, it + 1)
                for b2 in range(2):
                    dst = dram_ap(scr["gate_scr"], it * (2 * GC) + b2 * S, [[NTOK, XE], [2 * S, PAIRS // NIT], [1, S]])
                    act.dma_start(dst, gates[b2 * XE:(b2 + 1) * XE, :].rearrange("e (n s) -> e n s", s=S)
                                  ).then_inc(gates_stored, 16)
            act.wait_ge(gates_stored, 32 * (NIT + 1))

        @block.gpsimd
        def _(pool):
            for e in range(XE):
                nc.gpsimd.memset(negs[:, e:e + 1], float(-e)).then_inc(const, 1)
            nc.gpsimd.memset(esel[:], 0.0).then_inc(const, 1)
            pool.wait_ge(const, XE + 1)
            for e in range(XE):
                for b2 in range(2):
                    nc.gpsimd.memset(esel[b2 * XK:(b2 + 1) * XK, e, b2, e:e + 1], 1.0).then_inc(const, 1)
            pool.wait_ge(const, 3 * XE + 1)
            pool.wait_ge(picks_in, 64)
            pool.sem_inc(qs_made, CREDIT * HC)
            with pool.Fori(0, NIT) as it:
                part = pick_w[:, bass.ds(it * (PAIRS // NIT), PAIRS // NIT), :].rearrange("p n s -> p (n s)")
                for t in range(TURN):
                    hc, cb = t // HC, t // CH
                    if t % HC == 0:
                        pool.wait_ge(o_summed, free2(it * 4 + hc))
                    if t % CH == 0:
                        pool.wait_ge(kq_in[cb], it * 256 + 256)
                    if t % 2:
                        pool.wait_ge(hit, it * XE + (t // 2 + 1))
                    pool.wait_ge(state_op, it * (TURN * OPS) + (t + 1) * OPS)
                    nc.gpsimd.tensor_tensor(qs[hc % 2][:, :, t % HC, :], state[(t + 1) % 2][:],
                                            qrep[cb][:, :, t % CH, :], ALU.mult).then_inc(qs_made, 1)
                    if t % 2:
                        e = t // 2
                        nc.gpsimd.tensor_tensor(wsel[e % 2][:], wsel[e % 2][:], part, ALU.mult).then_inc(weighed, 1)

        @block.vector
        def _(dve):
            nc.vector.memset(state[0][:], 0.0).then_inc(empty, 1)
            dve.wait_ge(empty, 1)
            with dve.Fori(0, NIT) as it:
                for t in range(TURN):
                    cb = t // CH
                    k = krep[cb][:, :, t % CH, :]
                    old, new = state[t % 2], state[(t + 1) % 2]
                    ops = it * (TURN * OPS)
                    beta = w["bT"][:, bass.ds(it * TURN + t, 1), :].rearrange("p o b -> p (o b)")
                    v = w["vT"][:, bass.ds(it * TURN + t, 1), :].rearrange("p o b -> p (o b)")
                    if t % CH == 0:
                        dve.wait_ge(kq_in[cb], it * 256 + 256)
                    nc.vector.tensor_tensor(prod[:], old[:], k, ALU.mult).then_inc(state_op, 1)
                    dve.wait_ge(state_op, ops + (t * OPS + 1))
                    nc.vector.tensor_reduce(pred[:], prod[:].rearrange("p i b -> p b i"), AX.X, ALU.add).then_inc(state_op, 1)
                    dve.wait_ge(state_op, ops + (t * OPS + 2))
                    nc.vector.tensor_tensor(bpred[:], pred[:], beta, ALU.mult).then_inc(state_op, 1)
                    dve.wait_ge(state_op, ops + (t * OPS + 3))
                    nc.vector.tensor_tensor(upd[:], v, bpred[:], ALU.subtract).then_inc(state_op, 1)
                    dve.wait_ge(state_op, ops + (t * OPS + 4))
                    nc.vector.tensor_tensor(rise[:], k, upd[:].unsqueeze(1).to_broadcast([P, HD, B]),
                                            ALU.mult).then_inc(state_op, 1)
                    dve.wait_ge(state_op, ops + (t * OPS + 5))
                    dve.wait_ge(qs_made, it * TURN + (t + CREDIT * HC))
                    nc.vector.tensor_tensor(new[:], old[:], rise[:], ALU.add).then_inc(state_op, 1)
                    dve.wait_ge(state_op, ops + (t * OPS + 6))

        @block.tensor
        def _(pe):
            pe.sem_inc(o_summed, CREDIT)
            pe.sem_inc(gated, CREDIT)
            pe.wait_ge(const, 3 * XE + 1)
            with pe.Fori(0, NIT) as it:
                for hc in range(4):
                    n = it * 4 + hc
                    pe.wait_ge(qs_made, n * HC + (HC + CREDIT * HC))
                    pe.wait_ge(o_copied, free2(n))
                    for i in range(HD):
                        last = nc.tensor.matmul(ps_o[hc % 2][:, 0:HC * B], w["ident"][:],
                                                qs[hc % 2][:, i, :, :].rearrange("p t b -> p (t b)"),
                                                start=(i == 0), stop=(i == HD - 1))
                    last.then_inc(o_summed, 1)
                    for e in range(2 * hc, 2 * hc + 2):
                        pe.wait_ge(weighed, it * XE + (e + 1))
                        if e == 0:
                            pe.wait_ge(gates_copied, it)
                        nc.tensor.matmul(ps_g[:], esel[:, e, :, :].rearrange("p b e -> p (b e)"), wsel[e % 2][:],
                                         start=(e == 0), stop=(e == XE - 1)).then_inc(gated, 1)


def carry_dve(nc, w):
    nc.vector.memset(w["idle_dve"][:], 0.0)


def carry_pool(nc, w):
    nc.gpsimd.tensor_tensor(w["idle_pool"][:], w["halfpow"][:, 0:1], w["halfpow"][:, 0:1], ALU.mult)


class LayerNorm:

    def __init__(self, nc, ctx, sem, w, name):
        self.nc, self.w = nc, w
        self.stats, self.mean, self.var, self.rstd = (
            [ctx.enter_context(nc.sbuf_tensor(f"{name}_{what}{i}", [P, TILES, n], F32)) for i in range(2)]
            for what, n in (("stats", 6), ("mean", 2), ("var", 1), ("rstd", 1)))
        self.stats_done, self.mean_done, self.var_done, self.rstd_done = (
            sem(f"{name}_{what}") for what in ("stats_done", "mean_done", "var_done", "rstd_done"))

    def moments(self, dve, y, j, g):
        for n in range(TILES):
            last = self.nc.vector.bn_stats(self.stats[j][:, n, :], y[:, n, :])
        last.then_inc(self.stats_done, 1)
        dve.wait_ge(self.stats_done, g + 1)
        carry_dve(self.nc, self.w)
        for n in range(TILES):
            last = self.nc.vector.bn_aggr(self.mean[j][:, n, :], self.stats[j][:, n, :])
        last.then_inc(self.mean_done, 1)
        dve.wait_ge(self.mean_done, g + 1)
        self.nc.vector.tensor_scalar(self.var[j][:], self.mean[j][:, :, 1:2], LN_EPS, None, ALU.add
                                     ).then_inc(self.var_done, 1)

    def root(self, pool, halfpow, j, g):
        pool.wait_ge(self.var_done, g + 1)
        self.nc.gpsimd.tensor_tensor(self.rstd[j][:].rearrange("p n o -> p (n o)"),
                                     self.var[j][:].rearrange("p n o -> p (n o)"), halfpow[:, 0:TILES],
                                     ALU.pow).then_inc(self.rstd_done, 1)

    def normalise(self, dve, y, dst, j, g):
        dve.wait_ge(self.rstd_done, g + 1)
        for n in range(TILES):
            last = self.nc.vector.tensor_scalar(dst[:, n, :], y[:, n, :], self.mean[j][:, n, 0:1],
                                                self.rstd[j][:, n, :], ALU.subtract, ALU.mult)
        return last


def group_tiles(t, g):
    return t[:, bass.ds(g * TILES, TILES), :]


def group_cols(t, g):
    return t[:, bass.ds(g * GT, GT)]


def mix_in_stage(nc, a, w, sem):
    x_in = [sem("mi_x_in0"), sem("mi_x_in1")]
    (squared, summed, meaned, rooted, spread, turned, normed, projected, biased, added, x1_ready, x1_turned,
     x1T_ready, x1_kept) = (sem("mi_" + n) for n in (
         "squared", "summed", "meaned", "rooted", "spread", "turned", "normed", "projected", "biased", "added",
         "x1_ready", "x1_turned", "x1T_ready", "x1_kept"))
    x = a["x"].rearrange("b s d -> (b s) d")
    cols = w["cols"]
    with ExitStack() as ctx:
        def mem(name, shape):
            return [ctx.enter_context(nc.sbuf_tensor(f"mi_{name}{i}", shape, F32)) for i in range(2)]

        def bank(name, shape):
            return [ctx.enter_context(nc.psum_tensor(f"mi_{name}{i}", shape, F32)) for i in range(2)]

        xs = mem("xs", [P, TILES, D])
        sq = mem("sq", [P, GB, S])
        ms = mem("ms", [P, TILES * H])
        rms = mem("rms", [P, TILES * H])
        rexp = mem("rexp", [P, TILES * H, HD])
        on = mem("on", [P, GB, S])
        y = mem("y", [P, TILES, D])
        x1 = mem("x1", [P, TILES, D])
        ps_s = bank("ps_s", [P, 512])
        ps_r = bank("ps_r", [P, GB, S])
        ps_y = bank("ps_y", [P, TILES, D])
        ps_t = bank("ps_t", [P, TILES, P])
        ln = LayerNorm(nc, ctx, sem, w, "mi_ln")

        def cols_of(t, g):
            return t[:, :, bass.ds(g * GB, GB)].rearrange("p t b -> p b t")

        block = ctx.enter_context(nc.Block())

        @block.sync
        def _(sp):
            def load(g, j):
                sp.dma_start(xs[j][:], x[bass.ds(g * GT, GT), :].rearrange("(n p) d -> p n d", p=P)
                             ).then_inc(x_in[j], 16)
            load(0, 0)
            load(1, 1)
            with sp.Fori(0, G // 2 - 1) as it:
                for j in range(2):
                    g = it * 2 + j
                    sp.wait_ge(added, g + 1)
                    load(g + 2, j)

        @block.scalar
        def _(act):
            act.sem_inc(x1T_ready, CREDIT)
            with act.Fori(0, G // 2) as it:
                for j in range(2):
                    g = it * 2 + j
                    act.wait_ge(summed, free2(g))
                    nc.scalar.activation(sq[j][:], cols_of(w["bT"], g), ACT.Square).then_inc(squared, 1)
                    act.wait_ge(x1_turned, done(g))
                    nc.scalar.copy(group_cols(w["x1T"], g), ps_t[j][:].rearrange("p n d -> p (n d)")).then_inc(x1T_ready, 1)

        @block.tensor
        def _(pe):
            pe.sem_inc(summed, CREDIT)
            pe.sem_inc(turned, CREDIT)
            pe.sem_inc(x1_turned, CREDIT)
            with pe.Fori(0, G // 2) as it:
                for j in range(2):
                    g = it * 2 + j
                    pe.wait_ge(squared, g + 1)
                    pe.wait_ge(meaned, free2(g))
                    for n in range(TILES):
                        last = nc.tensor.matmul(ps_s[j][:, n * H:(n + 1) * H],
                                                sq[j][:].rearrange("p b s -> p (b s)")[:, n * P:(n + 1) * P],
                                                w["headsel"][:], start=True, stop=True)
                    last.then_inc(summed, 1)
                    pe.wait_ge(spread, g + 1)
                    pe.wait_ge(normed, free2(g))
                    for n in range(TILES):
                        last = nc.tensor.transpose(ps_r[j][:].rearrange("p b s -> p (b s)")[:, n * P:(n + 1) * P],
                                                   rexp[j][:, n * H:(n + 1) * H, :].rearrange("p h d -> p (h d)"),
                                                   w["ident"][:])
                    last.then_inc(turned, 1)
                    pe.wait_ge(normed, done(g))
                    pe.wait_ge(added, g)
                    for n in range(TILES):
                        last = nc.tensor.matmul(ps_y[j][:, n, :], on[j][:].rearrange("p b s -> p (b s)")[:, n * P:(n + 1) * P],
                                                w["wT"][:, O_, :], start=True, stop=True)
                    last.then_inc(projected, 1)
                    pe.wait_ge(x1_ready, g + 1)
                    pe.wait_ge(x1T_ready, free2(g))
                    for n in range(TILES):
                        last = nc.tensor.transpose(ps_t[j][:, n, :], x1[j][:, n, :], w["ident"][:])
                    last.then_inc(x1_turned, 1)

        @block.vector
        def _(dve):
            dve.sem_inc(meaned, CREDIT)
            dve.sem_inc(normed, CREDIT)
            with dve.Fori(0, G // 2) as it:
                for j in range(2):
                    g = it * 2 + j
                    dve.wait_ge(summed, done(g))
                    nc.vector.tensor_scalar(ms[j][:], ps_s[j][:, 0:TILES * H], 1.0 / HD, NORM_EPS, ALU.mult, ALU.add
                                            ).then_inc(meaned, 1)
                    dve.wait_ge(turned, done(g))
                    nc.vector.scalar_tensor_tensor(out=on[j][:], in0=cols_of(w["bT"], g),
                                                   scalar=cols[:, C_NORMW:C_NORMW + 1], in1=ps_r[j][:],
                                                   op0=ALU.mult, op1=ALU.mult).then_inc(normed, 1)
                    dve.wait_ge(projected, g + 1)
                    dve.wait_ge(biased, g + 1)
                    nc.vector.tensor_tensor(y[j][:], xs[j][:], ps_y[j][:], ALU.add).then_inc(added, 1)
                    dve.wait_ge(added, g + 1)
                    ln.moments(dve, y[j], j, g)
                    dve.wait_ge(x1_turned, free2(g))
                    dve.wait_ge(x1_kept, free2(g))
                    ln.normalise(dve, y[j], x1[j], j, g).then_inc(x1_ready, 1)

        @block.gpsimd
        def _(pool):
            pool.sem_inc(x1_kept, CREDIT)
            with pool.Fori(0, G // 2) as it:
                for j in range(2):
                    g = it * 2 + j
                    pool.wait_ge(x_in[j], it * 16 + 16)
                    nc.gpsimd.tensor_tensor(xs[j][:], xs[j][:], w["bo_row"][:].unsqueeze(1).to_broadcast([P, TILES, D]),
                                            ALU.add).then_inc(biased, 1)
                    pool.wait_ge(meaned, done(g))
                    nc.gpsimd.tensor_tensor(rms[j][:], ms[j][:], w["halfpow"][:], ALU.pow).then_inc(rooted, 1)
                    pool.wait_ge(rooted, g + 1)
                    pool.wait_ge(turned, free2(g))
                    carry_pool(nc, w)
                    nc.gpsimd.tensor_copy(rexp[j][:], rms[j][:].unsqueeze(2).to_broadcast([P, TILES * H, HD])
                                          ).then_inc(spread, 1)
                    ln.root(pool, w["halfpow"], j, g)
                    pool.wait_ge(x1_ready, g + 1)
                    carry_pool(nc, w)
                    nc.gpsimd.tensor_copy(group_tiles(w["x1"], g), x1[j][:]).then_inc(x1_kept, 1)


def xattn_stage(nc, w, scr, sem):
    gates_in = [sem("xa_gates_in0"), sem("xa_gates_in1")]
    NJ = XE * XC
    NB = 4
    (hidden, relued, used, sum_copied, turned, added, x2_ready) = (sem("xa_" + n) for n in (
        "hidden", "relued", "used", "sum_copied", "turned", "added", "x2_ready"))
    with ExitStack() as ctx:
        def mem(name, shape, n=2):
            return [ctx.enter_context(nc.sbuf_tensor(f"xa_{name}{i}", shape, F32)) for i in range(n)]

        def bank(name, shape, n):
            return [ctx.enter_context(nc.psum_tensor(f"xa_{name}{i}", shape, F32)) for i in range(n)]

        gates = mem("gates", [P, XE, GT])
        hid = mem("hid", [P, GT], NB)
        oT = mem("oT", [P, GT])
        y = mem("y", [P, TILES, D])
        ps_h = bank("ps_h", [P, GT], NB)
        ps_o = bank("ps_o", [P, GT], 2)
        ps_t, = bank("ps_t", [P, TILES, D], 1)
        ln = LayerNorm(nc, ctx, sem, w, "xa_ln")
        block = ctx.enter_context(nc.Block())

        @block.sync
        def _(sp):
            def load(g, j):
                src = dram_ap(scr["gate_scr"], g * GT, [[0, P], [NTOK, XE], [1, GT]])
                sp.dma_start(gates[j][:], src).then_inc(gates_in[j], 16)
            load(0, 0)
            load(1, 1)
            with sp.Fori(0, G // 2 - 1) as it:
                for j in range(2):
                    sp.wait_ge(relued, it * (2 * NJ) + ((j + 1) * NJ + NB))
                    load(it * 2 + (j + 2), j)

        @block.tensor
        def _(pe):
            pe.sem_inc(used, NB)
            pe.sem_inc(turned, CREDIT)
            with pe.Fori(0, G // 2) as it:
                for j in range(2):
                    g = it * 2 + j
                    x1T = group_cols(w["x1T"], g)

                    def out_part(m):
                        pe.wait_ge(relued, g * NJ + (m + 1 + NB))
                        if m == 0:
                            pe.wait_ge(sum_copied, free2(g))
                        nc.tensor.matmul(ps_o[j][:], w["poutT"][:, m, :], hid[m % NB][:], start=(m == 0),
                                         stop=(m == NJ - 1)).then_inc(used, 1)
                    for m in range(NJ):
                        pe.wait_ge(relued, g * NJ + (m + 1))
                        nc.tensor.matmul(ps_h[m % NB][:], w["pinT"][:, m, :], x1T, start=True, stop=True
                                         ).then_inc(hidden, 1)
                        if m >= 2:
                            out_part(m - 2)
                    out_part(NJ - 2)
                    out_part(NJ - 1)
                    pe.wait_ge(sum_copied, done(g))
                    pe.wait_ge(added, g + 1)
                    for n in range(TILES):
                        last = nc.tensor.transpose(ps_t[:, n, :], oT[j][:, n * P:(n + 1) * P], w["ident"][:])
                    last.then_inc(turned, 1)

        @block.scalar
        def _(act):
            act.sem_inc(sum_copied, CREDIT)
            with act.Fori(0, G // 2) as it:
                for j in range(2):
                    g = it * 2 + j
                    act.wait_ge(used, g * NJ + (NJ + NB))
                    act.wait_ge(turned, free2(g))
                    nc.scalar.copy(oT[j][:], ps_o[j][:]).then_inc(sum_copied, 1)

        @block.vector
        def _(dve):
            dve.sem_inc(relued, NB)
            dve.sem_inc(added, 1)
            with dve.Fori(0, G // 2) as it:
                for j in range(2):
                    g = it * 2 + j
                    dve.wait_ge(gates_in[j], it * 16 + 16)
                    for m in range(NJ):
                        dve.wait_ge(hidden, g * NJ + (m + 1))
                        dve.wait_ge(used, g * NJ + (m + 1))
                        nc.vector.scalar_tensor_tensor(out=hid[m % NB][:], in0=ps_h[m % NB][:], scalar=0.0,
                                                       in1=gates[j][:, m // XC, :], op0=ALU.max, op1=ALU.mult
                                                       ).then_inc(relued, 1)
                    dve.wait_ge(turned, done(g))
                    nc.vector.tensor_tensor(y[j][:], group_tiles(w["x1"], g), ps_t[:], ALU.add).then_inc(added, 1)
                    dve.wait_ge(added, g + 2)
                    ln.moments(dve, y[j], j, g)
                    ln.normalise(dve, y[j], group_tiles(w["x2"], g), j, g).then_inc(x2_ready, 1)

        @block.gpsimd
        def _(pool):
            with pool.Fori(0, G // 2) as it:
                for j in range(2):
                    ln.root(pool, w["halfpow"], j, it * 2 + j)


def attend_stage(nc, a, w, sem):
    UB = 4
    NU = GB // UB
    RG = 4
    NP = GB // 2
    NW = 11
    weights_in = sem("at_weights_in")
    (xh_ready, xh_turned, h1_ready, q_proj, q_read, k_proj, k_read, v_proj, v_read, scored, maxed, shifted,
     exped, p_turned, p_copied, mixed, inverted, c_ready, c_turned, c_copied, o_proj, h_added, h_ready, hh_ready,
     hh_turned, h2_ready, routed, logits_ready, h2_kept, const, mask_made) = (sem("at_" + n) for n in (
         "xh_ready", "xh_turned", "h1_ready", "q_proj", "q_read", "k_proj", "k_read", "v_proj", "v_read", "scored",
         "maxed", "shifted", "exped", "p_turned", "p_copied", "mixed", "inverted", "c_ready", "c_turned", "c_copied",
         "o_proj", "h_added", "h_ready", "hh_ready", "hh_turned", "h2_ready", "routed", "logits_ready", "h2_kept",
         "const", "mask_made"))
    cols = w["cols"]
    with ExitStack() as ctx:
        def mem(name, shape, n=2):
            return [ctx.enter_context(nc.sbuf_tensor(f"at_{name}{i}", shape, F32)) for i in range(n)]

        def bank(name, shape, n):
            return [ctx.enter_context(nc.psum_tensor(f"at_{name}{i}", shape, F32)) for i in range(n)]

        wqkv, = mem("wqkv", [P, 3, D], 1)
        wo, = mem("wo", [P, 2, D], 1)
        wg, = mem("wg", [P, NE], 1)
        bo, = mem("bo", [P, D], 1)
        bv, = mem("bv", [P, 2], 1)
        qmask, = mem("qmask", [P, RG], 1)
        xh = mem("xh", [P, TILES, D])
        h1T = mem("h1T", [P, GB, 2, S])
        qx = mem("qx", [P, GB, RG, S])
        kT = mem("kT", [P, GB, S])
        vx = mem("vx", [P, GB * RG, 2, 2, HD + 1])
        prob = mem("prob", [P, RG, 2 * UB, S])
        pT = mem("pT", [P, RG, P])
        top = mem("top", [P, RG * 2 * UB])
        rden = mem("rden", [P, 2 * RG, 2])
        cx = mem("cx", [P, GB, RG, 2, HD])
        cT = mem("cT", [P, P])
        h = mem("h", [P, TILES, D])
        hh = mem("hh", [P, TILES, D])
        h2T = mem("h2T", [P, GT])
        ps_s, = bank("ps_s", [P, RG, 2 * UB, S], 1)
        ps_p = bank("ps_p", [P, RG, P], 2)
        ps_c, = bank("ps_c", [P, 512], 1)
        ps_m, = bank("ps_m", [P, 512], 1)
        mix = ps_c[:, 0:2 * RG * 4 * (HD + 1)].rearrange("p (n a h d) -> p n a h d", a=2, h=2, d=HD + 1)
        ln1 = LayerNorm(nc, ctx, sem, w, "at_ln1")
        ln2 = LayerNorm(nc, ctx, sem, w, "at_ln2")
        tiles_m = ps_m[:].rearrange("p (n d) -> p n d", n=TILES)
        block = ctx.enter_context(nc.Block())

        @block.sync
        def _(sp):
            sp.dma_start(wqkv[:].rearrange("p a d -> p (a d)"), a["L0_ffn_w_qkv"]).then_inc(weights_in, 16)
            for half in range(2):
                for b2 in range(2):
                    src = dram_ap(a["L0_ffn_w_o"], half * HD * D, [[2 * HD * D, H // 2], [D, HD], [1, D]])
                    sp.dma_start(wo[b2 * 64:(b2 + 1) * 64, half, :], src).then_inc(weights_in, 16)
                    src = dram_ap(a["L0_ffn_b_qkv"], 2 * D + half * HD, [[2 * HD, H // 2], [1, HD], [1, 1]])
                    sp.dma_start(bv[b2 * 64:(b2 + 1) * 64, half:half + 1], src).then_inc(weights_in, 16)
            sp.dma_start(wg[:], a["L0_ffn_w_gate"]).then_inc(weights_in, 16)
            sp.dma_start(bo[:], dram_ap(a["L0_ffn_b_o"], 0, [[0, P], [1, D]])).then_inc(weights_in, 16)
            sp.wait_ge(weights_in, NW * 16)

        @block.gpsimd
        def _(pool):
            pool.sem_inc(h2_kept, CREDIT)
            for j in range(2):
                nc.gpsimd.memset(vx[j][:], 0.0).then_inc(const, 1)
            pool.wait_ge(const, 2)
            for j in range(2):
                for half in range(2):
                    nc.gpsimd.memset(vx[j][half * S:(half + 1) * S, :, half, :, HD:HD + 1], 1.0).then_inc(const, 1)
            pool.wait_ge(const, 6)
            with pool.Fori(0, G // 2) as it:
                for j in range(2):
                    g = it * 2 + j
                    ln1.root(pool, w["halfpow"], j, g)
                    ln2.root(pool, w["halfpow"], j, g)
                    pool.wait_ge(h2_ready, done(g))
                    carry_pool(nc, w)
                    nc.gpsimd.tensor_copy(group_cols(w["h2T"], g), h2T[j][:]).then_inc(h2_kept, 1)

        @block.tensor
        def _(pe):
            for s in (xh_turned, q_proj, hh_turned, routed, o_proj, p_turned, mixed, c_turned):
                pe.sem_inc(s, CREDIT)
            pe.wait_ge(weights_in, NW * 16)
            pe.wait_ge(const, 6)
            pe.wait_ge(mask_made, 5)
            with pe.Fori(0, G // 2) as it:
                for j in range(2):
                    g = it * 2 + j
                    h1 = h1T[j][:, :, 0, :]
                    pe.wait_ge(xh_ready, g + 1)
                    pe.wait_ge(logits_ready, g + 1)
                    for n in range(TILES):
                        last = nc.tensor.transpose(tiles_m[:, n, :], xh[j][:, n, :], w["ident"][:])
                    last.then_inc(xh_turned, 1)
                    pe.wait_ge(h1_ready, done(g))
                    nc.tensor.matmul(ps_m[:], wqkv[:, 0, :], h1, start=True, stop=True).then_inc(q_proj, 1)
                    pe.wait_ge(q_read, done(g))
                    nc.tensor.matmul(ps_m[:], wqkv[:, 1, :], h1, start=True, stop=True).then_inc(k_proj, 1)
                    pe.wait_ge(k_read, done(g))
                    for u in range(NU):
                        if u:
                            pe.wait_ge(v_read, g * NU + u)
                        for b in range(UB):
                            twice = h1T[j][:, u * UB + b, :, :].rearrange("p a s -> p (a s)")
                            last = nc.tensor.matmul(tiles_m[:, b, :], twice, wqkv[:, 2, :], start=True, stop=True)
                        last.then_inc(v_proj, 1)
                    pe.wait_ge(v_read, g * NU + NU)
                    for u in range(NU):
                        n = g * NU + u
                        pe.wait_ge(shifted, n + 1)
                        for b in range(UB):
                            bb = u * UB + b
                            for hp in range(2):
                                for r in range(RG):
                                    rows = slice(32 * r, 32 * r + 32)
                                    last = nc.tensor.matmul(
                                        ps_s[:, r, b * 2 + hp, :],
                                        qx[j][rows, bb, 2 * hp:2 * hp + 2, :].rearrange("p h s -> p (h s)"),
                                        kT[j][rows, bb, :], start=True, stop=True)
                        last.then_inc(scored, 1)
                        pe.wait_ge(exped, n + 1)
                        for b in range(UB):
                            m = n * UB + b
                            i = b % 2
                            pe.wait_ge(p_copied, m + 1)
                            for r in range(RG):
                                last = nc.tensor.transpose(
                                    ps_p[i][:, r, :], prob[u % 2][:, r, 2 * b:2 * b + 2, :].rearrange("p x s -> p (x s)"),
                                    w["ident"][:])
                            last.then_inc(p_turned, 1)
                            if i == 0:
                                pe.wait_ge(c_ready, n * 2 + (b // 2 + 1))
                            pe.wait_ge(p_copied, m + 3)
                            for r in range(RG):
                                last = nc.tensor.matmul(
                                    mix[:, i * RG + r, :, :, :].rearrange("p a h d -> p (a h d)"), pT[i][:, r, :],
                                    vx[j][:, (u * UB + b) * RG + r, :, :, :].rearrange("p a h d -> p (a h d)"),
                                    start=True, stop=True)
                            last.then_inc(mixed, 1)
                    pe.wait_ge(p_copied, g * GB + (GB + 2))
                    for p in range(NP):
                        m = g * NP + p
                        pe.wait_ge(c_ready, m + 2)
                        pe.wait_ge(c_copied, m + 1)
                        nc.tensor.transpose(ps_p[p % 2][:, 0, :],
                                            cx[j][:, 2 * p:2 * p + 2, :, :, :].rearrange("p b r x d -> p (b r x d)"),
                                            w["ident"][:]).then_inc(c_turned, 1)
                        pe.wait_ge(c_copied, m + 3)
                        nc.tensor.transpose(ps_p[p % 2][:, 1, :], w["ident"][:], w["ident"][:])
                        for b2 in range(2):
                            rows = slice(64 * b2, 64 * b2 + 64)
                            for half in range(2):
                                last = nc.tensor.matmul(tiles_m[rows, p, :], cT[p % 2][rows, half * S:(half + 1) * S],
                                                        wo[rows, half, :], start=(half == 0), stop=(half == 1))
                    last.then_inc(o_proj, 1)
                    pe.wait_ge(hh_ready, g + 1)
                    for n in range(TILES):
                        last = nc.tensor.transpose(tiles_m[:, n, :], hh[j][:, n, :], w["ident"][:])
                    last.then_inc(hh_turned, 1)
                    pe.wait_ge(h2_ready, done(g))
                    for n in range(TILES):
                        last = nc.tensor.matmul(ps_m[:, n * NE:(n + 1) * NE], h2T[j][:, n * P:(n + 1) * P], wg[:],
                                                start=True, stop=True)
                    last.then_inc(routed, 1)

        @block.scalar
        def _(act):
            for s in (h1_ready, k_read, p_copied, c_copied, h2_ready):
                act.sem_inc(s, CREDIT)
            act.sem_inc(logits_ready, 1)
            act.wait_ge(weights_in, NW * 16)
            act.wait_ge(const, 6)
            with act.Fori(0, G // 2) as it:
                for j in range(2):
                    g = it * 2 + j
                    act.wait_ge(xh_turned, done(g))
                    for twin in range(2):
                        last = nc.scalar.activation(h1T[j][:, :, twin, :], ps_m[:].rearrange("p (b s) -> p b s", b=GB),
                                                    ACT.Identity, bias=cols[:, C_LN1B:C_LN1B + 1],
                                                    scale=cols[:, C_LN1W:C_LN1W + 1])
                    last.then_inc(h1_ready, 1)
                    act.wait_ge(k_proj, g + 1)
                    nc.scalar.activation(kT[j][:].rearrange("p b s -> p (b s)"), ps_m[:], ACT.Identity,
                                         bias=cols[:, C_QKV + 1:C_QKV + 2]).then_inc(k_read, 1)
                    for u in range(NU):
                        act.wait_ge(v_proj, g * NU + (u + 1))
                        for half in range(2):
                            rows = slice(half * S, (half + 1) * S)
                            src = ps_m[rows, :].rearrange("p (n x h d) -> p n x h d", x=2, h=2, d=HD)[:, :, half, :, :]
                            dst = vx[j][rows, u * UB * RG:(u + 1) * UB * RG, half, :, 0:HD]
                            last = nc.scalar.copy(dst, src)
                        last.then_inc(v_read, 1)
                    for u in range(NU):
                        n = g * NU + u
                        act.wait_ge(shifted, n + 2)
                        pv = prob[u % 2][:].rearrange("p r x s -> p (r x s)")
                        nc.scalar.activation(pv, pv, ACT.Exp).then_inc(exped, 1)
                        for b in range(UB):
                            m = n * UB + b
                            act.wait_ge(p_turned, m + 3)
                            act.wait_ge(mixed, m + 1)
                            nc.scalar.copy(pT[b % 2][:], ps_p[b % 2][:]).then_inc(p_copied, 1)
                    act.wait_ge(o_proj, free1(g))
                    for p in range(NP):
                        act.wait_ge(c_turned, g * NP + (p + 3))
                        for half in range(2):
                            last = nc.scalar.activation(cT[p % 2][:, half * S:(half + 1) * S],
                                                        ps_p[p % 2][:, 0, half * S:(half + 1) * S], ACT.Identity,
                                                        bias=bv[:, half:half + 1])
                        last.then_inc(c_copied, 1)
                    act.wait_ge(hh_turned, done(g))
                    act.wait_ge(h2_kept, free2(g))
                    nc.scalar.activation(h2T[j][:], ps_m[:], ACT.Identity, bias=cols[:, C_LN2B:C_LN2B + 1],
                                         scale=cols[:, C_LN2W:C_LN2W + 1]).then_inc(h2_ready, 1)
                    act.wait_ge(routed, done(g))
                    nc.scalar.copy(group_tiles(w["logits"], g),
                                   ps_m[:, 0:TILES * NE].rearrange("p (n e) -> p n e", e=NE)).then_inc(logits_ready, 1)

        @block.vector
        def _(dve):
            for h4 in range(RG):
                nc.vector.tensor_reduce(qmask[:, h4:h4 + 1], w["headsel"][:, h4:H:RG], AX.X, ALU.add).then_inc(mask_made, 1)
            dve.wait_ge(mask_made, 4)
            nc.vector.tensor_scalar(qmask[:], qmask[:], float(HD) ** -0.5, None, ALU.mult).then_inc(mask_made, 1)
            dve.wait_ge(mask_made, 5)
            dve.wait_ge(weights_in, NW * 16)
            dve.sem_inc(q_read, CREDIT)
            dve.sem_inc(shifted, 1)
            dve.sem_inc(c_ready, 1)
            with dve.Fori(0, G // 2) as it:
                for j in range(2):
                    g = it * 2 + j
                    x2 = group_tiles(w["x2"], g)
                    ln1.moments(dve, x2, j, g)
                    ln1.normalise(dve, x2, xh[j], j, g).then_inc(xh_ready, 1)
                    dve.wait_ge(q_proj, done(g))
                    for h4 in range(RG):
                        last = nc.vector.tensor_scalar(qx[j][:, :, h4, :], ps_m[:].rearrange("p (b s) -> p b s", b=GB),
                                                       cols[:, C_QKV:C_QKV + 1], qmask[:, h4:h4 + 1], ALU.add, ALU.mult)
                    last.then_inc(q_read, 1)
                    for u in range(NU):
                        n = g * NU + u
                        dve.wait_ge(scored, n + 1)
                        sc = ps_s[:].rearrange("p r x s -> p (r x) s")
                        nc.vector.tensor_reduce(top[u % 2][:], sc, AX.X, ALU.max).then_inc(maxed, 1)
                        dve.wait_ge(maxed, n + 1)
                        nc.vector.tensor_tensor(prob[u % 2][:].rearrange("p r x s -> p (r x) s"), sc,
                                                top[u % 2][:].unsqueeze(2).to_broadcast([P, RG * 2 * UB, S]),
                                                ALU.subtract).then_inc(shifted, 1)
                        for pr in range(2):
                            m = n * 2 + pr
                            dve.wait_ge(mixed, n * UB + (2 * pr + 4))
                            for half in range(2):
                                rows = slice(half * S, (half + 1) * S)
                                last = nc.vector.reciprocal(rden[pr][rows, :, :], mix[rows, :, :, half, HD])
                            last.then_inc(inverted, 1)
                            dve.wait_ge(inverted, m + 1)
                            for half in range(2):
                                rows = slice(half * S, (half + 1) * S)
                                b0 = u * UB + 2 * pr
                                dst = cx[j][rows, b0:b0 + 2, :, :, :].rearrange("p b r x d -> p (b r) x d")
                                last = nc.vector.tensor_tensor(
                                    dst, mix[rows, :, :, half, 0:HD],
                                    rden[pr][rows, :, :].unsqueeze(3).to_broadcast([S, 2 * RG, 2, HD]), ALU.mult)
                            last.then_inc(c_ready, 1)
                    dve.wait_ge(o_proj, done(g))
                    nc.vector.tensor_tensor(h[j][:], x2, tiles_m, ALU.add).then_inc(h_added, 1)
                    dve.wait_ge(h_added, g + 1)
                    nc.vector.tensor_tensor(h[j][:], h[j][:], bo[:].unsqueeze(1).to_broadcast([P, TILES, D]),
                                            ALU.add).then_inc(h_ready, 1)
                    dve.wait_ge(h_ready, g + 1)
                    nc.vector.tensor_tensor(group_tiles(w["x1"], g), h[j][:], x2, ALU.add)
                    ln2.moments(dve, h[j], j, g)
                    ln2.normalise(dve, h[j], hh[j], j, g).then_inc(hh_ready, 1)


def moe_stage(nc, a, w, out, sem):
    NJ = NE * FC
    HB = 4
    GB_ = 2 * FC
    NT = NTOK // P
    w_in = [sem(f"mo_w_in{e}") for e in range(NE)]
    b_in, b1_turned, b1_ready = sem("mo_b_in"), sem("mo_b1_turned"), sem("mo_b1_ready")
    stored = [sem("mo_stored0"), sem("mo_stored1")]
    (exped, route, ranked, share_ready, we_copied, we_turned, weT_ready, biased, hidden, gelued, used,
     combined, o_ready) = (sem("mo_" + n) for n in (
         "exped", "route", "ranked", "share_ready", "we_copied", "we_turned", "weT_ready", "biased",
         "hidden", "gelued", "used", "combined", "o_ready"))
    with ExitStack() as ctx:
        def mem(name, shape, n=2):
            return [ctx.enter_context(nc.sbuf_tensor(f"mo_{name}{i}", shape, F32)) for i in range(n)]

        def bank(name, shape, n):
            return [ctx.enter_context(nc.psum_tensor(f"mo_{name}{i}", shape, F32)) for i in range(n)]

        w1, = mem("w1", [P, NE, FH], 1)
        w2, = mem("w2", [P, NE, FC, D], 1)
        b1_rows, = mem("b1_rows", [NJ, P], 1)
        b1, = mem("b1", [P, NE, FC], 1)
        b2, = mem("b2", [NE, D], 1)
        share, = mem("share", [P, NT, NE], 1)
        first, second, cand, ps = mem("rt", [P, NT, NE], 4)
        m1, m2, r1, r2 = mem("rs", [P, NT], 4)
        rank, = mem("rank", [P, NE], 1)
        we = mem("we", [P, TILES, NE])
        weT = mem("weT", [NE, GT])
        gel = mem("gel", [P, GT], GB_)
        acc = mem("acc", [P, TILES, D])
        fin = mem("fin", [P, TILES, D])
        ps_h = bank("ps_h", [P, GT], HB)
        ps_y = bank("ps_y", [P, TILES, D], 2)
        ps_w_all, = bank("ps_w", [P, GT], 1)
        ps_w = ps_w_all[0:NE, :]
        ps_b, = bank("ps_b", [P, TILES, D], 1)
        ln = LayerNorm(nc, ctx, sem, w, "mo_ln")
        block = ctx.enter_context(nc.Block())
        outv = out.rearrange("b s d -> (b s) d")

        @block.sync
        def _(sp):
            sp.dma_start(b1_rows[:], a["L0_ffn_b1"].rearrange("e (c p) -> (e c) p", p=P)).then_inc(b_in, 16)
            sp.dma_start(b2[:], a["L0_ffn_b2"]).then_inc(b_in, 16)
            for e in range(NE):
                sp.dma_start(w1[:, e, :], a["L0_ffn_w1"][e]).then_inc(w_in[e], 16)
                sp.dma_start(w2[:, e, :, :], a["L0_ffn_w2"][e].rearrange("(c p) d -> p c d", p=P)).then_inc(w_in[e], 16)
            with sp.Fori(0, G // 2) as it:
                for j in range(2):
                    g = it * 2 + j
                    sp.wait_ge(o_ready, g + 1)
                    sp.dma_start(outv[bass.ds(g * GT, GT), :].rearrange("(n p) d -> p n d", p=P), fin[j][:]
                                 ).then_inc(stored[j], 16)
            for j in range(2):
                sp.wait_ge(stored[j], 16 * (1 + G // 2))

        @block.gpsimd
        def _(pool):
            for e in range(NE):
                nc.gpsimd.memset(rank[:, e:e + 1], float(NE - e)).then_inc(ranked, 1)
            for j in range(2):
                pool.sem_inc(stored[j], 16)
            with pool.Fori(0, G // 2) as it:
                for j in range(2):
                    ln.root(pool, w["halfpow"], j, it * 2 + j)

        @block.tensor
        def _(pe):
            pe.sem_inc(we_turned, CREDIT)
            pe.sem_inc(used, 2)
            for e in range(NE):
                pe.wait_ge(w_in[e], 32)
            pe.wait_ge(b_in, 32)
            nc.tensor.transpose(ps_w_all[:, 0:NJ], b1_rows[:], w["ident"][0:NJ, 0:NJ]).then_inc(b1_turned, 1)
            with pe.Fori(0, G // 2) as it:
                for j in range(2):
                    g = it * 2 + j
                    h2 = group_cols(w["h2T"], g)

                    def up(e):
                        for c in range(FC):
                            m = e * FC + c
                            pe.wait_ge(gelued, g * NJ + (m + 1))
                            nc.tensor.matmul(ps_h[m % HB][:], w1[:, e, c * P:(c + 1) * P], h2, start=True, stop=True
                                             ).then_inc(hidden, 1)

                    def down(e):
                        pe.wait_ge(gelued, g * NJ + (e * FC + FC + HB))
                        pe.wait_ge(combined, g * NE + (e + 1))
                        for n in range(TILES):
                            for c in range(FC):
                                last = nc.tensor.matmul(ps_y[e % 2][:, n, :],
                                                        gel[(e * FC + c) % GB_][:, n * P:(n + 1) * P],
                                                        w2[:, e, c, :], start=(c == 0), stop=(c == FC - 1))
                        last.then_inc(used, 1)
                    up(0)
                    pe.wait_ge(we_copied, g + 1)
                    pe.wait_ge(weT_ready, g + 1)
                    for n in range(TILES):
                        last = nc.tensor.transpose(ps_w[:, n * P:(n + 1) * P], we[j][:, n, :], w["ident"][:])
                    last.then_inc(we_turned, 1)
                    up(1)
                    pe.wait_ge(weT_ready, g + 2)
                    pe.wait_ge(combined, g * NE + 2)
                    for n in range(TILES):
                        last = nc.tensor.matmul(ps_b[:, n, :], weT[j][:, n * P:(n + 1) * P], b2[:], start=True, stop=True)
                    last.then_inc(biased, 1)
                    for e in range(2, NE):
                        down(e - 2)
                        up(e)
                    down(NE - 2)
                    down(NE - 1)

        @block.scalar
        def _(act):
            act.sem_inc(gelued, HB)
            act.wait_ge(b1_turned, 1)
            nc.scalar.copy(b1[:].rearrange("p e c -> p (e c)"), ps_w_all[:, 0:NJ]).then_inc(b1_ready, 1)
            act.wait_ge(b1_ready, 1)
            act.sem_inc(weT_ready, 1)
            act.wait_ge(route, 2)
            nc.scalar.activation(ps[:], ps[:], ACT.Exp).then_inc(exped, 1)
            with act.Fori(0, G // 2) as it:
                for j in range(2):
                    g = it * 2 + j
                    for e in range(NE):
                        act.wait_ge(used, g * NE + (e + 1))
                        for c in range(FC):
                            m = e * FC + c
                            act.wait_ge(hidden, g * NJ + (m + 1))
                            nc.scalar.activation(gel[m % GB_][:], ps_h[m % HB][:], ACT.Gelu_apprx_tanh,
                                                 bias=b1[:, e, c:c + 1]).then_inc(gelued, 1)
                        if e == 0:
                            act.wait_ge(we_turned, done(g))
                            nc.scalar.copy(weT[j][:], ps_w).then_inc(weT_ready, 1)

        @block.vector
        def _(dve):
            count = [0]

            def link(ins):
                count[0] += 1
                ins.then_inc(route, 1)
                dve.wait_ge(route, count[0])

            lg = w["logits"]
            wide = [P, NT, NE]
            link(nc.vector.tensor_reduce(m1[:], lg[:], AX.X, ALU.max))
            link(nc.vector.tensor_tensor(ps[:], lg[:], m1[:].unsqueeze(2).to_broadcast(wide), ALU.subtract))
            dve.wait_ge(exped, 1)
            dve.wait_ge(ranked, NE)

            def pick(src, m, r, onehot):
                link(nc.vector.tensor_reduce(m[:], src[:], AX.X, ALU.max))
                link(nc.vector.tensor_tensor(cand[:], src[:], m[:].unsqueeze(2).to_broadcast(wide), ALU.is_equal))
                link(nc.vector.tensor_tensor(cand[:], cand[:], rank[:].unsqueeze(1).to_broadcast(wide), ALU.mult))
                link(nc.vector.tensor_reduce(r[:], cand[:], AX.X, ALU.max))
                link(nc.vector.tensor_tensor(onehot[:], cand[:], r[:].unsqueeze(2).to_broadcast(wide), ALU.is_equal))
            pick(ps, m1, r1, first)
            link(nc.vector.scalar_tensor_tensor(out=share[:], in0=first[:], scalar=-4.0, in1=ps[:], op0=ALU.mult, op1=ALU.add))
            pick(share, m2, r2, second)
            link(nc.vector.tensor_tensor(m1[:], m1[:], m2[:], ALU.add))
            link(nc.vector.reciprocal(m1[:], m1[:]))
            link(nc.vector.tensor_tensor(first[:], first[:], second[:], ALU.add))
            link(nc.vector.tensor_tensor(first[:], first[:], ps[:], ALU.mult))
            link(nc.vector.tensor_tensor(share[:], first[:], m1[:].unsqueeze(2).to_broadcast(wide), ALU.mult))
            dve.sem_inc(combined, 2)
            with dve.Fori(0, G // 2) as it:
                for j in range(2):
                    g = it * 2 + j
                    dve.wait_ge(we_turned, free2(g))
                    nc.vector.tensor_copy(we[j][:], group_tiles(share, g)).then_inc(we_copied, 1)
                    dve.wait_ge(we_copied, g + 1)
                    dve.wait_ge(biased, g + 1)
                    nc.vector.tensor_tensor(acc[j][:], group_tiles(w["x1"], g), ps_b[:], ALU.add).then_inc(share_ready, 1)
                    for e in range(NE):
                        dve.wait_ge(used, g * NE + (e + 3))
                        if e == 0:
                            dve.wait_ge(share_ready, g + 1)
                        else:
                            dve.wait_ge(combined, g * NE + (e + 2))
                        for n in range(TILES):
                            last = nc.vector.scalar_tensor_tensor(out=acc[j][:, n, :], in0=ps_y[e % 2][:, n, :],
                                                                  scalar=we[j][:, n, e:e + 1], in1=acc[j][:, n, :],
                                                                  op0=ALU.mult, op1=ALU.add)
                        last.then_inc(combined, 1)
                    dve.wait_ge(combined, g * NE + (NE + 2))
                    ln.moments(dve, acc[j], j, g)
                    dve.wait_ge(stored[j], it * 16 + 16)
                    ln.normalise(dve, acc[j], fin[j], j, g).then_inc(o_ready, 1)


_OUT_SHAPE = (64, 64, 128)


def kernel(**inputs):
    import numpy as _np
    import concourse.bacc as _bacc
    from concourse import mybir as _mybir
    from concourse.bass_utils import run_bass_kernel_spmd as _run

    nc = _bacc.Bacc("TRN2", target_bir_lowering=False, num_devices=1)
    arrays, args = {}, {}
    for name in inputs:
        v = _np.ascontiguousarray(inputs[name])
        arrays[f"in_{name}_dram"] = v
        args[name] = nc.dram_tensor(f"in_{name}_dram", v.shape, _mybir.dt.from_np(v.dtype), kind="ExternalInput").ap()
    out = nc.dram_tensor("out_0_dram", _OUT_SHAPE, F32, kind="ExternalOutput").ap()
    decoder_layer(nc, args, out)
    r = _run(nc, [arrays], core_ids=[0])
    return r.results[0]["out_0_dram"]
```

```python
from contextlib import ExitStack

import concourse.bass as bass
from concourse import mybir

F32 = mybir.dt.float32
I32 = mybir.dt.int32
ALU = mybir.AluOpType
ACT = mybir.ActivationFunctionType
AX = mybir.AxisListType

P = 128
B, S, D = 64, 64, 128
NTOK = B * S
H, HD = 16, 8
TAPS = 4
GT = 512
G = NTOK // GT
GB = GT // S
TILES = GT // P
PAD = S + TAPS - 1
CH = GT // B
NCH = S // CH
HC = CH // 2
XE, XH = 8, 256
XC = XH // P
XK = 64
NE, FH = 8, 512
FC = FH // P
NORM_EPS = 1e-6
LN_EPS = 1e-5
CREDIT = 2

K_, Q_, V_, O_ = 0, 1, 2, 3
COLS = ["L0_attn_bk", "L0_attn_bq", "L0_attn_bv", "L0_attn_bk_conv", "L0_attn_bq_conv", "L0_attn_bv_conv",
        "L0_ffn_ln1_w", "L0_ffn_ln1_b", "L0_ffn_ln2_w", "L0_ffn_ln2_b"]
C_LN1W, C_LN1B, C_LN2W, C_LN2B = 6, 7, 8, 9
C_BETA, C_NORMW, C_FOLD, C_QKV, C_EPS, C_ONE, C_LNEPS = 10, 11, 12, 15, 18, 19, 20
NCOL = 24


def done(g):
    return g + (1 + CREDIT)


def free2(g):
    return g + 1


def free1(g):
    return g + 2


def dram_ap(t, offset, dims):
    return bass.AP(tensor=t.tensor, offset=offset, ap=[list(d) for d in dims])


def decoder_layer(nc, a, out):
    with ExitStack() as whole:
        def keep(name, shape, dt=F32):
            return whole.enter_context(nc.sbuf_tensor(name, shape, dt))

        def sem(name):
            return whole.enter_context(nc.semaphore(name))

        w = {
            "ident": keep("ident", [P, P]),
            "headsel": keep("headsel", [P, H]),
            "samehead": keep("samehead", [P, P]),
            "halfpow": keep("halfpow", [P, TILES * H]),
            "wT": keep("wT", [P, 4, P]),
            "wbT": keep("wbT", [P, H, HD]),
            "pinT": keep("pinT", [P, XE * XC, P]),
            "poutT": keep("poutT", [P, XE * XC, P]),
            "cols": keep("cols", [P, NCOL]),
            "taps": keep("taps", [P, 3, TAPS]),
            "bo_row": keep("bo_row", [P, D]),
        }
        scr = {n: nc.dram_tensor(n, shape, F32, kind="Internal").ap()
               for n, shape in (("k_scr", [P, NTOK]), ("q_scr", [P, NTOK]), ("gate_scr", [XE, NTOK]),
                                ("x1_scr", [P, NTOK]), ("x2_scr", [P, NTOK]))}
        w["idle_dve"], w["idle_pool"] = keep("idle_dve", [P, 1]), keep("idle_pool", [P, 4])
        weights_stage(nc, a, w, sem)

        w["bT"] = keep("bT", [P, S, B])
        with ExitStack() as early:
            for name, shape in (("vT", [P, S, B]),
                                ("kT", [P, S, B]), ("qT", [P, S, B]), ("ss", [P, G, 2 * TILES * H])):
                w[name] = early.enter_context(nc.sbuf_tensor(name, shape, F32))
            project_stage(nc, a, w, sem)
            scale_stage(nc, w, sem)
            delta_stage(nc, a, w, scr, sem)
        w["x1"] = keep("x1", [P, G * TILES, D])
        w["x1T"] = keep("x1T", [P, NTOK])
        mix_in_stage(nc, a, w, sem)
        w["x2"] = keep("x2", [P, G * TILES, D])
        xattn_stage(nc, w, scr, sem)
        w["h2T"] = w["x1T"]
        w["logits"] = keep("logits", [P, G * TILES, NE])
        attend_stage(nc, a, w, sem)
        moe_stage(nc, a, w, out, sem)


def weights_stage(nc, a, w, sem):
    raw_in, col_in, made, set_up, turned, moved_even, moved_odd, folded = (
        sem(n) for n in ("raw_in", "col_in", "made", "set_up", "turned", "moved_even", "moved_odd", "folded"))
    with ExitStack() as ctx:
        raw = ctx.enter_context(nc.sbuf_tensor("raw", [P, 4, D], F32))
        raw_b = ctx.enter_context(nc.sbuf_tensor("raw_b", [H, D], F32))
        raw_pin = ctx.enter_context(nc.sbuf_tensor("raw_pin", [P, XE * XC, D], F32))
        raw_pout = ctx.enter_context(nc.sbuf_tensor("raw_pout", [P, XE, XH], F32))
        NT = 4 + XE * XC * 2
        bank = [ctx.enter_context(nc.psum_tensor(f"turn{i}", [P, 4, P], F32)) for i in range(2)]
        bank_b = ctx.enter_context(nc.psum_tensor("turn_b", [P, H], F32))
        cols, taps = w["cols"], w["taps"]
        n_small = len(COLS) + 3 + 3 + 3
        block = ctx.enter_context(nc.Block())

        @block.sync
        def _(sp):
            for i, n in enumerate(("L0_attn_Wk", "L0_attn_Wq", "L0_attn_Wv", "L0_attn_Wo")):
                sp.dma_start(raw[:, i, :], a[n]).then_inc(raw_in, 16)
            sp.dma_start(raw_b[:], a["L0_attn_Wbeta"]).then_inc(raw_in, 16)
            sp.dma_start(raw_pin[:], a["L0_xattn_proj_in"].rearrange("e (c p) i -> p (e c) i", p=P)).then_inc(raw_in, 16)
            sp.dma_start(raw_pout[:], a["L0_xattn_proj_out"].rearrange("e i d -> i e d")).then_inc(raw_in, 16)
            sp.wait_ge(raw_in, 7 * 16)

        @block.scalar
        def _(act):
            for i, n in enumerate(COLS):
                act.dma_start(cols[:, i:i + 1], dram_ap(a[n], 0, [[1, P], [1, 1]])).then_inc(col_in, 16)
            for i, n in enumerate(("L0_attn_wk_conv", "L0_attn_wq_conv", "L0_attn_wv_conv")):
                act.dma_start(taps[:, i, :], a[n]).then_inc(col_in, 16)
            act.dma_start(cols[:, C_BETA:C_BETA + 1],
                          dram_ap(a["L0_attn_bbeta"], 0, [[1, H], [0, HD], [1, 1]])).then_inc(col_in, 16)
            act.dma_start(cols[:, C_NORMW:C_NORMW + 1],
                          dram_ap(a["L0_attn_norm_w"], 0, [[0, H], [1, HD], [1, 1]])).then_inc(col_in, 16)
            act.dma_start(w["bo_row"][:], dram_ap(a["L0_attn_bo"], 0, [[0, P], [1, D]])).then_inc(col_in, 16)
            for i in range(3):
                act.dma_start(cols[:, C_QKV + i:C_QKV + i + 1],
                              dram_ap(a["L0_ffn_b_qkv"], i * D, [[1, P], [1, 1]])).then_inc(col_in, 16)
            act.wait_ge(turned, 1)
            nc.scalar.copy(w["wT"][:], bank[0][:]).then_inc(moved_even, 1)
            for b in range(2, NT // 4, 2):
                act.wait_ge(turned, b + 1)
                t = 4 * (b - 1)
                dst = w["pinT"] if t < XE * XC else w["poutT"]
                nc.scalar.copy(dst[:, t % (XE * XC):t % (XE * XC) + 4, :], bank[0][:]).then_inc(moved_even, 1)

        @block.gpsimd
        def _(pool):
            ident, headsel = w["ident"], w["headsel"]
            nc.gpsimd.memset(ident[:], 0.0).then_inc(made, 1)
            nc.gpsimd.memset(headsel[:], 1.0).then_inc(made, 1)
            nc.gpsimd.memset(w["samehead"][:], 1.0).then_inc(made, 1)
            nc.gpsimd.memset(w["halfpow"][:], -0.5).then_inc(set_up, 1)
            pool.wait_ge(made, 3)
            nc.gpsimd.affine_select(out=ident[:], in_=ident[:], compare_op=ALU.not_equal, fill=1.0, base=0,
                                    pattern=[[-1, P]], channel_multiplier=1).then_inc(set_up, 1)
            nc.gpsimd.affine_select(out=headsel[:], in_=headsel[:], compare_op=ALU.is_ge, fill=0.0, base=0,
                                    pattern=[[-HD, H]], channel_multiplier=1).then_inc(made, 1)
            same = w["samehead"][:].rearrange("p (h d) -> p h d", d=HD)
            nc.gpsimd.affine_select(out=same, in_=same, compare_op=ALU.is_ge, fill=0.0, base=0,
                                    pattern=[[-HD, H], [0, HD]], channel_multiplier=1).then_inc(made, 1)
            pool.wait_ge(made, 5)
            nc.gpsimd.affine_select(out=headsel[:], in_=headsel[:], compare_op=ALU.is_ge, fill=0.0, base=HD - 1,
                                    pattern=[[HD, H]], channel_multiplier=-1).then_inc(set_up, 1)
            nc.gpsimd.affine_select(out=same, in_=same, compare_op=ALU.is_ge, fill=0.0, base=HD - 1,
                                    pattern=[[HD, H], [0, HD]], channel_multiplier=-1).then_inc(set_up, 1)

        @block.tensor
        def _(pe):
            pe.wait_ge(set_up, 4)
            pe.wait_ge(raw_in, 7 * 16)
            for b in range(NT // 4):
                if b >= 2:
                    pe.wait_ge(moved_odd if b % 2 else moved_even, b // 2)
                for i in range(4):
                    t = 4 * b + i - 4
                    if b == 0:
                        src = raw[:, i, :]
                    elif t < XE * XC:
                        src = raw_pin[:, t, :]
                    else:
                        t -= XE * XC
                        src = raw_pout[:, t // XC, (t % XC) * P:(t % XC + 1) * P]
                    last = nc.tensor.transpose(bank[b % 2][:, i, :], src, w["ident"][:])
                last.then_inc(turned, 1)
            nc.tensor.transpose(bank_b[:], raw_b[:], w["ident"][0:H, 0:H]).then_inc(turned, 1)

        @block.vector
        def _(dve):
            for b in range(1, NT // 4, 2):
                dve.wait_ge(turned, b + 1)
                t = 4 * (b - 1)
                dst = w["pinT"] if t < XE * XC else w["poutT"]
                nc.vector.tensor_copy(dst[:, t % (XE * XC):t % (XE * XC) + 4, :], bank[1][:]).then_inc(moved_odd, 1)
            dve.wait_ge(turned, NT // 4 + 1)
            nc.vector.tensor_copy(w["wbT"][:], bank_b[:].unsqueeze(2).to_broadcast([P, H, HD])).then_inc(set_up, 1)
            dve.wait_ge(col_in, 16 * (len(COLS) + 9))
            for i in range(3):
                nc.vector.scalar_tensor_tensor(out=cols[:, C_FOLD + i:C_FOLD + i + 1], in0=cols[:, i:i + 1],
                                               scalar=taps[:, i, TAPS - 1:TAPS], in1=cols[:, 3 + i:4 + i],
                                               op0=ALU.mult, op1=ALU.add).then_inc(folded, 1)
            nc.vector.memset(cols[:, C_EPS:C_EPS + 1], NORM_EPS).then_inc(folded, 1)
            nc.vector.memset(cols[:, C_ONE:C_ONE + 1], 1.0).then_inc(folded, 1)
            dve.wait_ge(folded, 5)


def project_stage(nc, a, w, sem):
    x_in = [sem("x_in0"), sem("x_in1")]
    (x_turned, xT_ready, proj_done, padded, first_tap, beta_ready, taps_done, sig_ready, v_ready, squared,
     summed, ss_ready, zeroed) = (sem("pr_" + n) for n in (
         "x_turned", "xT_ready", "proj_done", "padded", "first_tap", "beta_ready", "taps_done", "sig_ready",
         "v_ready", "squared", "summed", "ss_ready", "zeroed"))
    cols, taps = w["cols"], w["taps"]
    x = a["x"].rearrange("b s d -> (b s) d")
    with ExitStack() as ctx:
        def mem(name, shape):
            return [ctx.enter_context(nc.sbuf_tensor(f"{name}{i}", shape, F32)) for i in range(2)]

        xs = mem("xs", [P, TILES, D])
        xT = mem("xT", [P, GT])
        pad = mem("pad", [P, 3, GB, PAD])
        conv = mem("conv", [P, 3, GB, S])
        sig = mem("sig", [P, GB, S])
        sq = mem("sq", [P, 2, GB, S])
        ps_t = [ctx.enter_context(nc.psum_tensor(f"ps_t{i}", [P, GT], F32)) for i in range(2)]
        ps_p = [ctx.enter_context(nc.psum_tensor(f"ps_p{i}", [P, GB, S], F32)) for i in range(4)]
        ps_s = [ctx.enter_context(nc.psum_tensor(f"ps_s{i}", [P, 2 * TILES * H], F32)) for i in range(2)]

        def cols_of(t, g):
            return t[:, :, bass.ds(g * GB, GB)].rearrange("p t b -> p b t")

        block = ctx.enter_context(nc.Block())

        @block.sync
        def _(sp):
            def load(g, j):
                sp.dma_start(xs[j][:], x[bass.ds(g * GT, GT), :].rearrange("(n p) d -> p n d", p=P)
                             ).then_inc(x_in[j], 16)
            load(0, 0)
            load(1, 1)
            with sp.Fori(0, G // 2 - 1) as it:
                for j in range(2):
                    g = it * 2 + j
                    sp.wait_ge(x_turned, done(g))
                    load(g + 2, j)

        @block.tensor
        def _(pe):
            pe.sem_inc(x_turned, CREDIT)
            pe.sem_inc(summed, CREDIT)
            with pe.Fori(0, G // 2) as it:
                for j in range(2):
                    g = it * 2 + j
                    pe.wait_ge(x_in[j], it * 16 + 16)
                    pe.wait_ge(xT_ready, free2(g))
                    for i in range(TILES):
                        last = nc.tensor.transpose(ps_t[j][:, i * P:(i + 1) * P], xs[j][:, i, :], w["ident"][:])
                    last.then_inc(x_turned, 1)
                    pe.wait_ge(xT_ready, done(g))
                    for i in range(4):
                        if i < 3:
                            pe.wait_ge(first_tap, g * 3 + (i + 1))
                        else:
                            pe.wait_ge(beta_ready, free1(g))
                        lhsT = w["wT"][:, i, :] if i < 3 else w["wbT"][:].rearrange("p h d -> p (h d)")
                        nc.tensor.matmul(ps_p[i][:].rearrange("p b s -> p (b s)"), lhsT, xT[j][:],
                                         start=True, stop=True).then_inc(proj_done, 1)
                    pe.wait_ge(squared, done(g))
                    pe.wait_ge(ss_ready, free2(g))
                    sqv = sq[j][:].rearrange("p w b s -> p w (b s)")
                    for i in range(2):
                        for n in range(TILES):
                            o = (i * TILES + n) * H
                            last = nc.tensor.matmul(ps_s[j][:, o:o + H], sqv[:, i, n * P:(n + 1) * P],
                                                    w["headsel"][:], start=True, stop=True)
                    last.then_inc(summed, 1)

        @block.scalar
        def _(act):
            act.sem_inc(xT_ready, CREDIT)
            act.sem_inc(beta_ready, CREDIT)
            act.sem_inc(sig_ready, CREDIT)
            act.sem_inc(ss_ready, CREDIT)
            act.sem_inc(first_tap, 3)
            act.wait_ge(zeroed, 2)
            with act.Fori(0, G // 2) as it:
                for j in range(2):
                    g = it * 2 + j
                    act.wait_ge(x_turned, done(g))
                    act.wait_ge(proj_done, g * 4)
                    nc.scalar.copy(xT[j][:], ps_t[j][:]).then_inc(xT_ready, 1)
                    for i in range(3):
                        act.wait_ge(proj_done, g * 4 + (i + 1))
                        if i == 0:
                            act.wait_ge(v_ready, free2(g))
                            act.wait_ge(squared, free2(g))
                        nc.scalar.activation(pad[j][:, i, :, TAPS - 1:PAD], ps_p[i][:], ACT.Identity,
                                             bias=cols[:, i:i + 1]).then_inc(padded, 1)
                        nc.scalar.activation(conv[j][:, i, :, :], ps_p[i][:], ACT.Identity,
                                             bias=cols[:, C_FOLD + i:C_FOLD + i + 1],
                                             scale=taps[:, i, TAPS - 1:TAPS]).then_inc(first_tap, 1)
                    act.wait_ge(proj_done, g * 4 + 4)
                    nc.scalar.activation(cols_of(w["bT"], g), ps_p[3][:], ACT.Sigmoid,
                                         bias=cols[:, C_BETA:C_BETA + 1]).then_inc(beta_ready, 1)
                    act.wait_ge(taps_done, g * 9 + 9)
                    nc.scalar.activation(sig[j][:], conv[j][:, V_, :, :], ACT.Sigmoid).then_inc(sig_ready, 1)
                    act.wait_ge(summed, done(g))
                    nc.scalar.copy(w["ss"][:, bass.ds(g, 1), :].rearrange("p o n -> p (o n)"), ps_s[j][:]).then_inc(ss_ready, 1)

        @block.vector
        def _(dve):
            dve.sem_inc(v_ready, CREDIT)
            nc.vector.memset(pad[0][:, :, :, 0:TAPS - 1], 0.0).then_inc(zeroed, 1)
            nc.vector.memset(pad[1][:, :, :, 0:TAPS - 1], 0.0).then_inc(zeroed, 1)
            with dve.Fori(0, G // 2) as it:
                for j in range(2):
                    g = it * 2 + j
                    for t in range(TAPS - 1):
                        for i in range(3):
                            o = 3 * t + i
                            if t == 0:
                                dve.wait_ge(padded, g * 3 + (i + 1))
                                dve.wait_ge(first_tap, g * 3 + (i + 4))
                            else:
                                dve.wait_ge(taps_done, g * 9 + (o - 2))
                            dst = conv[j][:, i, :, :]
                            if t == TAPS - 2 and i < V_:
                                dst = cols_of(w["kT"] if i == K_ else w["qT"], g)
                            nc.vector.scalar_tensor_tensor(out=dst, in0=pad[j][:, i, :, t:t + S],
                                                           scalar=taps[:, i, t:t + 1], in1=conv[j][:, i, :, :],
                                                           op0=ALU.mult, op1=ALU.add).then_inc(taps_done, 1)
                    dve.wait_ge(sig_ready, done(g))
                    nc.vector.tensor_tensor(cols_of(w["vT"], g), conv[j][:, V_, :, :], sig[j][:],
                                            ALU.mult).then_inc(v_ready, 1)

        @block.gpsimd
        def _(pool):
            pool.sem_inc(squared, CREDIT)
            with pool.Fori(0, G // 2) as it:
                for j in range(2):
                    g = it * 2 + j
                    pool.wait_ge(taps_done, g * 9 + 8)
                    pool.wait_ge(summed, free2(g))
                    nc.gpsimd.tensor_tensor(sq[j][:, 0, :, :], cols_of(w["kT"], g), cols_of(w["kT"], g), ALU.mult)
                    nc.gpsimd.tensor_tensor(sq[j][:, 1, :, :], cols_of(w["qT"], g), cols_of(w["qT"], g),
                                            ALU.mult).then_inc(squared, 1)


def scale_stage(nc, w, sem):
    rooted, inverted, spread, turned, scaled, v_scaled = (
        sem("sc_" + n) for n in ("rooted", "inverted", "spread", "turned", "scaled", "v_scaled"))
    with ExitStack() as ctx:
        rexp = [ctx.enter_context(nc.sbuf_tensor(f"rexp{i}", [P, 2, TILES, H, HD], F32)) for i in range(2)]
        ps_r = [ctx.enter_context(nc.psum_tensor(f"ps_r{i}", [P, 2, GB, S], F32)) for i in range(2)]
        ss = w["ss"]

        def cols_of(t, g):
            return t[:, :, bass.ds(g * GB, GB)].rearrange("p t b -> p b t")

        block = ctx.enter_context(nc.Block())

        @block.scalar
        def _(act):
            nc.scalar.activation(ss[:], ss[:], ACT.Sqrt).then_inc(rooted, 1)

        @block.vector
        def _(dve):
            dve.sem_inc(v_scaled, CREDIT)
            dve.sem_inc(scaled, CREDIT * 2)
            dve.wait_ge(rooted, 1)
            nc.vector.tensor_scalar(ss[:], ss[:], NORM_EPS, None, ALU.add).then_inc(rooted, 1)
            dve.wait_ge(rooted, 2)
            nc.vector.reciprocal(ss[:], ss[:]).then_inc(inverted, 1)
            with dve.Fori(0, G // 2) as it:
                for j in range(2):
                    g = it * 2 + j
                    dve.wait_ge(turned, done(g))
                    kT, qT, vT, bT = (cols_of(w[n], g) for n in ("kT", "qT", "vT", "bT"))
                    nc.vector.tensor_tensor(kT, kT, ps_r[j][:, 0, :, :], ALU.mult)
                    nc.vector.tensor_tensor(vT, vT, ps_r[j][:, 0, :, :], ALU.mult).then_inc(scaled, 1)
                    nc.vector.tensor_tensor(qT, qT, ps_r[j][:, 1, :, :], ALU.mult).then_inc(scaled, 1)
                    dve.wait_ge(scaled, g * 2 + (1 + 2 * CREDIT))
                    nc.vector.tensor_tensor(vT, vT, bT, ALU.mult).then_inc(v_scaled, 1)

        @block.gpsimd
        def _(pool):
            pool.sem_inc(spread, CREDIT)
            pool.wait_ge(inverted, 1)
            with pool.Fori(0, G // 2) as it:
                for j in range(2):
                    g = it * 2 + j
                    pool.wait_ge(turned, free2(g))
                    src = ss[:, bass.ds(g, 1), :].rearrange("p o n -> p (o n)").unsqueeze(2)
                    nc.gpsimd.tensor_copy(rexp[j][:].rearrange("p w n h d -> p (w n h) d"),
                                          src.to_broadcast([P, 2 * TILES * H, HD])).then_inc(spread, 1)

        @block.tensor
        def _(pe):
            pe.sem_inc(turned, CREDIT)
            with pe.Fori(0, G // 2) as it:
                for j in range(2):
                    g = it * 2 + j
                    pe.wait_ge(spread, done(g))
                    pe.wait_ge(scaled, g * 2 + 2)
                    for i in range(2):
                        for n in range(TILES):
                            last = nc.tensor.transpose(
                                ps_r[j][:, i, :, :].rearrange("p b s -> p (b s)")[:, n * P:(n + 1) * P],
                                rexp[j][:, i, n, :, :].rearrange("p h d -> p (h d)"), w["ident"][:])
                    last.then_inc(turned, 1)


def delta_stage(nc, a, w, scr, sem):
    stored = [sem(f"kq_stored{c}") for c in range(NCH)]
    kq_in = [sem("kq_in0"), sem("kq_in1")]
    (state_op, qs_made, o_summed, o_copied, dist_ready, hit, weighed, gated, gates_copied, gates_stored,
     const, picks_in, empty) = (sem("de_" + n) for n in (
         "state_op", "qs_made", "o_summed", "o_copied", "dist_ready", "hit", "weighed", "gated", "gates_copied",
         "gates_stored", "const", "picks_in", "empty"))
    OPS = 6
    NIT = NCH // 2
    TURN = 2 * CH
    PAIRS = B // 2
    GC = PAIRS // NIT * S
    with ExitStack() as ctx:
        def mem(name, shape, n=2, dt=F32):
            return [ctx.enter_context(nc.sbuf_tensor(f"{name}{i}", shape, dt)) for i in range(n)]

        krep = mem("krep", [P, HD, CH, B])
        qrep = mem("qrep", [P, HD, CH, B])
        qs = mem("qs", [P, HD, HC, B])
        state = mem("state", [P, HD, B])
        prod, = mem("prod", [P, HD, B], 1)
        rise, = mem("rise", [P, HD, B], 1)
        pred, bpred, upd = mem("small", [P, B], 3)
        pick_w, = mem("pick_w", [P, PAIRS, S], 1)
        pick_e, = mem("pick_e", [P, PAIRS, S], 1, I32)
        dist = mem("dist", [P, GC])
        wsel = mem("wsel", [P, GC])
        negs, = mem("negs", [P, XE], 1)
        esel, = mem("esel", [P, XE, 2, XE], 1)
        gates, = mem("gates", [2 * XE, GC], 1)
        ps_o = [ctx.enter_context(nc.psum_tensor(f"ps_o{i}", [P, 512], F32)) for i in range(2)]
        ps_g = ctx.enter_context(nc.psum_tensor("ps_g", [2 * XE, GC], F32))
        oT = w["bT"]
        block = ctx.enter_context(nc.Block())

        @block.sync
        def _(sp):
            def load(first, cb):
                for t, name in ((krep, "k_scr"), (qrep, "q_scr")):
                    for i in range(HD):
                        src = dram_ap(scr[name], first + i * NTOK,
                                      [[HD * NTOK, H], [0, HD], [1, CH * B]])
                        sp.dma_start(t[cb][:, i, :, :].rearrange("p t b -> p (t b)"), src).then_inc(kq_in[cb], 16)
            for cb in range(2):
                sp.wait_ge(stored[cb], 32)
                load(cb * CH * B, cb)
            for c in range(2, NCH):
                sp.wait_ge(stored[c], 32)
            with sp.Fori(1, NIT) as it:
                for cb in range(2):
                    first = sp.snap((it * 2 + cb) * (CH * B))
                    sp.wait_ge(qs_made, it * TURN + ((cb - 1) * CH + CREDIT * HC))
                    load(first, cb)

        @block.scalar
        def _(act):
            for c in range(NCH):
                for t, name in ((w["kT"], "k_scr"), (w["qT"], "q_scr")):
                    act.dma_start(scr[name][:, c * CH * B:(c + 1) * CH * B],
                                  t[:, c * CH:(c + 1) * CH, :].rearrange("p t b -> p (t b)")).then_inc(stored[c], 16)
            for t, name in ((pick_w, "ctx_512"), (pick_e, "itok_BxS2xS_0_7")):
                for b2 in range(2):
                    src = dram_ap(a[name], b2 * XK * S, [[S, XK], [2 * XK * S, PAIRS], [1, S]])
                    act.dma_start(t[b2 * XK:(b2 + 1) * XK, :, :], src).then_inc(picks_in, 16)
            act.sem_inc(o_copied, CREDIT)
            act.sem_inc(gates_stored, 32)
            act.wait_ge(const, 3 * XE + 1)
            act.wait_ge(picks_in, 64)
            with act.Fori(0, NIT) as it:
                part = pick_e[:, bass.ds(it * (PAIRS // NIT), PAIRS // NIT), :].rearrange("p n s -> p (n s)")
                for e in range(XE):
                    n = it * XE + e
                    nc.scalar.activation(dist[e % 2][:], part, ACT.Abs, bias=negs[:, e:e + 1]).then_inc(dist_ready, 1)
                    act.wait_ge(dist_ready, n + 1)
                    act.wait_ge(gated, free2(n))
                    nc.scalar.activation(wsel[e % 2][:], dist[e % 2][:], ACT.Relu, bias=w["cols"][:, C_ONE:C_ONE + 1],
                                         scale=-1.0).then_inc(hit, 1)
                    if e % 2:
                        hc = it * 4 + e // 2
                        act.wait_ge(o_summed, done(hc))
                        nc.scalar.copy(oT[:, bass.ds(hc * HC, HC), :].rearrange("p t b -> p (t b)"),
                                       ps_o[(e // 2) % 2][:, 0:HC * B]).then_inc(o_copied, 1)
                act.wait_ge(gated, it * XE + (XE + CREDIT))
                act.wait_ge(gates_stored, it * 32 + 32)
                nc.scalar.copy(gates[:], ps_g[:]).then_inc(gates_copied, 1)
                act.wait_ge(gates_copied, it + 1)
                for b2 in range(2):
                    dst = dram_ap(scr["gate_scr"], it * (2 * GC) + b2 * S, [[NTOK, XE], [2 * S, PAIRS // NIT], [1, S]])
                    act.dma_start(dst, gates[b2 * XE:(b2 + 1) * XE, :].rearrange("e (n s) -> e n s", s=S)
                                  ).then_inc(gates_stored, 16)
            act.wait_ge(gates_stored, 32 * (NIT + 1))

        @block.gpsimd
        def _(pool):
            for e in range(XE):
                nc.gpsimd.memset(negs[:, e:e + 1], float(-e)).then_inc(const, 1)
            nc.gpsimd.memset(esel[:], 0.0).then_inc(const, 1)
            pool.wait_ge(const, XE + 1)
            for e in range(XE):
                for b2 in range(2):
                    nc.gpsimd.memset(esel[b2 * XK:(b2 + 1) * XK, e, b2, e:e + 1], 1.0).then_inc(const, 1)
            pool.wait_ge(const, 3 * XE + 1)
            pool.wait_ge(picks_in, 64)
            pool.sem_inc(qs_made, CREDIT * HC)
            with pool.Fori(0, NIT) as it:
                part = pick_w[:, bass.ds(it * (PAIRS // NIT), PAIRS // NIT), :].rearrange("p n s -> p (n s)")
                for t in range(TURN):
                    hc, cb = t // HC, t // CH
                    if t % HC == 0:
                        pool.wait_ge(o_summed, free2(it * 4 + hc))
                    if t % CH == 0:
                        pool.wait_ge(kq_in[cb], it * 256 + 256)
                    if t % 2:
                        pool.wait_ge(hit, it * XE + (t // 2 + 1))
                    pool.wait_ge(state_op, it * (TURN * OPS) + (t + 1) * OPS)
                    nc.gpsimd.tensor_tensor(qs[hc % 2][:, :, t % HC, :], state[(t + 1) % 2][:],
                                            qrep[cb][:, :, t % CH, :], ALU.mult).then_inc(qs_made, 1)
                    if t % 2:
                        e = t // 2
                        nc.gpsimd.tensor_tensor(wsel[e % 2][:], wsel[e % 2][:], part, ALU.mult).then_inc(weighed, 1)

        @block.vector
        def _(dve):
            nc.vector.memset(state[0][:], 0.0).then_inc(empty, 1)
            dve.wait_ge(empty, 1)
            with dve.Fori(0, NIT) as it:
                for t in range(TURN):
                    cb = t // CH
                    k = krep[cb][:, :, t % CH, :]
                    old, new = state[t % 2], state[(t + 1) % 2]
                    ops = it * (TURN * OPS)
                    beta = w["bT"][:, bass.ds(it * TURN + t, 1), :].rearrange("p o b -> p (o b)")
                    v = w["vT"][:, bass.ds(it * TURN + t, 1), :].rearrange("p o b -> p (o b)")
                    if t % CH == 0:
                        dve.wait_ge(kq_in[cb], it * 256 + 256)
                    nc.vector.tensor_tensor(prod[:], old[:], k, ALU.mult).then_inc(state_op, 1)
                    dve.wait_ge(state_op, ops + (t * OPS + 1))
                    nc.vector.tensor_reduce(pred[:], prod[:].rearrange("p i b -> p b i"), AX.X, ALU.add).then_inc(state_op, 1)
                    dve.wait_ge(state_op, ops + (t * OPS + 2))
                    nc.vector.tensor_tensor(bpred[:], pred[:], beta, ALU.mult).then_inc(state_op, 1)
                    dve.wait_ge(state_op, ops + (t * OPS + 3))
                    nc.vector.tensor_tensor(upd[:], v, bpred[:], ALU.subtract).then_inc(state_op, 1)
                    dve.wait_ge(state_op, ops + (t * OPS + 4))
                    nc.vector.tensor_tensor(rise[:], k, upd[:].unsqueeze(1).to_broadcast([P, HD, B]),
                                            ALU.mult).then_inc(state_op, 1)
                    dve.wait_ge(state_op, ops + (t * OPS + 5))
                    dve.wait_ge(qs_made, it * TURN + (t + CREDIT * HC))
                    nc.vector.tensor_tensor(new[:], old[:], rise[:], ALU.add).then_inc(state_op, 1)
                    dve.wait_ge(state_op, ops + (t * OPS + 6))

        @block.tensor
        def _(pe):
            pe.sem_inc(o_summed, CREDIT)
            pe.sem_inc(gated, CREDIT)
            pe.wait_ge(const, 3 * XE + 1)
            with pe.Fori(0, NIT) as it:
                for hc in range(4):
                    n = it * 4 + hc
                    pe.wait_ge(qs_made, n * HC + (HC + CREDIT * HC))
                    pe.wait_ge(o_copied, free2(n))
                    for i in range(HD):
                        last = nc.tensor.matmul(ps_o[hc % 2][:, 0:HC * B], w["ident"][:],
                                                qs[hc % 2][:, i, :, :].rearrange("p t b -> p (t b)"),
                                                start=(i == 0), stop=(i == HD - 1))
                    last.then_inc(o_summed, 1)
                    for e in range(2 * hc, 2 * hc + 2):
                        pe.wait_ge(weighed, it * XE + (e + 1))
                        if e == 0:
                            pe.wait_ge(gates_copied, it)
                        nc.tensor.matmul(ps_g[:], esel[:, e, :, :].rearrange("p b e -> p (b e)"), wsel[e % 2][:],
                                         start=(e == 0), stop=(e == XE - 1)).then_inc(gated, 1)


def carry_dve(nc, w):
    nc.vector.memset(w["idle_dve"][:], 0.0)


def carry_pool(nc, w, place=0):
    nc.gpsimd.tensor_tensor(w["idle_pool"][:, place:place + 1], w["halfpow"][:, 0:1], w["halfpow"][:, 0:1], ALU.mult)


class LayerNorm:

    def __init__(self, nc, ctx, sem, w, name):
        self.nc, self.w = nc, w
        self.stats, self.mean, self.var, self.rstd = (
            [ctx.enter_context(nc.sbuf_tensor(f"{name}_{what}{i}", [P, TILES, n], F32)) for i in range(2)]
            for what, n in (("stats", 6), ("mean", 2), ("var", 1), ("rstd", 1)))
        self.stats_done, self.mean_done, self.var_done, self.rstd_done = (
            sem(f"{name}_{what}") for what in ("stats_done", "mean_done", "var_done", "rstd_done"))

    def moments(self, dve, y, j, g):
        for n in range(TILES):
            last = self.nc.vector.bn_stats(self.stats[j][:, n, :], y[:, n, :])
        last.then_inc(self.stats_done, 1)
        dve.wait_ge(self.stats_done, g + 1)
        carry_dve(self.nc, self.w)
        for n in range(TILES):
            last = self.nc.vector.bn_aggr(self.mean[j][:, n, :], self.stats[j][:, n, :])
        last.then_inc(self.mean_done, 1)
        dve.wait_ge(self.mean_done, g + 1)
        self.nc.vector.tensor_scalar(self.var[j][:], self.mean[j][:, :, 1:2], LN_EPS, None, ALU.add
                                     ).then_inc(self.var_done, 1)

    def root(self, pool, halfpow, j, g):
        pool.wait_ge(self.var_done, g + 1)
        self.nc.gpsimd.tensor_tensor(self.rstd[j][:].rearrange("p n o -> p (n o)"),
                                     self.var[j][:].rearrange("p n o -> p (n o)"), halfpow[:, 0:TILES],
                                     ALU.pow).then_inc(self.rstd_done, 1)

    def normalise(self, dve, y, dst, j, g):
        dve.wait_ge(self.rstd_done, g + 1)
        for n in range(TILES):
            last = self.nc.vector.tensor_scalar(dst[:, n, :], y[:, n, :], self.mean[j][:, n, 0:1],
                                                self.rstd[j][:, n, :], ALU.subtract, ALU.mult)
        return last


def group_tiles(t, g):
    return t[:, bass.ds(g * TILES, TILES), :]


def group_cols(t, g):
    return t[:, bass.ds(g * GT, GT)]


def all_groups(eng, group):
    group(0, 0)
    with eng.Fori(0, (G - 2) // 2) as it:
        group(it * 2 + 1, 1)
        group(it * 2 + 2, 0)
    group(G - 1, 1)


def first(g):
    return isinstance(g, int) and g == 0


def final(g):
    return isinstance(g, int) and g == G - 1


def mix_in_stage(nc, a, w, sem):
    x_in = [sem("mi_x_in0"), sem("mi_x_in1")]
    (squared, summed, rooted, inverted, normed, projected, biased, added, x1_ready, x1_turned, x1T_ready, x1_kept) = (
        sem("mi_" + n) for n in (
            "squared", "summed", "rooted", "inverted", "normed", "projected", "biased", "added", "x1_ready",
            "x1_turned", "x1T_ready", "x1_kept"))
    x = a["x"].rearrange("b s d -> (b s) d")
    cols = w["cols"]
    with ExitStack() as ctx:
        def mem(name, shape):
            return [ctx.enter_context(nc.sbuf_tensor(f"mi_{name}{i}", shape, F32)) for i in range(2)]

        def bank(name, shape):
            return [ctx.enter_context(nc.psum_tensor(f"mi_{name}{i}", shape, F32)) for i in range(2)]

        xs = mem("xs", [P, TILES, D])
        sq = mem("sq", [P, GB, S])
        rms = mem("rms", [P, GB, S])
        on = mem("on", [P, GB, S])
        y = mem("y", [P, TILES, D])
        x1 = mem("x1", [P, TILES, D])
        ps_s = bank("ps_s", [P, GB, S])
        ps_y = bank("ps_y", [P, TILES, D])
        ps_t = bank("ps_t", [P, TILES, P])
        ln = LayerNorm(nc, ctx, sem, w, "mi_ln")

        def cols_of(t, g):
            return t[:, :, bass.ds(g * GB, GB)].rearrange("p t b -> p b t")

        block = ctx.enter_context(nc.Block())

        @block.sync
        def _(sp):
            def load(g, j):
                sp.dma_start(xs[j][:], x[bass.ds(g * GT, GT), :].rearrange("(n p) d -> p n d", p=P)
                             ).then_inc(x_in[j], 16)
            load(0, 0)
            load(1, 1)
            with sp.Fori(0, G // 2 - 1) as it:
                for j in range(2):
                    g = it * 2 + j
                    sp.wait_ge(added, g + 1)
                    load(g + 2, j)

        @block.scalar
        def _(act):
            def norms(x, j):
                if not isinstance(x, int) or x >= 2:
                    act.wait_ge(summed, x - 1)
                nc.scalar.activation(sq[j][:], cols_of(w["bT"], x), ACT.Square).then_inc(squared, 1)
                act.wait_ge(summed, x + 1)
                if not isinstance(x, int) or x >= 2:
                    act.wait_ge(normed, x - 1)
                nc.scalar.activation(rms[j][:], ps_s[j][:], ACT.Sqrt, bias=cols[:, C_EPS:C_EPS + 1], scale=1.0 / HD
                                     ).then_inc(rooted, 1)

            def group(g, j):
                if not final(g):
                    norms(g + 1, 1 - j)
                act.wait_ge(x1_turned, g + 1)
                nc.scalar.activation(group_cols(w["x1T"], g), ps_t[j][:].rearrange("p n d -> p (n d)"), ACT.Identity
                                     ).then_inc(x1T_ready, 1)
            norms(0, 0)
            all_groups(act, group)

        @block.tensor
        def _(pe):
            def project(x, j):
                pe.wait_ge(squared, x + 1)
                if not isinstance(x, int) or x >= 2:
                    pe.wait_ge(rooted, x - 1)
                nc.tensor.matmul(ps_s[j][:].rearrange("p b s -> p (b s)"), w["samehead"][:],
                                 sq[j][:].rearrange("p b s -> p (b s)"), start=True, stop=True).then_inc(summed, 1)
                pe.wait_ge(normed, x + 1)
                if not isinstance(x, int) or x >= 2:
                    pe.wait_ge(added, x - 1)
                for n in range(TILES):
                    last = nc.tensor.matmul(ps_y[j][:, n, :], on[j][:].rearrange("p b s -> p (b s)")[:, n * P:(n + 1) * P],
                                            w["wT"][:, O_, :], start=True, stop=True)
                last.then_inc(projected, 1)

            def group(g, j):
                if not final(g):
                    project(g + 1, 1 - j)
                pe.wait_ge(x1_ready, g + 1)
                if not isinstance(g, int) or g >= 2:
                    pe.wait_ge(x1T_ready, g - 1)
                for n in range(TILES):
                    last = nc.tensor.transpose(ps_t[j][:, n, :], x1[j][:, n, :], w["ident"][:])
                last.then_inc(x1_turned, 1)
            project(0, 0)
            all_groups(pe, group)

        @block.vector
        def _(dve):
            def norms(x, j):
                dve.wait_ge(rooted, x + 1)
                nc.vector.reciprocal(rms[j][:], rms[j][:]).then_inc(inverted, 1)
                dve.wait_ge(inverted, x + 1)
                nc.vector.scalar_tensor_tensor(out=on[j][:], in0=cols_of(w["bT"], x),
                                               scalar=cols[:, C_NORMW:C_NORMW + 1], in1=rms[j][:],
                                               op0=ALU.mult, op1=ALU.mult).then_inc(normed, 1)

            def group(g, j):
                dve.wait_ge(biased, g + 1)
                dve.wait_ge(projected, g + 1)
                nc.vector.tensor_tensor(y[j][:], xs[j][:], ps_y[j][:], ALU.add).then_inc(added, 1)
                dve.wait_ge(added, g + 1)
                ln.moments(dve, y[j], j, g)
                if not final(g):
                    norms(g + 1, 1 - j)
                if not isinstance(g, int) or g >= 2:
                    dve.wait_ge(x1_turned, g - 1)
                    dve.wait_ge(x1_kept, g - 1)
                ln.normalise(dve, y[j], x1[j], j, g).then_inc(x1_ready, 1)
            norms(0, 0)
            all_groups(dve, group)

        @block.gpsimd
        def _(pool):
            def add_bias(x, j):
                pool.wait_ge(x_in[j], (x - j) * 8 + 16)
                nc.gpsimd.tensor_tensor(xs[j][:], xs[j][:], w["bo_row"][:].unsqueeze(1).to_broadcast([P, TILES, D]),
                                        ALU.add).then_inc(biased, 1)

            def group(g, j):
                if not final(g):
                    add_bias(g + 1, 1 - j)
                ln.root(pool, w["halfpow"], j, g)
                pool.wait_ge(x1_ready, g + 1)
                if not isinstance(g, int):
                    carry_pool(nc, w)
                nc.gpsimd.tensor_copy(group_tiles(w["x1"], g), x1[j][:]).then_inc(x1_kept, 1)
            add_bias(0, 0)
            all_groups(pool, group)


def xattn_stage(nc, w, scr, sem):
    gates_in = [sem("xa_gates_in0"), sem("xa_gates_in1")]
    NJ = XE * XC
    NB = 4
    TURN_AT, ADD_AT, NORM_AT = 4, 6, 10
    (hidden, relued, used, sum_copied, turned, added, x2_ready) = (sem("xa_" + n) for n in (
        "hidden", "relued", "used", "sum_copied", "turned", "added", "x2_ready"))
    with ExitStack() as ctx:
        def mem(name, shape, n=2):
            return [ctx.enter_context(nc.sbuf_tensor(f"xa_{name}{i}", shape, F32)) for i in range(n)]

        def bank(name, shape, n):
            return [ctx.enter_context(nc.psum_tensor(f"xa_{name}{i}", shape, F32)) for i in range(n)]

        gates = mem("gates", [P, XE, GT])
        hid = mem("hid", [P, GT], NB)
        oT = mem("oT", [P, GT])
        y = mem("y", [P, TILES, D])
        ps_h = bank("ps_h", [P, GT], NB)
        ps_o = bank("ps_o", [P, GT], 2)
        ps_t, = bank("ps_t", [P, TILES, D], 1)
        ln = LayerNorm(nc, ctx, sem, w, "xa_ln")
        block = ctx.enter_context(nc.Block())

        @block.sync
        def _(sp):
            def load(g, j):
                src = dram_ap(scr["gate_scr"], g * GT, [[0, P], [NTOK, XE], [1, GT]])
                sp.dma_start(gates[j][:], src).then_inc(gates_in[j], 16)
            load(0, 0)
            load(1, 1)
            with sp.Fori(0, G // 2 - 1) as it:
                for j in range(2):
                    sp.wait_ge(relued, it * (2 * NJ) + ((j + 1) * NJ + NB))
                    load(it * 2 + (j + 2), j)

        @block.tensor
        def _(pe):
            def turn(x, j):
                pe.wait_ge(sum_copied, x + 1)
                if not first(x):
                    pe.wait_ge(added, x)
                for n in range(TILES):
                    last = nc.tensor.transpose(ps_t[:, n, :], oT[j][:, n * P:(n + 1) * P], w["ident"][:])
                last.then_inc(turned, 1)

            def group(g, j):
                x1T = group_cols(w["x1T"], g)

                def out_part(m):
                    pe.wait_ge(relued, g * NJ + (m + 1 + NB))
                    if m == 0 and (not isinstance(g, int) or g >= 2):
                        pe.wait_ge(sum_copied, g - 1)
                    nc.tensor.matmul(ps_o[j][:], w["poutT"][:, m, :], hid[m % NB][:], start=(m == 0),
                                     stop=(m == NJ - 1)).then_inc(used, 1)
                for m in range(NJ):
                    pe.wait_ge(relued, g * NJ + (m + 1))
                    nc.tensor.matmul(ps_h[m % NB][:], w["pinT"][:, m, :], x1T, start=True, stop=True
                                     ).then_inc(hidden, 1)
                    if m >= 2:
                        out_part(m - 2)
                    if m == TURN_AT and not first(g):
                        turn(g - 1, 1 - j)
                out_part(NJ - 2)
                out_part(NJ - 1)
            pe.sem_inc(used, NB)
            all_groups(pe, group)
            turn(G - 1, 1)

        @block.scalar
        def _(act):
            def group(g, j):
                act.wait_ge(used, g * NJ + (NJ + NB))
                if not isinstance(g, int) or g >= 2:
                    act.wait_ge(turned, g - 1)
                nc.scalar.copy(oT[j][:], ps_o[j][:]).then_inc(sum_copied, 1)
            all_groups(act, group)

        @block.vector
        def _(dve):
            dve.sem_inc(relued, NB)

            def add(x, j):
                dve.wait_ge(turned, x + 1)
                nc.vector.tensor_tensor(y[j][:], group_tiles(w["x1"], x), ps_t[:], ALU.add).then_inc(added, 1)
                dve.wait_ge(added, x + 1)
                ln.moments(dve, y[j], j, x)

            def normalise(x, j):
                ln.normalise(dve, y[j], group_tiles(w["x2"], x), j, x).then_inc(x2_ready, 1)

            def group(g, j):
                dve.wait_ge(gates_in[j], (g - j) * 8 + 16)
                for m in range(NJ):
                    dve.wait_ge(hidden, g * NJ + (m + 1))
                    dve.wait_ge(used, g * NJ + (m + 1))
                    nc.vector.scalar_tensor_tensor(out=hid[m % NB][:], in0=ps_h[m % NB][:], scalar=0.0,
                                                   in1=gates[j][:, m // XC, :], op0=ALU.max, op1=ALU.mult
                                                   ).then_inc(relued, 1)
                    if m == ADD_AT and not first(g):
                        add(g - 1, 1 - j)
                    if m == NORM_AT and not first(g):
                        normalise(g - 1, 1 - j)
            all_groups(dve, group)
            add(G - 1, 1)
            normalise(G - 1, 1)

        @block.gpsimd
        def _(pool):
            all_groups(pool, lambda g, j: ln.root(pool, w["halfpow"], j, g))


def attend_stage(nc, a, w, sem):
    UB = 2
    NU = GB // UB
    RG = 4
    NPR = GB // 2
    AHEAD = 2
    NW = 11
    NT = NTOK // P
    weights_in = sem("at_weights_in")
    (moments, rooted, xh_ready, xh_turned, h1_ready, twin_ready, q_proj, q_read, k_proj, k_read, v_proj, v_read,
     scored, maxed, shifted, exped, p_turned, p_copied, mixed, inverted, c_ready, c_turned, c_copied, o_proj,
     x2_biased, h_ready, summed, hh_ready, hh_turned, h2_ready, routed, logits_ready, h2_kept, const, mask_made) = (
         sem("at_" + n) for n in (
             "moments", "rooted", "xh_ready", "xh_turned", "h1_ready", "twin_ready", "q_proj", "q_read", "k_proj",
             "k_read", "v_proj", "v_read", "scored", "maxed", "shifted", "exped", "p_turned", "p_copied", "mixed",
             "inverted", "c_ready", "c_turned", "c_copied", "o_proj", "x2_biased", "h_ready", "summed", "hh_ready",
             "hh_turned", "h2_ready", "routed", "logits_ready", "h2_kept", "const", "mask_made"))
    cols = w["cols"]
    with ExitStack() as ctx:
        def mem(name, shape, n=2):
            return [ctx.enter_context(nc.sbuf_tensor(f"at_{name}{i}", shape, F32)) for i in range(n)]

        def bank(name, shape, n):
            return [ctx.enter_context(nc.psum_tensor(f"at_{name}{i}", shape, F32)) for i in range(n)]

        wqkv, = mem("wqkv", [P, 3, D], 1)
        wo, = mem("wo", [P, 2, D], 1)
        wg, = mem("wg", [P, NE], 1)
        bo, = mem("bo", [P, D], 1)
        bv, = mem("bv", [P, 2], 1)
        qmask, = mem("qmask", [P, RG], 1)
        stats, = mem("stats", [P, NT, 6], 1)
        mean, = mem("mean", [P, NT, 2], 1)
        var, = mem("var", [P, NT], 1)
        rstd, = mem("rstd", [P, NT, 1], 1)
        xh = mem("xh", [P, TILES, D])
        h1T, = mem("h1T", [P, GB, 2, S], 1)
        qx = mem("qx", [P, GB, RG, S])
        kx = mem("kx", [P, GB, RG, S])
        vx = mem("vx", [P, GB * 2, 2, 2, 2, HD + 1])
        prob = mem("prob", [P, 2 * UB, RG, S], NU)
        pT = mem("pT", [P, RG, P], UB)
        top = mem("top", [P, 2 * UB * RG])
        rden = mem("rden", [P, UB * 8])
        cx = mem("cx", [P, GB * 8, HD])
        cT, = mem("cT", [P, NPR, 2, 2, S], 1)
        xb = mem("xb", [P, TILES, D])
        h = mem("h", [P, TILES, D])
        hh = mem("hh", [P, TILES, D])
        h2T = mem("h2T", [P, GT])
        ps_s = bank("ps_s", [P, 2 * UB, RG, S], 2)
        ps_p = bank("ps_p", [P, RG, P], UB)
        ps_c, = bank("ps_c", [P, 512], 1)
        ps_m, = bank("ps_m", [P, 512], 1)
        mix = ps_c[:, 0:UB * 16 * (HD + 1)].rearrange("p (n x y h d) -> p n x y h d", x=2, y=2, h=2, d=HD + 1)
        mix_slots = ps_c[:, 0:UB * 16 * (HD + 1)].rearrange("p (n h d) -> p n h d", h=2, d=HD + 1)
        ln2 = LayerNorm(nc, ctx, sem, w, "at_ln2")
        tiles_m = ps_m[:].rearrange("p (n d) -> p n d", n=TILES)
        batches_m = ps_m[:].rearrange("p (b s) -> p b s", b=GB)
        block = ctx.enter_context(nc.Block())

        @block.sync
        def _(sp):
            sp.dma_start(wqkv[:].rearrange("p a d -> p (a d)"), a["L0_ffn_w_qkv"]).then_inc(weights_in, 16)
            for half in range(2):
                for b2 in range(2):
                    src = dram_ap(a["L0_ffn_w_o"], half * HD * D, [[2 * HD * D, H // 2], [D, HD], [1, D]])
                    sp.dma_start(wo[b2 * 64:(b2 + 1) * 64, half, :], src).then_inc(weights_in, 16)
                    src = dram_ap(a["L0_ffn_b_qkv"], 2 * D + half * HD, [[2 * HD, H // 2], [1, HD], [1, 1]])
                    sp.dma_start(bv[b2 * 64:(b2 + 1) * 64, half:half + 1], src).then_inc(weights_in, 16)
            sp.dma_start(wg[:], a["L0_ffn_w_gate"]).then_inc(weights_in, 16)
            sp.dma_start(bo[:], dram_ap(a["L0_ffn_b_o"], 0, [[0, P], [1, D]])).then_inc(weights_in, 16)
            sp.wait_ge(weights_in, NW * 16)

        @block.gpsimd
        def _(pool):
            for t in (*vx, *kx, cT):
                nc.gpsimd.memset(t[:], 0.0).then_inc(const, 1)
            pool.wait_ge(const, 5)
            for j in range(2):
                for half in range(2):
                    nc.gpsimd.memset(vx[j][half * S:(half + 1) * S, :, half, :, :, HD:HD + 1], 1.0).then_inc(const, 1)
            pool.wait_ge(const, 9)
            pool.wait_ge(moments, NT + 2)
            nc.gpsimd.tensor_tensor(rstd[:].rearrange("p n o -> p (n o)"), var[:], w["halfpow"][:, 0:NT], ALU.pow
                                    ).then_inc(rooted, 1)
            pool.wait_ge(weights_in, NW * 16)

            def output(x, j):
                ln2.root(pool, w["halfpow"], j, x)
                pool.wait_ge(h_ready, done(x))
                if not isinstance(x, int):
                    carry_pool(nc, w, 0)
                nc.gpsimd.tensor_tensor(group_tiles(w["x1"], x), h[j][:], group_tiles(w["x2"], x), ALU.add
                                        ).then_inc(summed, 1)
                pool.wait_ge(h2_ready, done(x))
                if not isinstance(x, int):
                    carry_pool(nc, w, 1)
                nc.gpsimd.tensor_copy(group_cols(w["h2T"], x), h2T[j][:]).then_inc(h2_kept, 1)

            def twin(x):
                pool.wait_ge(h1_ready, x + 1)
                if not isinstance(x, int):
                    carry_pool(nc, w, 3)
                nc.gpsimd.tensor_copy(h1T[:, :, 1, :], h1T[:, :, 0, :]).then_inc(twin_ready, 1)

            def group(g, j):
                if not final(g):
                    twin(g + 1)
                if not isinstance(g, int) or g >= 2:
                    pool.wait_ge(h_ready, free2(g))
                    carry_pool(nc, w, 2)
                nc.gpsimd.tensor_tensor(xb[j][:], group_tiles(w["x2"], g),
                                        bo[:].unsqueeze(1).to_broadcast([P, TILES, D]), ALU.add).then_inc(x2_biased, 1)
                if not first(g):
                    output(g - 1, 1 - j)
            pool.sem_inc(h2_kept, CREDIT)
            pool.sem_inc(summed, CREDIT)
            twin(0)
            all_groups(pool, group)
            output(G - 1, 1)

        @block.tensor
        def _(pe):
            pe.wait_ge(weights_in, NW * 16)
            pe.wait_ge(const, 9)
            pe.wait_ge(mask_made, 5)

            def turn_x(x, j):
                if not first(x):
                    pe.wait_ge(v_read, x * 2)
                    pe.wait_ge(logits_ready, x)
                pe.wait_ge(xh_ready, x + 1)
                for n in range(TILES):
                    last = nc.tensor.transpose(tiles_m[:, n, :], xh[j][:, n, :], w["ident"][:])
                last.then_inc(xh_turned, 1)

            def make_q(x):
                pe.wait_ge(h1_ready, x + 1)
                nc.tensor.matmul(ps_m[:], wqkv[:, 0, :], h1T[:, :, 0, :], start=True, stop=True).then_inc(q_proj, 1)

            def make_k(x):
                pe.wait_ge(q_read, x + 1)
                nc.tensor.matmul(ps_m[:], wqkv[:, 1, :], h1T[:, :, 0, :], start=True, stop=True).then_inc(k_proj, 1)

            def make_v(x, half):
                if half == 0:
                    pe.wait_ge(k_read, x + 1)
                    pe.wait_ge(twin_ready, x + 1)
                else:
                    pe.wait_ge(v_read, x * 2 + 1)
                for b in range(4):
                    last = nc.tensor.matmul(tiles_m[:, b, :], h1T[:, half * 4 + b, :, :].rearrange("p a s -> p (a s)"),
                                            wqkv[:, 2, :], start=True, stop=True)
                last.then_inc(v_proj, 1)

            def scores(n, j, u):
                if not isinstance(n, int) or n >= 2:
                    pe.wait_ge(shifted, n - 1)
                for b in range(UB):
                    for hp in range(2):
                        last = nc.tensor.matmul(
                            ps_s[u % 2][:, b * 2 + hp, :, :].rearrange("p r s -> p (r s)"),
                            qx[j][:, u * UB + b, 2 * hp:2 * hp + 2, :].rearrange("p h s -> p (h s)"),
                            kx[j][:, u * UB + b, :, :].rearrange("p r s -> p (r s)"), start=True, stop=True)
                last.then_inc(scored, 1)

            def turn_probs(n, u, b):
                pe.wait_ge(p_copied, n * UB + (b + 1))
                for rp in range(2):
                    for hp in range(2):
                        last = nc.tensor.transpose(
                            ps_p[b][:, rp * 2 + hp, :],
                            prob[u][:, b * 2 + hp, 2 * rp:2 * rp + 2, :].rearrange("p r s -> p (r s)"), w["ident"][:])
                last.then_inc(p_turned, 1)

            def mix_values(n, j, u, b):
                pe.wait_ge(p_copied, n * UB + (b + 3))
                for rp in range(2):
                    for hp in range(2):
                        last = nc.tensor.matmul(mix[:, b * 2 + rp, :, hp, :, :].rearrange("p x h d -> p x (h d)"),
                                                pT[b][:, rp * 2 + hp, :],
                                                vx[j][:, (u * UB + b) * 2 + rp, :, hp, :, :].rearrange(
                                                    "p x h d -> p x (h d)"), start=True, stop=True)
                last.then_inc(mixed, 1)

            def turn_mix(x, j, after_v):
                pe.wait_ge(c_ready, x * NU + NU)
                if after_v:
                    pe.wait_ge(v_read, x * 2 + 6)
                elif not first(x):
                    pe.wait_ge(logits_ready, x + 2)
                for p in range(NPR):
                    last = nc.tensor.transpose(tiles_m[:, p, :], cx[j][:, p * 16:p * 16 + 16, :].rearrange("p n d -> p (n d)"),
                                               w["ident"][:])
                last.then_inc(c_turned, 1)

            def make_output(x):
                pe.wait_ge(c_copied, x + 1)
                for p in range(NPR):
                    for half in range(2):
                        last = nc.tensor.matmul(tiles_m[:, p, :], cT[:, p, half, :, :].rearrange("p b s -> p (b s)"),
                                                wo[:, half, :], start=(half == 0), stop=(half == 1))
                last.then_inc(o_proj, 1)

            def turn_h(x, j):
                pe.wait_ge(hh_ready, x + 1)
                for n in range(TILES):
                    last = nc.tensor.transpose(tiles_m[:, n, :], hh[j][:, n, :], w["ident"][:])
                last.then_inc(hh_turned, 1)

            def route(x, j):
                pe.wait_ge(h2_ready, done(x))
                for n in range(TILES):
                    last = nc.tensor.matmul(ps_m[:, n * NE:(n + 1) * NE], h2T[j][:, n * P:(n + 1) * P], wg[:],
                                            start=True, stop=True)
                last.then_inc(routed, 1)

            def group(g, j):
                ahead, behind = not final(g), not first(g)
                for u in range(NU):
                    n = g * NU + u
                    if u < AHEAD:
                        scores(n + AHEAD, j, u + AHEAD)
                    elif ahead:
                        if u == AHEAD:
                            pe.wait_ge(q_read, g + 2)
                            pe.wait_ge(k_read, g + 2)
                        scores(n + AHEAD, 1 - j, u + AHEAD - NU)
                    pe.wait_ge(exped, n + 1)
                    turn_probs(n, u, 0)
                    turn_probs(n, u, 1)
                    if u == 0 and ahead:
                        turn_x(g + 1, 1 - j)
                    if u == 1 and ahead:
                        make_k(g + 1)
                    if u == 2 and ahead:
                        make_v(g + 1, 1)
                    if not (first(g) and u == 0):
                        pe.wait_ge(c_ready, n)
                    mix_values(n, j, u, 0)
                    if u == 0 and ahead:
                        make_q(g + 1)
                    if u == 2 and behind:
                        turn_mix(g - 1, 1 - j, ahead)
                    if u == 3 and behind:
                        turn_h(g - 1, 1 - j)
                    mix_values(n, j, u, 1)
                    if u == 1 and ahead:
                        make_v(g + 1, 0)
                    if u == 2 and behind:
                        make_output(g - 1)
                    if u == 3 and behind:
                        route(g - 1, 1 - j)

            turn_x(0, 0)
            make_q(0)
            make_k(0)
            make_v(0, 0)
            make_v(0, 1)
            pe.wait_ge(q_read, 1)
            for u in range(AHEAD):
                scores(u, 0, u)
            all_groups(pe, group)
            turn_mix(G - 1, 1, False)
            make_output(G - 1)
            turn_h(G - 1, 1)
            route(G - 1, 1)

        @block.scalar
        def _(act):
            act.sem_inc(p_copied, CREDIT)
            act.sem_inc(logits_ready, CREDIT)
            act.sem_inc(h2_ready, CREDIT)
            act.wait_ge(weights_in, NW * 16)
            act.wait_ge(const, 9)

            def read_h1(x):
                act.wait_ge(xh_turned, x + 1)
                nc.scalar.activation(h1T[:, :, 0, :], batches_m, ACT.Identity, bias=cols[:, C_LN1B:C_LN1B + 1],
                                     scale=cols[:, C_LN1W:C_LN1W + 1]).then_inc(h1_ready, 1)

            def read_k(x, j):
                act.wait_ge(k_proj, x + 1)
                for r in range(RG):
                    rows = slice(32 * r, 32 * r + 32)
                    last = nc.scalar.activation(kx[j][rows, :, r, :], batches_m[rows], ACT.Identity,
                                                bias=cols[rows, C_QKV + 1:C_QKV + 2])
                last.then_inc(k_read, 1)

            def read_v(x, j, half):
                act.wait_ge(v_proj, x * 2 + (half + 1))
                for r2 in range(2):
                    rows = slice(r2 * S, (r2 + 1) * S)
                    src = ps_m[rows, :].rearrange("p (n x y d) -> p n x y d", x=2, y=4, d=HD)[:, :, r2, :, :]
                    dst = vx[j][rows, half * GB:(half + 1) * GB, r2, :, :, 0:HD].rearrange("p n y h d -> p n (y h) d")
                    last = nc.scalar.activation(dst, src, ACT.Identity)
                last.then_inc(v_read, 1)

            def copy_turned(n, b):
                act.wait_ge(p_turned, n * UB + (b + 1))
                nc.scalar.activation(pT[b][:], ps_p[b][:], ACT.Identity).then_inc(p_copied, 1)

            def exp(n, u):
                act.wait_ge(shifted, n + 1)
                pv = prob[u][:].rearrange("p x r s -> p (x r s)")
                nc.scalar.activation(pv, pv, ACT.Exp).then_inc(exped, 1)

            def read_mix(x):
                act.wait_ge(c_turned, x + 1)
                src = ps_m[:].rearrange("p (n h s) -> p n h s", n=NPR, h=2)
                for b2 in range(2):
                    rows = slice(b2 * 64, (b2 + 1) * 64)
                    for half in range(2):
                        last = nc.scalar.activation(cT[rows, :, half, b2, :], src[rows, :, half, :], ACT.Identity,
                                                    bias=bv[rows, half:half + 1])
                last.then_inc(c_copied, 1)

            def read_h2(x, j):
                act.wait_ge(hh_turned, x + 1)
                act.wait_ge(h2_kept, free2(x))
                nc.scalar.activation(h2T[j][:], ps_m[:], ACT.Identity, bias=cols[:, C_LN2B:C_LN2B + 1],
                                     scale=cols[:, C_LN2W:C_LN2W + 1]).then_inc(h2_ready, 1)

            def read_logits(x):
                act.wait_ge(routed, x + 1)
                nc.scalar.activation(group_tiles(w["logits"], x),
                                     ps_m[:, 0:TILES * NE].rearrange("p (n e) -> p n e", e=NE), ACT.Identity
                                     ).then_inc(logits_ready, 1)

            def group(g, j):
                ahead, behind = not final(g), not first(g)
                for u in range(NU):
                    n = g * NU + u
                    copy_turned(n, 0)
                    copy_turned(n, 1)
                    if u == 0 and ahead:
                        read_h1(g + 1)
                    if u == 1 and ahead:
                        read_k(g + 1, 1 - j)
                    if u == 2 and ahead:
                        read_v(g + 1, 1 - j, 1)
                    if u < AHEAD or ahead:
                        exp(n + AHEAD, (u + AHEAD) % NU)
                    if u == 2 and behind:
                        read_mix(g - 1)
                    if u == 3 and behind:
                        read_h2(g - 1, 1 - j)
                    if u == 1 and ahead:
                        read_v(g + 1, 1 - j, 0)
                    if u == 3 and behind:
                        read_logits(g - 1)

            read_h1(0)
            read_k(0, 0)
            read_v(0, 0, 0)
            read_v(0, 0, 1)
            for u in range(AHEAD):
                exp(u, u)
            all_groups(act, group)
            read_mix(G - 1)
            read_h2(G - 1, 1)
            read_logits(G - 1)

        @block.vector
        def _(dve):
            for h4 in range(RG):
                nc.vector.tensor_reduce(qmask[:, h4:h4 + 1], w["headsel"][:, h4:H:RG], AX.X, ALU.add).then_inc(mask_made, 1)
            with dve.Fori(0, NT) as t:
                nc.vector.bn_stats(stats[:, bass.ds(t, 1), :].rearrange("p n s -> p (n s)"),
                                   w["x2"][:, bass.ds(t, 1), :].rearrange("p n d -> p (n d)")).then_inc(moments, 1)
            dve.wait_ge(moments, NT)
            for t in range(NT):
                last = nc.vector.bn_aggr(mean[:, t, :], stats[:, t, :])
            last.then_inc(moments, 1)
            dve.wait_ge(moments, NT + 1)
            nc.vector.tensor_scalar(var[:], mean[:, :, 1], LN_EPS, None, ALU.add).then_inc(moments, 1)
            dve.wait_ge(mask_made, 4)
            nc.vector.tensor_scalar(qmask[:], qmask[:], float(HD) ** -0.5, None, ALU.mult).then_inc(mask_made, 1)
            dve.wait_ge(mask_made, 5)
            dve.wait_ge(weights_in, NW * 16)
            dve.wait_ge(rooted, 1)
            dve.sem_inc(h_ready, CREDIT)

            def normalise_x(x, j):
                if not isinstance(x, int) or x >= 2:
                    dve.wait_ge(xh_turned, x - 1)
                for n in range(TILES):
                    t = bass.ds(x * TILES + n, 1)
                    last = nc.vector.tensor_scalar(xh[j][:, n, :], w["x2"][:, t, :].rearrange("p n d -> p (n d)"),
                                                   mean[:, t, 0:1].rearrange("p n o -> p (n o)"),
                                                   rstd[:, t, :].rearrange("p n o -> p (n o)"), ALU.subtract, ALU.mult)
                last.then_inc(xh_ready, 1)

            def read_q(x, j):
                dve.wait_ge(q_proj, x + 1)
                for h4 in range(RG):
                    last = nc.vector.tensor_scalar(qx[j][:, :, h4, :], batches_m, cols[:, C_QKV:C_QKV + 1],
                                                   qmask[:, h4:h4 + 1], ALU.add, ALU.mult)
                last.then_inc(q_read, 1)

            def shift(n, u):
                dve.wait_ge(scored, n + 1)
                sc = ps_s[u % 2][:].rearrange("p x r s -> p (x r) s")
                nc.vector.tensor_reduce(top[u % 2][:], sc, AX.X, ALU.max).then_inc(maxed, 1)
                dve.wait_ge(maxed, n + 1)
                nc.vector.tensor_tensor(prob[u][:].rearrange("p x r s -> p (x r) s"), sc,
                                        top[u % 2][:].unsqueeze(2).to_broadcast([P, 2 * UB * RG, S]),
                                        ALU.subtract).then_inc(shifted, 1)

            def divide(n, j, u):
                dve.wait_ge(mixed, n * UB + UB)
                for half in range(2):
                    rows = slice(half * S, (half + 1) * S)
                    last = nc.vector.reciprocal(rden[u % 2][rows, :], mix_slots[rows, :, half, HD])
                last.then_inc(inverted, 1)
                dve.wait_ge(inverted, n + 1)
                for half in range(2):
                    rows = slice(half * S, (half + 1) * S)
                    last = nc.vector.tensor_tensor(cx[j][rows, u * 16:u * 16 + 16, :], mix_slots[rows, :, half, 0:HD],
                                                   rden[u % 2][rows, :].unsqueeze(2).to_broadcast([S, UB * 8, HD]),
                                                   ALU.mult)
                last.then_inc(c_ready, 1)

            def residual(x, j):
                dve.wait_ge(x2_biased, x + 1)
                dve.wait_ge(summed, free2(x))
                dve.wait_ge(o_proj, x + 1)
                nc.vector.tensor_tensor(h[j][:], xb[j][:], tiles_m, ALU.add).then_inc(h_ready, 1)
                dve.wait_ge(h_ready, done(x))
                ln2.moments(dve, h[j], j, x)

            def normalise_h(x, j):
                ln2.normalise(dve, h[j], hh[j], j, x).then_inc(hh_ready, 1)

            def group(g, j):
                ahead, behind = not final(g), not first(g)
                for u in range(NU):
                    n = g * NU + u
                    if u == 0 and ahead:
                        normalise_x(g + 1, 1 - j)
                    if u > 0:
                        divide(n - 1, j, u - 1)
                    elif behind:
                        divide(n - 1, 1 - j, NU - 1)
                    if u == 3 and behind:
                        normalise_h(g - 1, 1 - j)
                    if u < AHEAD or ahead:
                        shift(n + AHEAD, (u + AHEAD) % NU)
                    if u == 0 and ahead:
                        read_q(g + 1, 1 - j)
                    if u == 2 and behind:
                        residual(g - 1, 1 - j)

            normalise_x(0, 0)
            read_q(0, 0)
            for u in range(AHEAD):
                shift(u, u)
            all_groups(dve, group)
            divide(G * NU - 1, 1, NU - 1)
            residual(G - 1, 1)
            normalise_h(G - 1, 1)


def moe_stage(nc, a, w, out, sem):
    NJ = NE * FC
    HB = 4
    GB_ = 2 * FC
    NT = NTOK // P
    w_in = [sem(f"mo_w_in{e}") for e in range(NE)]
    b_in, b1_turned, b1_ready = sem("mo_b_in"), sem("mo_b1_turned"), sem("mo_b1_ready")
    stored = [sem("mo_stored0"), sem("mo_stored1")]
    (exped, route, ranked, share_ready, we_copied, we_turned, weT_ready, biased, hidden, gelued, used,
     combined, o_ready) = (sem("mo_" + n) for n in (
         "exped", "route", "ranked", "share_ready", "we_copied", "we_turned", "weT_ready", "biased",
         "hidden", "gelued", "used", "combined", "o_ready"))
    with ExitStack() as ctx:
        def mem(name, shape, n=2):
            return [ctx.enter_context(nc.sbuf_tensor(f"mo_{name}{i}", shape, F32)) for i in range(n)]

        def bank(name, shape, n):
            return [ctx.enter_context(nc.psum_tensor(f"mo_{name}{i}", shape, F32)) for i in range(n)]

        w1, = mem("w1", [P, NE, FH], 1)
        w2, = mem("w2", [P, NE, FC, D], 1)
        b1_rows, = mem("b1_rows", [NJ, P], 1)
        b1, = mem("b1", [P, NE, FC], 1)
        b2, = mem("b2", [NE, D], 1)
        share, = mem("share", [P, NT, NE], 1)
        first, second, cand, ps = mem("rt", [P, NT, NE], 4)
        m1, m2, r1, r2 = mem("rs", [P, NT], 4)
        rank, = mem("rank", [P, NE], 1)
        we = mem("we", [P, TILES, NE])
        weT = mem("weT", [NE, GT])
        gel = mem("gel", [P, GT], GB_)
        acc = mem("acc", [P, TILES, D])
        fin = mem("fin", [P, TILES, D])
        ps_h = bank("ps_h", [P, GT], HB)
        ps_y = bank("ps_y", [P, TILES, D], 2)
        ps_w_all, = bank("ps_w", [P, GT], 1)
        ps_w = ps_w_all[0:NE, :]
        ps_b, = bank("ps_b", [P, TILES, D], 1)
        ln = LayerNorm(nc, ctx, sem, w, "mo_ln")
        block = ctx.enter_context(nc.Block())
        outv = out.rearrange("b s d -> (b s) d")

        @block.sync
        def _(sp):
            sp.dma_start(b1_rows[:], a["L0_ffn_b1"].rearrange("e (c p) -> (e c) p", p=P)).then_inc(b_in, 16)
            sp.dma_start(b2[:], a["L0_ffn_b2"]).then_inc(b_in, 16)
            for e in range(NE):
                sp.dma_start(w1[:, e, :], a["L0_ffn_w1"][e]).then_inc(w_in[e], 16)
                sp.dma_start(w2[:, e, :, :], a["L0_ffn_w2"][e].rearrange("(c p) d -> p c d", p=P)).then_inc(w_in[e], 16)
            with sp.Fori(0, G // 2) as it:
                for j in range(2):
                    g = it * 2 + j
                    sp.wait_ge(o_ready, g + 1)
                    sp.dma_start(outv[bass.ds(g * GT, GT), :].rearrange("(n p) d -> p n d", p=P), fin[j][:]
                                 ).then_inc(stored[j], 16)
            for j in range(2):
                sp.wait_ge(stored[j], 16 * (1 + G // 2))

        @block.gpsimd
        def _(pool):
            for e in range(NE):
                nc.gpsimd.memset(rank[:, e:e + 1], float(NE - e)).then_inc(ranked, 1)
            for j in range(2):
                pool.sem_inc(stored[j], 16)
            with pool.Fori(0, G // 2) as it:
                for j in range(2):
                    ln.root(pool, w["halfpow"], j, it * 2 + j)

        @block.tensor
        def _(pe):
            pe.sem_inc(we_turned, CREDIT)
            pe.sem_inc(used, 2)
            for e in range(NE):
                pe.wait_ge(w_in[e], 32)
            pe.wait_ge(b_in, 32)
            nc.tensor.transpose(ps_w_all[:, 0:NJ], b1_rows[:], w["ident"][0:NJ, 0:NJ]).then_inc(b1_turned, 1)
            with pe.Fori(0, G // 2) as it:
                for j in range(2):
                    g = it * 2 + j
                    h2 = group_cols(w["h2T"], g)

                    def up(e):
                        for c in range(FC):
                            m = e * FC + c
                            pe.wait_ge(gelued, g * NJ + (m + 1))
                            nc.tensor.matmul(ps_h[m % HB][:], w1[:, e, c * P:(c + 1) * P], h2, start=True, stop=True
                                             ).then_inc(hidden, 1)

                    def down(e):
                        pe.wait_ge(gelued, g * NJ + (e * FC + FC + HB))
                        pe.wait_ge(combined, g * NE + (e + 1))
                        for n in range(TILES):
                            for c in range(FC):
                                last = nc.tensor.matmul(ps_y[e % 2][:, n, :],
                                                        gel[(e * FC + c) % GB_][:, n * P:(n + 1) * P],
                                                        w2[:, e, c, :], start=(c == 0), stop=(c == FC - 1))
                        last.then_inc(used, 1)
                    up(0)
                    pe.wait_ge(we_copied, g + 1)
                    pe.wait_ge(weT_ready, g + 1)
                    for n in range(TILES):
                        last = nc.tensor.transpose(ps_w[:, n * P:(n + 1) * P], we[j][:, n, :], w["ident"][:])
                    last.then_inc(we_turned, 1)
                    up(1)
                    pe.wait_ge(weT_ready, g + 2)
                    pe.wait_ge(combined, g * NE + 2)
                    for n in range(TILES):
                        last = nc.tensor.matmul(ps_b[:, n, :], weT[j][:, n * P:(n + 1) * P], b2[:], start=True, stop=True)
                    last.then_inc(biased, 1)
                    for e in range(2, NE):
                        down(e - 2)
                        up(e)
                    down(NE - 2)
                    down(NE - 1)

        @block.scalar
        def _(act):
            act.sem_inc(gelued, HB)
            act.wait_ge(b1_turned, 1)
            nc.scalar.copy(b1[:].rearrange("p e c -> p (e c)"), ps_w_all[:, 0:NJ]).then_inc(b1_ready, 1)
            act.wait_ge(b1_ready, 1)
            act.sem_inc(weT_ready, 1)
            act.wait_ge(route, 2)
            nc.scalar.activation(ps[:], ps[:], ACT.Exp).then_inc(exped, 1)
            with act.Fori(0, G // 2) as it:
                for j in range(2):
                    g = it * 2 + j
                    for e in range(NE):
                        act.wait_ge(used, g * NE + (e + 1))
                        for c in range(FC):
                            m = e * FC + c
                            act.wait_ge(hidden, g * NJ + (m + 1))
                            nc.scalar.activation(gel[m % GB_][:], ps_h[m % HB][:], ACT.Gelu_apprx_tanh,
                                                 bias=b1[:, e, c:c + 1]).then_inc(gelued, 1)
                        if e == 0:
                            act.wait_ge(we_turned, done(g))
                            nc.scalar.copy(weT[j][:], ps_w).then_inc(weT_ready, 1)

        @block.vector
        def _(dve):
            count = [0]

            def link(ins):
                count[0] += 1
                ins.then_inc(route, 1)
                dve.wait_ge(route, count[0])

            lg = w["logits"]
            wide = [P, NT, NE]
            link(nc.vector.tensor_reduce(m1[:], lg[:], AX.X, ALU.max))
            link(nc.vector.tensor_tensor(ps[:], lg[:], m1[:].unsqueeze(2).to_broadcast(wide), ALU.subtract))
            dve.wait_ge(exped, 1)
            dve.wait_ge(ranked, NE)

            def pick(src, m, r, onehot):
                link(nc.vector.tensor_reduce(m[:], src[:], AX.X, ALU.max))
                link(nc.vector.tensor_tensor(cand[:], src[:], m[:].unsqueeze(2).to_broadcast(wide), ALU.is_equal))
                link(nc.vector.tensor_tensor(cand[:], cand[:], rank[:].unsqueeze(1).to_broadcast(wide), ALU.mult))
                link(nc.vector.tensor_reduce(r[:], cand[:], AX.X, ALU.max))
                link(nc.vector.tensor_tensor(onehot[:], cand[:], r[:].unsqueeze(2).to_broadcast(wide), ALU.is_equal))
            pick(ps, m1, r1, first)
            link(nc.vector.scalar_tensor_tensor(out=share[:], in0=first[:], scalar=-4.0, in1=ps[:], op0=ALU.mult, op1=ALU.add))
            pick(share, m2, r2, second)
            link(nc.vector.tensor_tensor(m1[:], m1[:], m2[:], ALU.add))
            link(nc.vector.reciprocal(m1[:], m1[:]))
            link(nc.vector.tensor_tensor(first[:], first[:], second[:], ALU.add))
            link(nc.vector.tensor_tensor(first[:], first[:], ps[:], ALU.mult))
            link(nc.vector.tensor_tensor(share[:], first[:], m1[:].unsqueeze(2).to_broadcast(wide), ALU.mult))
            dve.sem_inc(combined, 2)
            with dve.Fori(0, G // 2) as it:
                for j in range(2):
                    g = it * 2 + j
                    dve.wait_ge(we_turned, free2(g))
                    nc.vector.tensor_copy(we[j][:], group_tiles(share, g)).then_inc(we_copied, 1)
                    dve.wait_ge(we_copied, g + 1)
                    dve.wait_ge(biased, g + 1)
                    nc.vector.tensor_tensor(acc[j][:], group_tiles(w["x1"], g), ps_b[:], ALU.add).then_inc(share_ready, 1)
                    for e in range(NE):
                        dve.wait_ge(used, g * NE + (e + 3))
                        if e == 0:
                            dve.wait_ge(share_ready, g + 1)
                        else:
                            dve.wait_ge(combined, g * NE + (e + 2))
                        for n in range(TILES):
                            last = nc.vector.scalar_tensor_tensor(out=acc[j][:, n, :], in0=ps_y[e % 2][:, n, :],
                                                                  scalar=we[j][:, n, e:e + 1], in1=acc[j][:, n, :],
                                                                  op0=ALU.mult, op1=ALU.add)
                        last.then_inc(combined, 1)
                    dve.wait_ge(combined, g * NE + (NE + 2))
                    ln.moments(dve, acc[j], j, g)
                    dve.wait_ge(stored[j], it * 16 + 16)
                    ln.normalise(dve, acc[j], fin[j], j, g).then_inc(o_ready, 1)


_OUT_SHAPE = (64, 64, 128)


def kernel(**inputs):
    import numpy as _np
    import concourse.bacc as _bacc
    from concourse import mybir as _mybir
    from concourse.bass_utils import run_bass_kernel_spmd as _run

    nc = _bacc.Bacc("TRN2", target_bir_lowering=False, num_devices=1)
    arrays, args = {}, {}
    for name in inputs:
        v = _np.ascontiguousarray(inputs[name])
        arrays[f"in_{name}_dram"] = v
        args[name] = nc.dram_tensor(f"in_{name}_dram", v.shape, _mybir.dt.from_np(v.dtype), kind="ExternalInput").ap()
    out = nc.dram_tensor("out_0_dram", _OUT_SHAPE, F32, kind="ExternalOutput").ap()
    decoder_layer(nc, args, out)
    r = _run(nc, [arrays], core_ids=[0])
    return r.results[0]["out_0_dram"]
```

```python
from contextlib import ExitStack

import concourse.bass as bass
from concourse import mybir

F32 = mybir.dt.float32
F32R = mybir.dt.float32r
I32 = mybir.dt.int32
ALU = mybir.AluOpType
ACT = mybir.ActivationFunctionType
AX = mybir.AxisListType

P = 128
B, S, D = 64, 64, 128
NTOK = B * S
H, HD = 16, 8
TAPS = 4
GT = 512
G = NTOK // GT
GB = GT // S
TILES = GT // P
PAD = S + TAPS - 1
CH = GT // B
NCH = S // CH
HC = CH // 2
XE, XH = 8, 256
XC = XH // P
XK = 64
NE, FH = 8, 512
FC = FH // P
NORM_EPS = 1e-6
LN_EPS = 1e-5
CREDIT = 2

GATE_TURNS = NCH // 2

K_, Q_, V_, O_ = 0, 1, 2, 3
COLS = ["L0_attn_bk", "L0_attn_bq", "L0_attn_bv", "L0_attn_bk_conv", "L0_attn_bq_conv", "L0_attn_bv_conv",
        "L0_ffn_ln1_w", "L0_ffn_ln1_b", "L0_ffn_ln2_w", "L0_ffn_ln2_b"]
C_LN1W, C_LN1B, C_LN2W, C_LN2B = 6, 7, 8, 9
C_BETA, C_NORMW, C_FOLD, C_QKV, C_EPS, C_ONE = 10, 11, 12, 15, 18, 19
NCOL = 24


def done(g):
    return g + (1 + CREDIT)


def free2(g):
    return g + 1


def free1(g):
    return g + 2


def dram_ap(t, offset, dims):
    return bass.AP(tensor=t.tensor, offset=offset, ap=[list(d) for d in dims])


def decoder_layer(nc, a, out):
    with ExitStack() as whole:
        def keep(name, shape, dt=F32):
            return whole.enter_context(nc.sbuf_tensor(name, shape, dt))

        def sem(name):
            return whole.enter_context(nc.semaphore(name))

        w = {
            "ident": keep("ident", [P, P]),
            "headsel": keep("headsel", [P, H]),
            "halfpow": keep("halfpow", [P, TILES * H]),
            "wT": keep("wT", [P, 4, P]),
            "wbT": keep("wbT", [P, H, HD]),
            "pinT": keep("pinT", [P, XE * XC, P]),
            "poutT": keep("poutT", [P, XE * XC, P]),
            "cols": keep("cols", [P, NCOL]),
            "taps": keep("taps", [P, 3, TAPS]),
            "bo_row": keep("bo_row", [P, D]),
        }
        scr = {n: nc.dram_tensor(n, shape, F32, kind="Internal").ap()
               for n, shape in (("k_scr", [P, NTOK]), ("q_scr", [P, NTOK]), ("gate_scr", [XE, NTOK]))}
        w["idle_dve"], w["idle_pool"] = keep("idle_dve", [P, 1]), keep("idle_pool", [P, 4])
        w["ln_sems"] = [sem(f"ln_{what}") for what in ("stats_done", "mean_done", "var_done", "rstd_done")]
        w["ln_stages"] = 0
        weights_stage(nc, a, w, sem)

        w["gates_stored"], w["all_gates"] = sem("gates_stored"), 2 * 16 * GATE_TURNS
        w["bT"] = keep("bT", [P, S, B])
        with ExitStack() as early:
            for name, shape in (("vT", [P, S, B]),
                                ("kT", [P, S, B]), ("qT", [P, S, B])):
                w[name] = early.enter_context(nc.sbuf_tensor(name, shape, F32))
            project_stage(nc, a, w, sem)
            for name in ("krep", "qrep"):
                w[name] = [early.enter_context(nc.sbuf_tensor(f"{name}{i}", [P, HD, CH, B], F32)) for i in range(2)]
            w["stored"] = [sem(f"kq_stored{c}") for c in range(NCH)]
            w["kq_in"] = [sem("kq_in0"), sem("kq_in1")]
            w["pick_w"] = early.enter_context(nc.sbuf_tensor("pick_w", [P, B // 2, S], F32))
            w["pick_e"] = early.enter_context(nc.sbuf_tensor("pick_e", [P, B // 2, S], I32))
            w["picks_in"] = sem("picks_in")
            scale_stage(nc, a, w, scr, sem)
            delta_stage(nc, a, w, scr, sem)
        w["x1"] = keep("x1", [P, G * TILES, D])
        w["x1T"] = keep("x1T", [P, NTOK])
        mix_in_stage(nc, a, w, sem)
        w["x2"] = keep("x2", [P, G * TILES, D])
        w["stats"] = keep("stats", [P, G * TILES, 6])
        xattn_stage(nc, w, scr, sem)
        w["h2T"] = w["x1T"]
        w["logits"] = keep("logits", [P, G * TILES, NE])
        w["w1"] = [w["pinT"], w["poutT"]]
        w["w2"] = w["bT"][:].rearrange("p t b -> p (t b)")
        w["experts_in"] = sem("experts_in")
        attend_stage(nc, a, w, sem)
        moe_stage(nc, a, w, out, sem)


def weights_stage(nc, a, w, sem):
    raw_in, col_in, made, set_up, turned, moved_even, moved_odd, folded = (
        sem(n) for n in ("raw_in", "col_in", "made", "set_up", "turned", "moved_even", "moved_odd", "folded"))
    with ExitStack() as ctx:
        raw = ctx.enter_context(nc.sbuf_tensor("raw", [P, 4, D], F32))
        raw_b = ctx.enter_context(nc.sbuf_tensor("raw_b", [H, D], F32))
        raw_pin = ctx.enter_context(nc.sbuf_tensor("raw_pin", [P, XE * XC, D], F32))
        raw_pout = ctx.enter_context(nc.sbuf_tensor("raw_pout", [P, XE, XH], F32))
        NT = 4 + XE * XC * 2
        bank = [ctx.enter_context(nc.psum_tensor(f"turn{i}", [P, 4, P], F32)) for i in range(2)]
        bank_b = ctx.enter_context(nc.psum_tensor("turn_b", [P, H], F32))
        cols, taps = w["cols"], w["taps"]
        n_small = len(COLS) + 3 + 3 + 3
        block = ctx.enter_context(nc.Block())

        @block.sync
        def _(sp):
            for i, n in enumerate(("L0_attn_Wk", "L0_attn_Wq", "L0_attn_Wv", "L0_attn_Wo")):
                sp.dma_start(raw[:, i, :], a[n]).then_inc(raw_in, 16)
            sp.dma_start(raw_b[:], a["L0_attn_Wbeta"]).then_inc(raw_in, 16)
            sp.dma_start(raw_pin[:], a["L0_xattn_proj_in"].rearrange("e (c p) i -> p (e c) i", p=P)).then_inc(raw_in, 16)
            sp.dma_start(raw_pout[:], a["L0_xattn_proj_out"].rearrange("e i d -> i e d")).then_inc(raw_in, 16)
            sp.wait_ge(raw_in, 7 * 16)

        @block.scalar
        def _(act):
            for i, n in enumerate(COLS):
                act.dma_start(cols[:, i:i + 1], dram_ap(a[n], 0, [[1, P], [1, 1]])).then_inc(col_in, 16)
            for i, n in enumerate(("L0_attn_wk_conv", "L0_attn_wq_conv", "L0_attn_wv_conv")):
                act.dma_start(taps[:, i, :], a[n]).then_inc(col_in, 16)
            act.dma_start(cols[:, C_BETA:C_BETA + 1],
                          dram_ap(a["L0_attn_bbeta"], 0, [[1, H], [0, HD], [1, 1]])).then_inc(col_in, 16)
            act.dma_start(cols[:, C_NORMW:C_NORMW + 1],
                          dram_ap(a["L0_attn_norm_w"], 0, [[0, H], [1, HD], [1, 1]])).then_inc(col_in, 16)
            act.dma_start(w["bo_row"][:], dram_ap(a["L0_attn_bo"], 0, [[0, P], [1, D]])).then_inc(col_in, 16)
            for i in range(3):
                act.dma_start(cols[:, C_QKV + i:C_QKV + i + 1],
                              dram_ap(a["L0_ffn_b_qkv"], i * D, [[1, P], [1, 1]])).then_inc(col_in, 16)
            act.wait_ge(turned, 1)
            nc.scalar.copy(w["wT"][:], bank[0][:]).then_inc(moved_even, 1)
            for b in range(2, NT // 4, 2):
                act.wait_ge(turned, b + 1)
                t = 4 * (b - 1)
                dst = w["pinT"] if t < XE * XC else w["poutT"]
                nc.scalar.copy(dst[:, t % (XE * XC):t % (XE * XC) + 4, :], bank[0][:]).then_inc(moved_even, 1)

        @block.gpsimd
        def _(pool):
            ident, headsel = w["ident"], w["headsel"]
            nc.gpsimd.memset(ident[:], 0.0).then_inc(made, 1)
            nc.gpsimd.memset(headsel[:], 1.0).then_inc(made, 1)
            nc.gpsimd.memset(w["halfpow"][:], -0.5).then_inc(set_up, 1)
            pool.wait_ge(made, 2)
            nc.gpsimd.affine_select(out=ident[:], in_=ident[:], compare_op=ALU.not_equal, fill=1.0, base=0,
                                    pattern=[[-1, P]], channel_multiplier=1).then_inc(set_up, 1)
            nc.gpsimd.affine_select(out=headsel[:], in_=headsel[:], compare_op=ALU.is_ge, fill=0.0, base=0,
                                    pattern=[[-HD, H]], channel_multiplier=1).then_inc(made, 1)
            pool.wait_ge(made, 3)
            nc.gpsimd.affine_select(out=headsel[:], in_=headsel[:], compare_op=ALU.is_ge, fill=0.0, base=HD - 1,
                                    pattern=[[HD, H]], channel_multiplier=-1).then_inc(set_up, 1)

        @block.tensor
        def _(pe):
            pe.wait_ge(set_up, 3)
            pe.wait_ge(raw_in, 7 * 16)
            for b in range(NT // 4):
                if b >= 2:
                    pe.wait_ge(moved_odd if b % 2 else moved_even, b // 2)
                for i in range(4):
                    t = 4 * b + i - 4
                    if b == 0:
                        src = raw[:, i, :]
                    elif t < XE * XC:
                        src = raw_pin[:, t, :]
                    else:
                        t -= XE * XC
                        src = raw_pout[:, t // XC, (t % XC) * P:(t % XC + 1) * P]
                    last = nc.tensor.transpose(bank[b % 2][:, i, :], src, w["ident"][:])
                last.then_inc(turned, 1)
            nc.tensor.transpose(bank_b[:], raw_b[:], w["ident"][0:H, 0:H]).then_inc(turned, 1)

        @block.vector
        def _(dve):
            for b in range(1, NT // 4, 2):
                dve.wait_ge(turned, b + 1)
                t = 4 * (b - 1)
                dst = w["pinT"] if t < XE * XC else w["poutT"]
                nc.vector.tensor_copy(dst[:, t % (XE * XC):t % (XE * XC) + 4, :], bank[1][:]).then_inc(moved_odd, 1)
            dve.wait_ge(turned, NT // 4 + 1)
            nc.vector.tensor_copy(w["wbT"][:], bank_b[:].unsqueeze(2).to_broadcast([P, H, HD])).then_inc(set_up, 1)
            dve.wait_ge(col_in, 16 * (len(COLS) + 9))
            for i in range(3):
                nc.vector.scalar_tensor_tensor(out=cols[:, C_FOLD + i:C_FOLD + i + 1], in0=cols[:, i:i + 1],
                                               scalar=taps[:, i, TAPS - 1:TAPS], in1=cols[:, 3 + i:4 + i],
                                               op0=ALU.mult, op1=ALU.add).then_inc(folded, 1)
            nc.vector.memset(cols[:, C_EPS:C_EPS + 1], NORM_EPS).then_inc(folded, 1)
            nc.vector.memset(cols[:, C_ONE:C_ONE + 1], 1.0).then_inc(folded, 1)
            dve.wait_ge(folded, 5)


def all_groups(eng, group):
    group(0, 0)
    with eng.Fori(0, (G - 2) // 2) as it:
        group(it * 2 + 1, 1)
        group(it * 2 + 2, 0)
    group(G - 1, 1)


def first(g):
    return isinstance(g, int) and g == 0


def final(g):
    return isinstance(g, int) and g == G - 1


def last_two(g):
    return isinstance(g, int) and g >= G - 2


def project_stage(nc, a, w, sem):
    x_in = [sem("x_in0"), sem("x_in1")]
    (x_turned, xT_ready, proj_done, padded, first_tap, beta_ready, taps_done, sig_ready, v_ready, zeroed) = (
        sem("pr_" + n) for n in (
            "x_turned", "xT_ready", "proj_done", "padded", "first_tap", "beta_ready", "taps_done", "sig_ready",
            "v_ready", "zeroed"))
    cols, taps = w["cols"], w["taps"]
    x = a["x"].rearrange("b s d -> (b s) d")
    with ExitStack() as ctx:
        def mem(name, shape):
            return [ctx.enter_context(nc.sbuf_tensor(f"{name}{i}", shape, F32)) for i in range(2)]

        xs = mem("xs", [P, TILES, D])
        xT = mem("xT", [P, GT])
        pad = mem("pad", [P, 3, GB, PAD])
        conv = mem("conv", [P, 3, GB, S])
        sig = mem("sig", [P, GB, S])
        ps_t = [ctx.enter_context(nc.psum_tensor(f"ps_t{i}", [P, GT], F32)) for i in range(2)]
        ps_p = [ctx.enter_context(nc.psum_tensor(f"ps_p{i}", [P, GB, S], F32)) for i in range(4)]

        def cols_of(t, g):
            return t[:, :, bass.ds(g * GB, GB)].rearrange("p t b -> p b t")

        block = ctx.enter_context(nc.Block())

        @block.sync
        def _(sp):
            def load(g, j):
                sp.dma_start(xs[j][:], x[bass.ds(g * GT, GT), :].rearrange("(n p) d -> p n d", p=P)
                             ).then_inc(x_in[j], 16)
            load(0, 0)
            load(1, 1)
            with sp.Fori(0, G // 2 - 1) as it:
                for j in range(2):
                    g = it * 2 + j
                    sp.wait_ge(x_turned, g + 1)
                    load(g + 2, j)

        @block.tensor
        def _(pe):
            def turn(x, j):
                pe.wait_ge(x_in[j], (x - j) * 8 + 16)
                if not isinstance(x, int) or x >= 2:
                    pe.wait_ge(xT_ready, x - 1)
                for i in range(TILES):
                    last = nc.tensor.transpose(ps_t[j][:, i * P:(i + 1) * P], xs[j][:, i, :], w["ident"][:])
                last.then_inc(x_turned, 1)

            def group(g, j):
                pe.wait_ge(xT_ready, g + 1)
                for i in range(4):
                    if i < 3:
                        pe.wait_ge(first_tap, g * 3 + (i + 1))
                    elif not first(g):
                        pe.wait_ge(beta_ready, g)
                    lhsT = w["wT"][:, i, :] if i < 3 else w["wbT"][:].rearrange("p h d -> p (h d)")
                    nc.tensor.matmul(ps_p[i][:].rearrange("p b s -> p (b s)"), lhsT, xT[j][:],
                                     start=True, stop=True).then_inc(proj_done, 1)
                if not final(g):
                    turn(g + 1, 1 - j)
            turn(0, 0)
            all_groups(pe, group)

        @block.scalar
        def _(act):
            def silu_gate(x, j):
                act.wait_ge(taps_done, x * 9 + 9)
                nc.scalar.activation(sig[j][:], conv[j][:, V_, :, :], ACT.Sigmoid).then_inc(sig_ready, 1)

            def copy_x(x, j):
                act.wait_ge(x_turned, x + 1)
                nc.scalar.activation(xT[j][:], ps_t[j][:], ACT.Identity).then_inc(xT_ready, 1)

            def group(g, j):
                for i in range(3):
                    act.wait_ge(proj_done, g * 4 + (i + 1))
                    if i == 0 and (not isinstance(g, int) or g >= 2):
                        act.wait_ge(v_ready, g - 1)
                    nc.scalar.activation(pad[j][:, i, :, TAPS - 1:PAD], ps_p[i][:], ACT.Identity,
                                         bias=cols[:, i:i + 1]).then_inc(padded, 1)
                    nc.scalar.activation(conv[j][:, i, :, :], ps_p[i][:], ACT.Identity,
                                         bias=cols[:, C_FOLD + i:C_FOLD + i + 1],
                                         scale=taps[:, i, TAPS - 1:TAPS]).then_inc(first_tap, 1)
                if not final(g):
                    copy_x(g + 1, 1 - j)
                act.wait_ge(proj_done, g * 4 + 4)
                nc.scalar.activation(cols_of(w["bT"], g), ps_p[3][:], ACT.Sigmoid,
                                     bias=cols[:, C_BETA:C_BETA + 1]).then_inc(beta_ready, 1)
                if not first(g):
                    silu_gate(g - 1, 1 - j)
            act.sem_inc(first_tap, 3)
            act.wait_ge(zeroed, 2)
            copy_x(0, 0)
            all_groups(act, group)
            silu_gate(G - 1, 1)

        @block.vector
        def _(dve):
            def silu(x, j):
                dve.wait_ge(sig_ready, x + 1)
                nc.vector.tensor_tensor(cols_of(w["vT"], x), conv[j][:, V_, :, :], sig[j][:], ALU.mult
                                        ).then_inc(v_ready, 1)

            def group(g, j):
                for t in range(TAPS - 1):
                    for i in range(3):
                        o = 3 * t + i
                        if t == 0:
                            dve.wait_ge(padded, g * 3 + (i + 1))
                            dve.wait_ge(first_tap, g * 3 + (i + 4))
                        else:
                            dve.wait_ge(taps_done, g * 9 + (o - 2))
                        dst = conv[j][:, i, :, :]
                        if t == TAPS - 2 and i < V_:
                            dst = cols_of(w["kT"] if i == K_ else w["qT"], g)
                        nc.vector.scalar_tensor_tensor(out=dst, in0=pad[j][:, i, :, t:t + S],
                                                       scalar=taps[:, i, t:t + 1], in1=conv[j][:, i, :, :],
                                                       op0=ALU.mult, op1=ALU.add).then_inc(taps_done, 1)
                    if t == 1 and not first(g):
                        silu(g - 1, 1 - j)
            nc.vector.memset(pad[0][:, :, :, 0:TAPS - 1], 0.0).then_inc(zeroed, 1)
            nc.vector.memset(pad[1][:, :, :, 0:TAPS - 1], 0.0).then_inc(zeroed, 1)
            all_groups(dve, group)
            silu(G - 1, 1)


def scale_stage(nc, a, w, scr, sem):
    (squared, summed, rooted, beta_rooted, guarded, inverted, spread, turned, rb_ready, k_scaled, v_scaled, q_scaled) = (
        sem("sc_" + n) for n in (
            "squared", "summed", "rooted", "beta_rooted", "guarded", "inverted", "spread", "turned", "rb_ready",
            "k_scaled", "v_scaled", "q_scaled"))
    CW = CH * B
    NN = 2 * TILES * H
    with ExitStack() as ctx:
        def mem(name, shape):
            return [ctx.enter_context(nc.sbuf_tensor(f"sc_{name}{i}", shape, F32)) for i in range(2)]

        sq = mem("sq", [P, 2, CW])
        norm = mem("norm", [P, NN])
        rexp = mem("rexp", [P, NN, HD])
        rb = mem("rb", [P, CW])
        ps_n = [ctx.enter_context(nc.psum_tensor(f"sc_ps_n{i}", [P, 512], F32)) for i in range(2)]
        ps_r = [ctx.enter_context(nc.psum_tensor(f"sc_ps_r{i}", [P, 2, CW], F32)) for i in range(2)]
        kT, qT, vT, bT = (w[n][:].rearrange("p t b -> p (t b)") for n in ("kT", "qT", "vT", "bT"))

        def chunk(t, c):
            return t[:, bass.ds(c * CW, CW)]

        block = ctx.enter_context(nc.Block())

        @block.sync
        def _(sp):
            for c in range(NCH):
                sp.wait_ge(k_scaled, c + 1)
                sp.dma_start(scr["k_scr"][:, c * CW:(c + 1) * CW], chunk(kT, c)).then_inc(w["stored"][c], 16)
                sp.wait_ge(q_scaled, c + 1)
                sp.dma_start(scr["q_scr"][:, c * CW:(c + 1) * CW], chunk(qT, c)).then_inc(w["stored"][c], 16)
                if c in (1, 2):
                    sp.wait_ge(w["stored"][c - 1], 32)
                    load_replicated(sp, w, scr, (c - 1) * CW, c - 1)

        @block.scalar
        def _(act):
            for t, name in ((w["pick_w"], "ctx_512"), (w["pick_e"], "itok_BxS2xS_0_7")):
                for b2 in range(2):
                    src = dram_ap(a[name], b2 * XK * S, [[S, XK], [2 * XK * S, B // 2], [1, S]])
                    act.dma_start(t[b2 * XK:(b2 + 1) * XK, :, :], src).then_inc(w["picks_in"], 16)

            def squares(x, j):
                if not isinstance(x, int) or x >= 2:
                    act.wait_ge(summed, x - 1)
                nc.scalar.activation(sq[j][:, 0, :], chunk(kT, x), ACT.Square)
                nc.scalar.activation(sq[j][:, 1, :], chunk(qT, x), ACT.Square).then_inc(squared, 1)
                nc.scalar.activation(chunk(bT, x), chunk(bT, x), ACT.Sqrt).then_inc(beta_rooted, 1)

            def group(c, j):
                act.wait_ge(summed, c + 1)
                nc.scalar.activation(norm[j][:], ps_n[j][:, 0:NN], ACT.Sqrt).then_inc(rooted, 1)
                if not final(c):
                    squares(c + 1, 1 - j)
                act.wait_ge(inverted, c + 1)
                if not isinstance(c, int) or c >= 2:
                    act.wait_ge(turned, c - 1)
                nc.scalar.activation(rexp[j][:], norm[j][:].unsqueeze(2).to_broadcast([P, NN, HD]), ACT.Identity
                                     ).then_inc(spread, 1)
            squares(0, 0)
            all_groups(act, group)

        @block.tensor
        def _(pe):
            def add_squares(x, j):
                pe.wait_ge(squared, x + 1)
                if not isinstance(x, int) or x >= 2:
                    pe.wait_ge(rooted, x - 1)
                for i in range(2):
                    for n in range(TILES):
                        o = (i * TILES + n) * H
                        last = nc.tensor.matmul(ps_n[j][:, o:o + H], sq[j][:, i, n * P:(n + 1) * P], w["headsel"][:],
                                                start=True, stop=True)
                last.then_inc(summed, 1)

            def group(c, j):
                if not final(c):
                    add_squares(c + 1, 1 - j)
                pe.wait_ge(spread, c + 1)
                if not isinstance(c, int) or c >= 2:
                    pe.wait_ge(rb_ready, c - 1)
                    pe.wait_ge(q_scaled, c - 1)
                for i in range(2):
                    for n in range(TILES):
                        o = (i * TILES + n) * H
                        last = nc.tensor.transpose(ps_r[j][:, i, n * P:(n + 1) * P],
                                                   rexp[j][:, o:o + H, :].rearrange("p h d -> p (h d)"), w["ident"][:])
                last.then_inc(turned, 1)
            add_squares(0, 0)
            all_groups(pe, group)

        @block.gpsimd
        def _(pool):
            def group(c, j):
                pool.wait_ge(rb_ready, c + 1)
                if not isinstance(c, int):
                    carry_pool(nc, w, j)
                nc.gpsimd.tensor_tensor(chunk(vT, c), chunk(vT, c), rb[j][:], ALU.mult).then_inc(v_scaled, 1)
            pool.sem_inc(v_scaled, CREDIT)
            all_groups(pool, group)

        @block.vector
        def _(dve):
            def invert(x, j):
                dve.wait_ge(rooted, x + 1)
                nc.vector.tensor_scalar(norm[j][:], norm[j][:], NORM_EPS, None, ALU.add).then_inc(guarded, 1)
                dve.wait_ge(guarded, x + 1)
                nc.vector.reciprocal(norm[j][:], norm[j][:]).then_inc(inverted, 1)

            def scale(c, j):
                dve.wait_ge(beta_rooted, c + 1)
                dve.wait_ge(turned, c + 1)
                dve.wait_ge(v_scaled, free2(c))
                nc.vector.tensor_tensor(rb[j][:], ps_r[j][:, 0, :], chunk(bT, c), ALU.mult).then_inc(rb_ready, 1)
                dve.wait_ge(rb_ready, c + 1)
                nc.vector.tensor_tensor(chunk(kT, c), chunk(kT, c), rb[j][:], ALU.mult).then_inc(k_scaled, 1)
                nc.vector.tensor_tensor(chunk(qT, c), chunk(qT, c), ps_r[j][:, 1, :], ALU.mult).then_inc(q_scaled, 1)

            def group(c, j):
                invert(c, j)
                if not first(c):
                    scale(c - 1, 1 - j)
            all_groups(dve, group)
            scale(NCH - 1, 1)


def load_replicated(sp, w, scr, column, cb):
    for t, name in ((w["krep"], "k_scr"), (w["qrep"], "q_scr")):
        for i in range(HD):
            src = dram_ap(scr[name], column + i * NTOK, [[HD * NTOK, H], [0, HD], [1, CH * B]])
            sp.dma_start(t[cb][:, i, :, :].rearrange("p t b -> p (t b)"), src).then_inc(w["kq_in"][cb], 16)


def delta_stage(nc, a, w, scr, sem):
    kq_in, krep, qrep = w["kq_in"], w["krep"], w["qrep"]
    gates_stored = w["gates_stored"]
    (state_op, qs_made, o_summed, o_copied, dist_ready, hit, weighed, gated, gates_copied,
     const, empty) = (sem("de_" + n) for n in (
         "state_op", "qs_made", "o_summed", "o_copied", "dist_ready", "hit", "weighed", "gated", "gates_copied",
         "const", "empty"))
    OPS = 10
    NIT = GATE_TURNS
    TURN = 2 * CH
    PAIRS = B // 2
    PT = PAIRS // NIT
    GC = PAIRS // NIT * S
    with ExitStack() as ctx:
        def mem(name, shape, n=2, dt=F32):
            return [ctx.enter_context(nc.sbuf_tensor(f"{name}{i}", shape, dt)) for i in range(n)]

        qs = mem("qs", [P, HD, HC, B])
        state = mem("state", [P, HD, B])
        prod, = mem("prod", [P, HD, B], 1)
        rise, = mem("rise", [P, HD, B], 1)
        pred, upd = mem("small", [P, B], 2)
        pick_w, pick_e, picks_in = w["pick_w"], w["pick_e"], w["picks_in"]
        dist = mem("dist", [P, GC])
        wsel = mem("wsel", [P, GC])
        negs, = mem("negs", [P, XE], 1)
        esel, = mem("esel", [P, XE, 2, XE], 1)
        gates, = mem("gates", [2 * XE, GC], 1)
        ps_o = [ctx.enter_context(nc.psum_tensor(f"ps_o{i}", [P, 512], F32)) for i in range(2)]
        ps_g = ctx.enter_context(nc.psum_tensor("ps_g", [2 * XE, GC], F32))
        oT = w["bT"]
        block = ctx.enter_context(nc.Block())

        @block.sync
        def _(sp):
            for c in range(CREDIT, NCH):
                sp.wait_ge(w["stored"][c], 32)
            with sp.Fori(1, NIT) as it:
                for cb in range(2):
                    column = sp.snap((it * 2 + cb) * (CH * B))
                    sp.wait_ge(qs_made, it * TURN + ((cb - 1) * CH + CREDIT * HC))
                    load_replicated(sp, w, scr, column, cb)

        @block.scalar
        def _(act):
            act.sem_inc(o_copied, CREDIT)
            act.wait_ge(const, 3 * XE + 1)
            act.wait_ge(picks_in, 64)

            def store_gates(turn):
                act.wait_ge(gated, turn * XE + (XE + CREDIT))
                if turn:
                    act.wait_ge(gates_stored, turn * 32)
                nc.scalar.activation(gates[:], ps_g[:], ACT.Identity).then_inc(gates_copied, 1)
                act.wait_ge(gates_copied, turn + 1)
                for b2 in range(2):
                    dst = dram_ap(scr["gate_scr"], turn * (2 * GC) + b2 * S, [[NTOK, XE], [2 * S, PT], [1, S]])
                    act.dma_start(dst, gates[b2 * XE:(b2 + 1) * XE, :].rearrange("e (n s) -> e n s", s=S)
                                  ).then_inc(gates_stored, 16)

            def copy_outputs(hc):
                act.wait_ge(o_summed, done(hc))
                nc.scalar.activation(oT[:, hc * HC:(hc + 1) * HC, :].rearrange("p t b -> p (t b)"),
                                     ps_o[hc % 2][:, 0:HC * B], ACT.Identity).then_inc(o_copied, 1)

            for n in range(NIT * XE):
                turn, e = n // XE, n % XE
                part = pick_e[:, turn * PT:(turn + 1) * PT, :].rearrange("p n s -> p (n s)")
                nc.scalar.activation(dist[e % 2][:], part, ACT.Abs, bias=negs[:, e:e + 1]).then_inc(dist_ready, 1)
                act.wait_ge(dist_ready, n + 1)
                act.wait_ge(gated, free2(n))
                nc.scalar.activation(wsel[e % 2][:], dist[e % 2][:], ACT.Relu, bias=w["cols"][:, C_ONE:C_ONE + 1],
                                     scale=-1.0).then_inc(hit, 1)
                if e == 1 and turn:
                    store_gates(turn - 1)
                if e % 2 and n > 1:
                    copy_outputs(n // 2 - 1)
            copy_outputs(S // HC - 1)
            store_gates(NIT - 1)

        @block.gpsimd
        def _(pool):
            for e in range(XE):
                nc.gpsimd.memset(negs[:, e:e + 1], float(-e)).then_inc(const, 1)
            nc.gpsimd.memset(esel[:], 0.0).then_inc(const, 1)
            pool.wait_ge(const, XE + 1)
            for e in range(XE):
                for b2 in range(2):
                    nc.gpsimd.memset(esel[b2 * XK:(b2 + 1) * XK, e, b2, e:e + 1], 1.0).then_inc(const, 1)
            pool.wait_ge(const, 3 * XE + 1)
            pool.sem_inc(qs_made, CREDIT * HC)
            for t in range(S):
                hc, c = t // HC, t // CH
                if t % HC == 0:
                    pool.wait_ge(o_summed, free2(hc))
                if t % CH == 0:
                    pool.wait_ge(kq_in[c % 2], c // 2 * 256 + 256)
                pool.wait_ge(state_op, (t + 1) * OPS)
                nc.gpsimd.tensor_tensor(qs[hc % 2][:, :, t % HC, :], state[(t + 1) % 2][:],
                                        qrep[c % 2][:, :, t % CH, :], ALU.mult).then_inc(qs_made, 1)
                if t % 2:
                    e, turn = t // 2 % XE, t // TURN
                    part = pick_w[:, turn * PT:(turn + 1) * PT, :].rearrange("p n s -> p (n s)")
                    if t == 1:
                        pool.wait_ge(picks_in, 64)
                    pool.wait_ge(hit, t // 2 + 1)
                    nc.gpsimd.tensor_tensor(wsel[e % 2][:], wsel[e % 2][:], part, ALU.mult).then_inc(weighed, 1)

        @block.vector
        def _(dve):
            nc.vector.memset(state[0][:], 0.0).then_inc(empty, 1)
            dve.wait_ge(empty, 1)
            for t in range(S):
                c = t // CH
                k = krep[c % 2][:, :, t % CH, :]
                old, new = state[t % 2], state[(t + 1) % 2]
                if t % CH == 0:
                    dve.wait_ge(kq_in[c % 2], c // 2 * 256 + 256)
                halves = (slice(0, B // 2), slice(B // 2, B))
                for i, b in enumerate(halves):
                    if t:
                        dve.wait_ge(state_op, t * OPS - 1 + i)
                    nc.vector.tensor_tensor(prod[:, :, b], old[:, :, b], k[:, :, b], ALU.mult).then_inc(state_op, 1)
                for i, b in enumerate(halves):
                    dve.wait_ge(state_op, t * OPS + 1 + i)
                    nc.vector.tensor_reduce(pred[:, b], prod[:, :, b].rearrange("p i b -> p b i"), AX.X, ALU.add
                                            ).then_inc(state_op, 1)
                for i, b in enumerate(halves):
                    dve.wait_ge(state_op, t * OPS + 3 + i)
                    nc.vector.tensor_tensor(upd[:, b], w["vT"][:, t, b], pred[:, b], ALU.subtract).then_inc(state_op, 1)
                for i, b in enumerate(halves):
                    dve.wait_ge(state_op, t * OPS + 5 + i)
                    nc.vector.tensor_tensor(rise[:, :, b], k[:, :, b], upd[:, b].unsqueeze(1).to_broadcast([P, HD, B // 2]),
                                            ALU.mult).then_inc(state_op, 1)
                if t >= 2:
                    dve.wait_ge(qs_made, t - 1 + CREDIT * HC)
                for i, b in enumerate(halves):
                    dve.wait_ge(state_op, t * OPS + 7 + i)
                    nc.vector.tensor_tensor(new[:, :, b], old[:, :, b], rise[:, :, b], ALU.add).then_inc(state_op, 1)

        @block.tensor
        def _(pe):
            pe.sem_inc(o_summed, CREDIT)
            pe.sem_inc(gated, CREDIT)
            pe.wait_ge(const, 3 * XE + 1)
            with pe.Fori(0, NIT) as it:
                for hc in range(4):
                    n = it * 4 + hc
                    pe.wait_ge(qs_made, n * HC + (HC + CREDIT * HC))
                    pe.wait_ge(o_copied, free2(n))
                    for i in range(HD):
                        last = nc.tensor.matmul(ps_o[hc % 2][:, 0:HC * B], w["ident"][:],
                                                qs[hc % 2][:, i, :, :].rearrange("p t b -> p (t b)"),
                                                start=(i == 0), stop=(i == HD - 1))
                    last.then_inc(o_summed, 1)
                    for e in range(2 * hc, 2 * hc + 2):
                        pe.wait_ge(weighed, it * XE + (e + 1))
                        if e == 0:
                            pe.wait_ge(gates_copied, it)
                        nc.tensor.matmul(ps_g[:], esel[:, e, :, :].rearrange("p b e -> p (b e)"), wsel[e % 2][:],
                                         start=(e == 0), stop=(e == XE - 1)).then_inc(gated, 1)


def carry_dve(nc, w):
    nc.vector.memset(w["idle_dve"][:], 0.0)


def carry_pool(nc, w, place=0):
    nc.gpsimd.tensor_tensor(w["idle_pool"][:, place:place + 1], w["halfpow"][:, 0:1], w["halfpow"][:, 0:1], ALU.mult)


class LayerNorm:

    def __init__(self, nc, ctx, sem, w, name):
        self.nc, self.w = nc, w
        self.stats, self.mean, self.var, self.rstd = (
            [ctx.enter_context(nc.sbuf_tensor(f"{name}_{what}{i}", [P, TILES, n], F32)) for i in range(2)]
            for what, n in (("stats", 6), ("mean", 2), ("var", 1), ("rstd", 1)))
        self.stats_done, self.mean_done, self.var_done, self.rstd_done = w["ln_sems"]
        self.before = G * w["ln_stages"]
        w["ln_stages"] += 1

    def moments(self, dve, y, j, g):
        for n in range(TILES):
            last = self.nc.vector.bn_stats(self.stats[j][:, n, :], y[:, n, :])
        last.then_inc(self.stats_done, 1)
        dve.wait_ge(self.stats_done, g + (1 + self.before))
        carry_dve(self.nc, self.w)
        for n in range(TILES):
            last = self.nc.vector.bn_aggr(self.mean[j][:, n, :], self.stats[j][:, n, :])
        last.then_inc(self.mean_done, 1)
        dve.wait_ge(self.mean_done, g + (1 + self.before))
        self.nc.vector.tensor_scalar(self.var[j][:], self.mean[j][:, :, 1:2], LN_EPS, None, ALU.add
                                     ).then_inc(self.var_done, 1)

    def root(self, pool, halfpow, j, g):
        pool.wait_ge(self.var_done, g + (1 + self.before))
        self.nc.gpsimd.tensor_tensor(self.rstd[j][:].rearrange("p n o -> p (n o)"),
                                     self.var[j][:].rearrange("p n o -> p (n o)"), halfpow[:, 0:TILES],
                                     ALU.pow).then_inc(self.rstd_done, 1)

    def normalise(self, dve, y, dst, j, g):
        dve.wait_ge(self.rstd_done, g + (1 + self.before))
        for n in range(TILES):
            last = self.nc.vector.tensor_scalar(dst[:, n, :], y[:, n, :], self.mean[j][:, n, 0:1],
                                                self.rstd[j][:, n, :], ALU.subtract, ALU.mult)
        return last


def group_tiles(t, g):
    return t[:, bass.ds(g * TILES, TILES), :]


def group_cols(t, g):
    return t[:, bass.ds(g * GT, GT)]


def mix_in_stage(nc, a, w, sem):
    x_in = [sem("mi_x_in0"), sem("mi_x_in1")]
    (squared, summed, rooted, inverted, spread, turned, normed, projected, biased, added, x1_ready, x1_turned, x1T_ready, x1_kept) = (
        sem("mi_" + n) for n in (
            "squared", "summed", "rooted", "inverted", "spread", "turned", "normed", "projected", "biased", "added", "x1_ready",
            "x1_turned", "x1T_ready", "x1_kept"))
    x = a["x"].rearrange("b s d -> (b s) d")
    cols = w["cols"]
    with ExitStack() as ctx:
        def mem(name, shape):
            return [ctx.enter_context(nc.sbuf_tensor(f"mi_{name}{i}", shape, F32)) for i in range(2)]

        def bank(name, shape):
            return [ctx.enter_context(nc.psum_tensor(f"mi_{name}{i}", shape, F32)) for i in range(2)]

        xs = mem("xs", [P, TILES, D])
        sq = mem("sq", [P, GB, S])
        rms = mem("rms", [P, TILES * H])
        rexp = mem("rexp", [P, TILES * H, HD])
        on = mem("on", [P, GB, S])
        y = mem("y", [P, TILES, D])
        x1 = mem("x1", [P, TILES, D])
        ps_s = bank("ps_s", [P, 512])
        ps_r, = [ctx.enter_context(nc.psum_tensor("mi_ps_r", [P, GB, S], F32))]
        ps_y = bank("ps_y", [P, TILES, D])
        ps_t, = [ctx.enter_context(nc.psum_tensor("mi_ps_t", [P, TILES, P], F32))]
        ln = LayerNorm(nc, ctx, sem, w, "mi_ln")

        def cols_of(t, g):
            return t[:, :, bass.ds(g * GB, GB)].rearrange("p t b -> p b t")

        block = ctx.enter_context(nc.Block())

        @block.sync
        def _(sp):
            def load(g, j):
                sp.dma_start(xs[j][:], x[bass.ds(g * GT, GT), :].rearrange("(n p) d -> p n d", p=P)
                             ).then_inc(x_in[j], 16)
            load(0, 0)
            load(1, 1)
            with sp.Fori(0, G // 2 - 1) as it:
                for j in range(2):
                    g = it * 2 + j
                    sp.wait_ge(added, g + 1)
                    load(g + 2, j)

        @block.scalar
        def _(act):
            def squares(x, j):
                if not isinstance(x, int) or x >= 2:
                    act.wait_ge(summed, x - 1)
                nc.scalar.activation(sq[j][:], cols_of(w["bT"], x), ACT.Square).then_inc(squared, 1)

            def root(x, j):
                act.wait_ge(summed, x + 1)
                nc.scalar.activation(rms[j][:], ps_s[j][:, 0:TILES * H], ACT.Sqrt, bias=cols[:, C_EPS:C_EPS + 1],
                                     scale=1.0 / HD).then_inc(rooted, 1)

            def repeat(x, j):
                act.wait_ge(inverted, x + 1)
                nc.scalar.activation(rexp[j][:], rms[j][:].unsqueeze(2).to_broadcast([P, TILES * H, HD]), ACT.Identity
                                     ).then_inc(spread, 1)

            def group(g, j):
                if not final(g):
                    repeat(g + 1, 1 - j)
                if not last_two(g):
                    squares(g + 2, j)
                    root(g + 2, j)
                act.wait_ge(x1_turned, done(g))
                nc.scalar.activation(group_cols(w["x1T"], g), ps_t[:].rearrange("p n d -> p (n d)"), ACT.Identity
                                     ).then_inc(x1T_ready, 1)
            act.sem_inc(x1T_ready, 1)
            squares(0, 0)
            squares(1, 1)
            root(0, 0)
            root(1, 1)
            repeat(0, 0)
            with act.Fori(0, (G - 2) // 2) as it:
                group(it * 2, 0)
                group(it * 2 + 1, 1)
            group(G - 2, 0)
            group(G - 1, 1)

        @block.tensor
        def _(pe):
            def add_squares(x, j):
                pe.wait_ge(squared, x + 1)
                if not isinstance(x, int) or x >= 2:
                    pe.wait_ge(rooted, x - 1)
                for n in range(TILES):
                    last = nc.tensor.matmul(ps_s[j][:, n * H:(n + 1) * H],
                                            sq[j][:].rearrange("p b s -> p (b s)")[:, n * P:(n + 1) * P],
                                            w["headsel"][:], start=True, stop=True)
                last.then_inc(summed, 1)

            def turn_norms(x, j):
                if not first(x):
                    pe.wait_ge(normed, x)
                pe.wait_ge(spread, x + 1)
                for n in range(TILES):
                    last = nc.tensor.transpose(ps_r[:].rearrange("p b s -> p (b s)")[:, n * P:(n + 1) * P],
                                               rexp[j][:, n * H:(n + 1) * H, :].rearrange("p h d -> p (h d)"),
                                               w["ident"][:])
                last.then_inc(turned, 1)

            def project(x, j):
                pe.wait_ge(normed, x + 1)
                if not isinstance(x, int) or x >= 2:
                    pe.wait_ge(added, x - 1)
                for n in range(TILES):
                    last = nc.tensor.matmul(ps_y[j][:, n, :], on[j][:].rearrange("p b s -> p (b s)")[:, n * P:(n + 1) * P],
                                            w["wT"][:, O_, :], start=True, stop=True)
                last.then_inc(projected, 1)

            def group(g, j):
                if not final(g):
                    turn_norms(g + 1, 1 - j)
                if not last_two(g):
                    add_squares(g + 2, j)
                if not final(g):
                    project(g + 1, 1 - j)
                pe.wait_ge(x1_ready, g + 1)
                pe.wait_ge(x1T_ready, g + 1)
                for n in range(TILES):
                    last = nc.tensor.transpose(ps_t[:, n, :], x1[j][:, n, :], w["ident"][:])
                last.then_inc(x1_turned, 1)
            pe.sem_inc(x1_turned, CREDIT)
            add_squares(0, 0)
            add_squares(1, 1)
            turn_norms(0, 0)
            project(0, 0)
            with pe.Fori(0, (G - 2) // 2) as it:
                group(it * 2, 0)
                group(it * 2 + 1, 1)
            group(G - 2, 0)
            group(G - 1, 1)

        @block.vector
        def _(dve):
            def norms(x, j):
                dve.wait_ge(rooted, x + 1)
                nc.vector.reciprocal(rms[j][:], rms[j][:]).then_inc(inverted, 1)

            def scale(x, j):
                dve.wait_ge(turned, x + 1)
                nc.vector.scalar_tensor_tensor(out=on[j][:], in0=cols_of(w["bT"], x),
                                               scalar=cols[:, C_NORMW:C_NORMW + 1], in1=ps_r[:],
                                               op0=ALU.mult, op1=ALU.mult).then_inc(normed, 1)

            def group(g, j):
                dve.wait_ge(biased, g + 1)
                dve.wait_ge(projected, g + 1)
                nc.vector.tensor_tensor(y[j][:], xs[j][:], ps_y[j][:], ALU.add).then_inc(added, 1)
                dve.wait_ge(added, g + 1)
                ln.moments(dve, y[j], j, g)
                if not final(g):
                    scale(g + 1, 1 - j)
                if not last_two(g):
                    norms(g + 2, j)
                dve.wait_ge(x1_turned, free2(g))
                dve.wait_ge(x1_kept, free2(g))
                ln.normalise(dve, y[j], x1[j], j, g).then_inc(x1_ready, 1)
            norms(0, 0)
            norms(1, 1)
            scale(0, 0)
            with dve.Fori(0, (G - 2) // 2) as it:
                group(it * 2, 0)
                group(it * 2 + 1, 1)
            group(G - 2, 0)
            group(G - 1, 1)

        @block.gpsimd
        def _(pool):
            def add_bias(x, j):
                pool.wait_ge(x_in[j], (x - j) * 8 + 16)
                nc.gpsimd.tensor_tensor(xs[j][:], xs[j][:], w["bo_row"][:].unsqueeze(1).to_broadcast([P, TILES, D]),
                                        ALU.add).then_inc(biased, 1)

            def group(g, j):
                if not final(g):
                    add_bias(g + 1, 1 - j)
                ln.root(pool, w["halfpow"], j, g)
                pool.wait_ge(x1_ready, g + 1)
                if not isinstance(g, int):
                    carry_pool(nc, w)
                nc.gpsimd.tensor_copy(group_tiles(w["x1"], g), x1[j][:]).then_inc(x1_kept, 1)
            pool.sem_inc(x1_kept, CREDIT)
            add_bias(0, 0)
            all_groups(pool, group)


def xattn_stage(nc, w, scr, sem):
    gates_in = [sem("xa_gates_in0"), sem("xa_gates_in1")]
    NJ = XE * XC
    NB = 4
    NS = 8
    LAG = 4
    COPY_AT, TURN_AT, ADD_AT, NORM_AT = 5, 7, 9, 13
    NEXT_AT = 8
    BY_DVE = 1
    (hidden, relued, used, high, low_pool, low_dve, x_high, x_split, w_high, pin_split, pout_split, sum_copied,
     turned, added, x2_ready, stats_done) = (sem("xa_" + n) for n in (
         "hidden", "relued", "used", "high", "low_pool", "low_dve", "x_high", "x_split", "w_high", "pin_split",
         "pout_split", "sum_copied", "turned", "added", "x2_ready", "stats_done"))
    with ExitStack() as ctx:
        def mem(name, shape, n=2, dt=F32):
            return [ctx.enter_context(nc.sbuf_tensor(f"xa_{name}{i}", shape, dt)) for i in range(n)]

        def bank(name, shape, n):
            return [ctx.enter_context(nc.psum_tensor(f"xa_{name}{i}", shape, F32)) for i in range(n)]

        gates = mem("gates", [P, XE, GT])
        hid = mem("hid", [P, GT], NB)
        hid_hi, hid_lo = mem("hid_hi", [P, GT], NS, F32R), mem("hid_lo", [P, GT], NS, F32R)
        x_hi, x_lo = mem("x_hi", [P, GT], 2, F32R), mem("x_lo", [P, GT], 2, F32R)
        (pin_hi, pin_lo), (pout_hi, pout_lo) = (mem(n, [P, NJ, P], 2, F32R) for n in ("pin", "pout"))
        oT = mem("oT", [P, GT])
        y = mem("y", [P, TILES, D])
        ps_h = bank("ps_h", [P, GT], NB)
        ps_o = bank("ps_o", [P, GT], 2)
        ps_t, = bank("ps_t", [P, TILES, D], 1)
        ln = LayerNorm(nc, ctx, sem, w, "xa_ln")
        block = ctx.enter_context(nc.Block())

        def wait(eng, semaphore, value):
            if not isinstance(value, int) or value > 0:
                eng.wait_ge(semaphore, value)

        def wait_low(eng, g, m):
            if m % NB == BY_DVE:
                wait(eng, low_dve, g * (NJ // NB) + (m // NB + 1))
            else:
                wait(eng, low_pool, g * (NJ - NJ // NB) + (m // NB * (NB - 1) + (m % NB + 1 if m % NB < BY_DVE else m % NB)))

        @block.sync
        def _(sp):
            sp.wait_ge(w["gates_stored"], w["all_gates"])
            def load(g, j):
                src = dram_ap(scr["gate_scr"], g * GT, [[0, P], [NTOK, XE], [1, GT]])
                sp.dma_start(gates[j][:], src).then_inc(gates_in[j], 16)
            load(0, 0)
            load(1, 1)
            with sp.Fori(0, G // 2 - 1) as it:
                for j in range(2):
                    sp.wait_ge(relued, it * (2 * NJ) + (j + 1) * NJ)
                    load(it * 2 + (j + 2), j)

        @block.tensor
        def _(pe):
            def product(out, weights, m, operand, start, stop):
                (w_hi, w_lo), (o_hi, o_lo) = weights, operand
                nc.tensor.matmul(out, w_hi[:, m, :], o_hi, start=start, stop=False)
                nc.tensor.matmul(out, w_hi[:, m, :], o_lo, start=False, stop=False)
                return nc.tensor.matmul(out, w_lo[:, m, :], o_hi, start=False, stop=stop)

            def turn(x, j):
                pe.wait_ge(sum_copied, x + 1)
                if not first(x):
                    pe.wait_ge(added, x)
                for n in range(TILES):
                    last = nc.tensor.transpose(ps_t[:, n, :], oT[j][:, n * P:(n + 1) * P], w["ident"][:])
                last.then_inc(turned, 1)

            def out_part(g, j, m):
                if first(g) and m % 4 == 0:
                    pe.wait_ge(pout_split, m // 4 + 1)
                wait_low(pe, g, m)
                if m == 0 and (not isinstance(g, int) or g >= 2):
                    pe.wait_ge(sum_copied, g - 1)
                product(ps_o[j][:], (pout_hi, pout_lo), m, (hid_hi[m % NS][:], hid_lo[m % NS][:]),
                        m == 0, m == NJ - 1).then_inc(used, 1)

            def group(g, j):
                pe.wait_ge(x_split, g + 1)
                for m in range(NJ):
                    if first(g) and m % 4 == 0:
                        pe.wait_ge(pin_split, m // 4 + 1)
                    wait(pe, relued, g * NJ + (m + 1 - NB))
                    product(ps_h[m % NB][:], (pin_hi, pin_lo), m, (x_hi[j][:], x_lo[j][:]), True, True
                            ).then_inc(hidden, 1)
                    if m >= LAG:
                        out_part(g, j, m - LAG)
                    elif not first(g):
                        out_part(g - 1, 1 - j, NJ + m - LAG)
                    if m == TURN_AT and not first(g):
                        turn(g - 1, 1 - j)
            pe.sem_inc(turned, CREDIT)
            all_groups(pe, group)
            for m in range(NJ - LAG, NJ):
                out_part(G - 1, 1, m)
            turn(G - 1, 1)

        @block.scalar
        def _(act):
            def split_x(x, j):
                if not isinstance(x, int) or x >= 2:
                    act.wait_ge(hidden, (x - 1) * NJ)
                nc.scalar.activation(x_hi[j][:], group_cols(w["x1T"], x), ACT.Identity).then_inc(x_high, 1)

            def copy_sum(x, j):
                act.wait_ge(used, x * NJ + NJ)
                act.wait_ge(turned, free2(x))
                nc.scalar.activation(oT[j][:], ps_o[j][:], ACT.Identity).then_inc(sum_copied, 1)

            def group(g, j):
                for m in range(NJ):
                    act.wait_ge(relued, g * NJ + (m + 1))
                    wait(act, used, g * NJ + (m + 1 - NS))
                    nc.scalar.activation(hid_hi[m % NS][:], hid[m % NB][:], ACT.Identity).then_inc(high, 1)
                    if m == COPY_AT and not first(g):
                        copy_sum(g - 1, 1 - j)
                    if m == NEXT_AT and not final(g):
                        split_x(g + 1, 1 - j)
            split_x(0, 0)
            for b in range(NJ // 4):
                for hi, src in ((pin_hi, w["pinT"]), (pout_hi, w["poutT"])):
                    nc.scalar.activation(hi[:, 4 * b:4 * b + 4, :], src[:, 4 * b:4 * b + 4, :], ACT.Identity
                                         ).then_inc(w_high, 1)
            all_groups(act, group)
            copy_sum(G - 1, 1)

        @block.vector
        def _(dve):
            def add(x, j):
                dve.wait_ge(turned, done(x))
                nc.vector.tensor_tensor(y[j][:], group_tiles(w["x1"], x), ps_t[:], ALU.add).then_inc(added, 1)
                dve.wait_ge(added, x + 1)
                ln.moments(dve, y[j], j, x)

            def normalise(x, j):
                ln.normalise(dve, y[j], group_tiles(w["x2"], x), j, x).then_inc(x2_ready, 1)
                dve.wait_ge(x2_ready, x + 1)
                if not isinstance(x, int):
                    carry_dve(nc, w)
                for n in range(TILES):
                    t = bass.ds(x * TILES + n, 1)
                    last = nc.vector.bn_stats(w["stats"][:, t, :].rearrange("p n s -> p (n s)"),
                                              w["x2"][:, t, :].rearrange("p n d -> p (n d)"))
                last.then_inc(stats_done, 1)

            def group(g, j):
                dve.wait_ge(gates_in[j], (g - j) * 8 + 16)
                for m in range(NJ):
                    dve.wait_ge(hidden, g * NJ + (m + 1))
                    wait_low(dve, g, m - NB)
                    nc.vector.scalar_tensor_tensor(out=hid[m % NB][:], in0=ps_h[m % NB][:], scalar=0.0,
                                                   in1=gates[j][:, m // XC, :], op0=ALU.max, op1=ALU.mult
                                                   ).then_inc(relued, 1)
                    if m % NB == BY_DVE + 2:
                        dve.wait_ge(high, g * NJ + (m - 1))
                        nc.vector.tensor_tensor(hid_lo[(m - 2) % NS][:], hid[BY_DVE][:],
                                                hid_hi[(m - 2) % NS][:].bitcast(F32), ALU.subtract).then_inc(low_dve, 1)
                    if m == ADD_AT and not first(g):
                        add(g - 1, 1 - j)
                    if m == NORM_AT and not first(g):
                        normalise(g - 1, 1 - j)
            for b in range(NJ // 4):
                part = slice(4 * b, 4 * b + 4)
                dve.wait_ge(w_high, 2 * b + 1)
                nc.vector.tensor_tensor(pin_lo[:, part, :], w["pinT"][:, part, :], pin_hi[:, part, :].bitcast(F32),
                                        ALU.subtract).then_inc(pin_split, 1)
            all_groups(dve, group)
            add(G - 1, 1)
            normalise(G - 1, 1)

        @block.gpsimd
        def _(pool):
            def split_x(x, j):
                pool.wait_ge(x_high, x + 1)
                if not isinstance(x, int):
                    carry_pool(nc, w, j)
                nc.gpsimd.tensor_tensor(x_lo[j][:], group_cols(w["x1T"], x), x_hi[j][:].bitcast(F32), ALU.subtract
                                        ).then_inc(x_split, 1)

            def group(g, j):
                for m in range(NJ):
                    if m % NB != BY_DVE:
                        pool.wait_ge(high, g * NJ + (m + 1))
                        nc.gpsimd.tensor_tensor(hid_lo[m % NS][:], hid[m % NB][:], hid_hi[m % NS][:].bitcast(F32),
                                                ALU.subtract).then_inc(low_pool, 1)
                    if m == ADD_AT + 1 and not first(g):
                        ln.root(pool, w["halfpow"], 1 - j, g - 1)
                    if m == NEXT_AT + 1 and not final(g):
                        split_x(g + 1, 1 - j)
            split_x(0, 0)
            for b in range(NJ // 4):
                part = slice(4 * b, 4 * b + 4)
                pool.wait_ge(w_high, 2 * b + 2)
                nc.gpsimd.tensor_tensor(pout_lo[:, part, :], w["poutT"][:, part, :], pout_hi[:, part, :].bitcast(F32),
                                        ALU.subtract).then_inc(pout_split, 1)
            all_groups(pool, group)
            ln.root(pool, w["halfpow"], 1, G - 1)


def attend_stage(nc, a, w, sem):
    UB = 2
    NU = GB // UB
    RG = 4
    NPR = GB // 2
    AHEAD = 2
    NW = 11
    NT = NTOK // P
    weights_in = sem("at_weights_in")
    (moments, rooted, xh_ready, xh_turned, h1_ready, twin_ready, q_proj, q_read, k_proj, k_read, v_proj, v_read,
     scored, maxed, shifted, exped, p_turned, p_copied, mixed, inverted, c_ready, c_turned, c_copied, o_proj,
     x2_biased, h_ready, summed, hh_ready, hh_turned, h2_ready, routed, logits_ready, h2_kept, const, mask_made) = (
         sem("at_" + n) for n in (
             "moments", "rooted", "xh_ready", "xh_turned", "h1_ready", "twin_ready", "q_proj", "q_read", "k_proj",
             "k_read", "v_proj", "v_read", "scored", "maxed", "shifted", "exped", "p_turned", "p_copied", "mixed",
             "inverted", "c_ready", "c_turned", "c_copied", "o_proj", "x2_biased", "h_ready", "summed", "hh_ready",
             "hh_turned", "h2_ready", "routed", "logits_ready", "h2_kept", "const", "mask_made"))
    cols = w["cols"]
    with ExitStack() as ctx:
        def mem(name, shape, n=2):
            return [ctx.enter_context(nc.sbuf_tensor(f"at_{name}{i}", shape, F32)) for i in range(n)]

        def bank(name, shape, n):
            return [ctx.enter_context(nc.psum_tensor(f"at_{name}{i}", shape, F32)) for i in range(n)]

        wqkv, = mem("wqkv", [P, 3, D], 1)
        wo, = mem("wo", [P, 2, D], 1)
        wg, = mem("wg", [P, NE], 1)
        bo, = mem("bo", [P, D], 1)
        bv, = mem("bv", [P, 2], 1)
        qmask, = mem("qmask", [P, RG], 1)
        mean, = mem("mean", [P, NT, 2], 1)
        var, = mem("var", [P, NT], 1)
        dev, = mem("dev", [P, NT], 1)
        rstd, = mem("rstd", [P, NT, 1], 1)
        xh = mem("xh", [P, TILES, D])
        h1T, = mem("h1T", [P, GB, 2, S], 1)
        qx = mem("qx", [P, GB, RG, S])
        kx = mem("kx", [P, GB, RG, S])
        vx = mem("vx", [P, GB * 2, 2, 2, 2, HD + 1])
        prob = mem("prob", [P, 2 * UB, RG, S], NU)
        pT = mem("pT", [P, RG, P], UB)
        top = mem("top", [P, 2 * UB * RG])
        rden = mem("rden", [P, UB * 8])
        cx = mem("cx", [P, GB * 8, HD])
        cT, = mem("cT", [P, NPR, 2, 2, S], 1)
        xb = mem("xb", [P, TILES, D])
        h = mem("h", [P, TILES, D])
        hh = mem("hh", [P, TILES, D])
        h2T = mem("h2T", [P, GT])
        ps_s = bank("ps_s", [P, 2 * UB, RG, S], 2)
        ps_p = bank("ps_p", [P, RG, P], UB)
        ps_c, = bank("ps_c", [P, 512], 1)
        ps_m, = bank("ps_m", [P, 512], 1)
        mix = ps_c[:, 0:UB * 16 * (HD + 1)].rearrange("p (n x y h d) -> p n x y h d", x=2, y=2, h=2, d=HD + 1)
        mix_slots = ps_c[:, 0:UB * 16 * (HD + 1)].rearrange("p (n h d) -> p n h d", h=2, d=HD + 1)
        ln2 = LayerNorm(nc, ctx, sem, w, "at_ln2")
        tiles_m = ps_m[:].rearrange("p (n d) -> p n d", n=TILES)
        batches_m = ps_m[:].rearrange("p (b s) -> p b s", b=GB)
        block = ctx.enter_context(nc.Block())

        @block.sync
        def _(sp):
            sp.dma_start(wqkv[:].rearrange("p a d -> p (a d)"), a["L0_ffn_w_qkv"]).then_inc(weights_in, 16)
            for half in range(2):
                for b2 in range(2):
                    src = dram_ap(a["L0_ffn_w_o"], half * HD * D, [[2 * HD * D, H // 2], [D, HD], [1, D]])
                    sp.dma_start(wo[b2 * 64:(b2 + 1) * 64, half, :], src).then_inc(weights_in, 16)
                    src = dram_ap(a["L0_ffn_b_qkv"], 2 * D + half * HD, [[2 * HD, H // 2], [1, HD], [1, 1]])
                    sp.dma_start(bv[b2 * 64:(b2 + 1) * 64, half:half + 1], src).then_inc(weights_in, 16)
            sp.dma_start(wg[:], a["L0_ffn_w_gate"]).then_inc(weights_in, 16)
            sp.dma_start(bo[:], dram_ap(a["L0_ffn_b_o"], 0, [[0, P], [1, D]])).then_inc(weights_in, 16)
            for e in range(NE):
                sp.dma_start(w["w1"][e // 4][:, e % 4 * FC:(e % 4 + 1) * FC, :].rearrange("p c f -> p (c f)"),
                             a["L0_ffn_w1"][e]).then_inc(w["experts_in"], 16)
                sp.dma_start(w["w2"][:, e * FC * D:(e + 1) * FC * D].rearrange("p (c d) -> p c d", d=D),
                             a["L0_ffn_w2"][e].rearrange("(c p) d -> p c d", p=P)).then_inc(w["experts_in"], 16)
            sp.wait_ge(weights_in, NW * 16)
            sp.wait_ge(w["experts_in"], NE * 32)

        @block.gpsimd
        def _(pool):
            for t in (*vx, *kx, cT):
                nc.gpsimd.memset(t[:], 0.0).then_inc(const, 1)
            pool.wait_ge(const, 5)
            for j in range(2):
                for half in range(2):
                    nc.gpsimd.memset(vx[j][half * S:(half + 1) * S, :, half, :, :, HD:HD + 1], 1.0).then_inc(const, 1)
            pool.wait_ge(const, 9)
            pool.wait_ge(weights_in, NW * 16)

            def output(x, j):
                ln2.root(pool, w["halfpow"], j, x)
                pool.wait_ge(h_ready, done(x))
                if not isinstance(x, int):
                    carry_pool(nc, w, 0)
                nc.gpsimd.tensor_tensor(group_tiles(w["x1"], x), h[j][:], group_tiles(w["x2"], x), ALU.add
                                        ).then_inc(summed, 1)
                pool.wait_ge(h2_ready, done(x))
                if not isinstance(x, int):
                    carry_pool(nc, w, 1)
                nc.gpsimd.tensor_copy(group_cols(w["h2T"], x), h2T[j][:]).then_inc(h2_kept, 1)

            def twin(x):
                pool.wait_ge(h1_ready, x + 1)
                if not isinstance(x, int):
                    carry_pool(nc, w, 3)
                nc.gpsimd.tensor_copy(h1T[:, :, 1, :], h1T[:, :, 0, :]).then_inc(twin_ready, 1)

            def group(g, j):
                if not final(g):
                    twin(g + 1)
                if not isinstance(g, int) or g >= 2:
                    pool.wait_ge(h_ready, free2(g))
                    carry_pool(nc, w, 2)
                nc.gpsimd.tensor_tensor(xb[j][:], group_tiles(w["x2"], g),
                                        bo[:].unsqueeze(1).to_broadcast([P, TILES, D]), ALU.add).then_inc(x2_biased, 1)
                if not first(g):
                    output(g - 1, 1 - j)
            pool.sem_inc(h2_kept, CREDIT)
            pool.sem_inc(summed, CREDIT)
            twin(0)
            all_groups(pool, group)
            output(G - 1, 1)

        @block.tensor
        def _(pe):
            pe.wait_ge(weights_in, NW * 16)
            pe.wait_ge(const, 9)
            pe.wait_ge(mask_made, 5)

            def turn_x(x, j):
                if not first(x):
                    pe.wait_ge(v_read, x * 2)
                    pe.wait_ge(logits_ready, x)
                pe.wait_ge(xh_ready, x + 1)
                for n in range(TILES):
                    last = nc.tensor.transpose(tiles_m[:, n, :], xh[j][:, n, :], w["ident"][:])
                last.then_inc(xh_turned, 1)

            def make_q(x):
                pe.wait_ge(h1_ready, x + 1)
                nc.tensor.matmul(ps_m[:], wqkv[:, 0, :], h1T[:, :, 0, :], start=True, stop=True).then_inc(q_proj, 1)

            def make_k(x):
                pe.wait_ge(q_read, x + 1)
                nc.tensor.matmul(ps_m[:], wqkv[:, 1, :], h1T[:, :, 0, :], start=True, stop=True).then_inc(k_proj, 1)

            def make_v(x, half):
                if half == 0:
                    pe.wait_ge(k_read, x + 1)
                    pe.wait_ge(twin_ready, x + 1)
                else:
                    pe.wait_ge(v_read, x * 2 + 1)
                for b in range(4):
                    last = nc.tensor.matmul(tiles_m[:, b, :], h1T[:, half * 4 + b, :, :].rearrange("p a s -> p (a s)"),
                                            wqkv[:, 2, :], start=True, stop=True)
                last.then_inc(v_proj, 1)

            def scores(n, j, u):
                if not isinstance(n, int) or n >= 2:
                    pe.wait_ge(shifted, n - 1)
                for b in range(UB):
                    for hp in range(2):
                        last = nc.tensor.matmul(
                            ps_s[u % 2][:, b * 2 + hp, :, :].rearrange("p r s -> p (r s)"),
                            qx[j][:, u * UB + b, 2 * hp:2 * hp + 2, :].rearrange("p h s -> p (h s)"),
                            kx[j][:, u * UB + b, :, :].rearrange("p r s -> p (r s)"), start=True, stop=True)
                last.then_inc(scored, 1)

            def turn_probs(n, u, b):
                pe.wait_ge(p_copied, n * UB + (b + 1))
                for rp in range(2):
                    for hp in range(2):
                        last = nc.tensor.transpose(
                            ps_p[b][:, rp * 2 + hp, :],
                            prob[u][:, b * 2 + hp, 2 * rp:2 * rp + 2, :].rearrange("p r s -> p (r s)"), w["ident"][:])
                last.then_inc(p_turned, 1)

            def mix_values(n, j, u, b):
                pe.wait_ge(p_copied, n * UB + (b + 3))
                for rp in range(2):
                    for hp in range(2):
                        last = nc.tensor.matmul(mix[:, b * 2 + rp, :, hp, :, :].rearrange("p x h d -> p x (h d)"),
                                                pT[b][:, rp * 2 + hp, :],
                                                vx[j][:, (u * UB + b) * 2 + rp, :, hp, :, :].rearrange(
                                                    "p x h d -> p x (h d)"), start=True, stop=True)
                last.then_inc(mixed, 1)

            def turn_mix(x, j, after_v):
                pe.wait_ge(c_ready, x * NU + NU)
                if after_v:
                    pe.wait_ge(v_read, x * 2 + 6)
                elif not first(x):
                    pe.wait_ge(logits_ready, x + 2)
                for p in range(NPR):
                    last = nc.tensor.transpose(tiles_m[:, p, :], cx[j][:, p * 16:p * 16 + 16, :].rearrange("p n d -> p (n d)"),
                                               w["ident"][:])
                last.then_inc(c_turned, 1)

            def make_output(x):
                pe.wait_ge(c_copied, x + 1)
                for p in range(NPR):
                    for half in range(2):
                        last = nc.tensor.matmul(tiles_m[:, p, :], cT[:, p, half, :, :].rearrange("p b s -> p (b s)"),
                                                wo[:, half, :], start=(half == 0), stop=(half == 1))
                last.then_inc(o_proj, 1)

            def turn_h(x, j):
                pe.wait_ge(hh_ready, x + 1)
                for n in range(TILES):
                    last = nc.tensor.transpose(tiles_m[:, n, :], hh[j][:, n, :], w["ident"][:])
                last.then_inc(hh_turned, 1)

            def route(x, j):
                pe.wait_ge(h2_ready, done(x))
                for n in range(TILES):
                    last = nc.tensor.matmul(ps_m[:, n * NE:(n + 1) * NE], h2T[j][:, n * P:(n + 1) * P], wg[:],
                                            start=True, stop=True)
                last.then_inc(routed, 1)

            def group(g, j):
                ahead, behind = not final(g), not first(g)
                for u in range(NU):
                    n = g * NU + u
                    if u < AHEAD:
                        scores(n + AHEAD, j, u + AHEAD)
                    elif ahead:
                        if u == AHEAD:
                            pe.wait_ge(q_read, g + 2)
                            pe.wait_ge(k_read, g + 2)
                        scores(n + AHEAD, 1 - j, u + AHEAD - NU)
                    pe.wait_ge(exped, n + 1)
                    turn_probs(n, u, 0)
                    turn_probs(n, u, 1)
                    if u == 0 and ahead:
                        turn_x(g + 1, 1 - j)
                    if u == 1 and ahead:
                        make_k(g + 1)
                    if u == 2 and ahead:
                        make_v(g + 1, 1)
                    if not (first(g) and u == 0):
                        pe.wait_ge(c_ready, n)
                    mix_values(n, j, u, 0)
                    if u == 0 and ahead:
                        make_q(g + 1)
                    if u == 2 and behind:
                        turn_mix(g - 1, 1 - j, ahead)
                    if u == 3 and behind:
                        turn_h(g - 1, 1 - j)
                    mix_values(n, j, u, 1)
                    if u == 1 and ahead:
                        make_v(g + 1, 0)
                    if u == 2 and behind:
                        make_output(g - 1)
                    if u == 3 and behind:
                        route(g - 1, 1 - j)

            turn_x(0, 0)
            make_q(0)
            make_k(0)
            make_v(0, 0)
            make_v(0, 1)
            pe.wait_ge(q_read, 1)
            for u in range(AHEAD):
                scores(u, 0, u)
            all_groups(pe, group)
            turn_mix(G - 1, 1, False)
            make_output(G - 1)
            turn_h(G - 1, 1)
            route(G - 1, 1)

        @block.scalar
        def _(act):
            act.sem_inc(p_copied, CREDIT)
            act.sem_inc(logits_ready, CREDIT)
            act.wait_ge(moments, 2)
            nc.scalar.activation(dev[:], var[:], ACT.Sqrt).then_inc(rooted, 1)
            act.sem_inc(h2_ready, CREDIT)
            act.wait_ge(weights_in, NW * 16)
            act.wait_ge(const, 9)

            def read_h1(x):
                act.wait_ge(xh_turned, x + 1)
                nc.scalar.activation(h1T[:, :, 0, :], batches_m, ACT.Identity, bias=cols[:, C_LN1B:C_LN1B + 1],
                                     scale=cols[:, C_LN1W:C_LN1W + 1]).then_inc(h1_ready, 1)

            def read_k(x, j):
                act.wait_ge(k_proj, x + 1)
                for r in range(RG):
                    rows = slice(32 * r, 32 * r + 32)
                    last = nc.scalar.activation(kx[j][rows, :, r, :], batches_m[rows], ACT.Identity,
                                                bias=cols[rows, C_QKV + 1:C_QKV + 2])
                last.then_inc(k_read, 1)

            def read_v(x, j, half):
                act.wait_ge(v_proj, x * 2 + (half + 1))
                for r2 in range(2):
                    rows = slice(r2 * S, (r2 + 1) * S)
                    src = ps_m[rows, :].rearrange("p (n x y d) -> p n x y d", x=2, y=4, d=HD)[:, :, r2, :, :]
                    dst = vx[j][rows, half * GB:(half + 1) * GB, r2, :, :, 0:HD].rearrange("p n y h d -> p n (y h) d")
                    last = nc.scalar.activation(dst, src, ACT.Identity)
                last.then_inc(v_read, 1)

            def copy_turned(n, b):
                act.wait_ge(p_turned, n * UB + (b + 1))
                nc.scalar.activation(pT[b][:], ps_p[b][:], ACT.Identity).then_inc(p_copied, 1)

            def exp(n, u):
                act.wait_ge(shifted, n + 1)
                pv = prob[u][:].rearrange("p x r s -> p (x r s)")
                nc.scalar.activation(pv, pv, ACT.Exp).then_inc(exped, 1)

            def read_mix(x):
                act.wait_ge(c_turned, x + 1)
                src = ps_m[:].rearrange("p (n h s) -> p n h s", n=NPR, h=2)
                for b2 in range(2):
                    rows = slice(b2 * 64, (b2 + 1) * 64)
                    for half in range(2):
                        last = nc.scalar.activation(cT[rows, :, half, b2, :], src[rows, :, half, :], ACT.Identity,
                                                    bias=bv[rows, half:half + 1])
                last.then_inc(c_copied, 1)

            def read_h2(x, j):
                act.wait_ge(hh_turned, x + 1)
                act.wait_ge(h2_kept, free2(x))
                nc.scalar.activation(h2T[j][:], ps_m[:], ACT.Identity, bias=cols[:, C_LN2B:C_LN2B + 1],
                                     scale=cols[:, C_LN2W:C_LN2W + 1]).then_inc(h2_ready, 1)

            def read_logits(x):
                act.wait_ge(routed, x + 1)
                nc.scalar.activation(group_tiles(w["logits"], x),
                                     ps_m[:, 0:TILES * NE].rearrange("p (n e) -> p n e", e=NE), ACT.Identity
                                     ).then_inc(logits_ready, 1)

            def group(g, j):
                ahead, behind = not final(g), not first(g)
                for u in range(NU):
                    n = g * NU + u
                    copy_turned(n, 0)
                    copy_turned(n, 1)
                    if u == 0 and ahead:
                        read_h1(g + 1)
                    if u == 1 and ahead:
                        read_k(g + 1, 1 - j)
                    if u == 2 and ahead:
                        read_v(g + 1, 1 - j, 1)
                    if u == 2 and behind:
                        read_mix(g - 1)
                    if u == 3 and behind:
                        read_h2(g - 1, 1 - j)
                    if u < AHEAD or ahead:
                        exp(n + AHEAD, (u + AHEAD) % NU)
                    if u == 1 and ahead:
                        read_v(g + 1, 1 - j, 0)
                    if u == 3 and behind:
                        read_logits(g - 1)

            read_h1(0)
            read_k(0, 0)
            read_v(0, 0, 0)
            read_v(0, 0, 1)
            for u in range(AHEAD):
                exp(u, u)
            all_groups(act, group)
            read_mix(G - 1)
            read_h2(G - 1, 1)
            read_logits(G - 1)

        @block.vector
        def _(dve):
            for h4 in range(RG):
                nc.vector.tensor_reduce(qmask[:, h4:h4 + 1], w["headsel"][:, h4:H:RG], AX.X, ALU.add).then_inc(mask_made, 1)
            for t in range(NT):
                last = nc.vector.bn_aggr(mean[:, t, :], w["stats"][:, t, :])
            last.then_inc(moments, 1)
            dve.wait_ge(moments, 1)
            nc.vector.tensor_scalar(var[:], mean[:, :, 1], LN_EPS, None, ALU.add).then_inc(moments, 1)
            dve.wait_ge(mask_made, 4)
            nc.vector.tensor_scalar(qmask[:], qmask[:], float(HD) ** -0.5, None, ALU.mult).then_inc(mask_made, 1)
            dve.wait_ge(mask_made, 5)
            dve.wait_ge(weights_in, NW * 16)
            dve.sem_inc(h_ready, CREDIT)
            dve.wait_ge(rooted, 1)
            r = rstd[:].rearrange("p n o -> p (n o)")
            nc.vector.reciprocal(r, dev[:]).then_inc(moments, 1)
            dve.wait_ge(moments, 3)
            nc.vector.tensor_tensor(dev[:], r, r, ALU.mult).then_inc(moments, 1)
            dve.wait_ge(moments, 4)
            nc.vector.tensor_tensor(dev[:], dev[:], var[:], ALU.mult).then_inc(moments, 1)
            dve.wait_ge(moments, 5)
            nc.vector.tensor_scalar(dev[:], dev[:], -0.5, 1.5, ALU.mult, ALU.add).then_inc(moments, 1)
            dve.wait_ge(moments, 6)
            nc.vector.tensor_tensor(r, r, dev[:], ALU.mult).then_inc(moments, 1)
            dve.wait_ge(moments, 7)

            def normalise_x(x, j):
                if not isinstance(x, int) or x >= 2:
                    dve.wait_ge(xh_turned, x - 1)
                for n in range(TILES):
                    t = bass.ds(x * TILES + n, 1)
                    last = nc.vector.tensor_scalar(xh[j][:, n, :], w["x2"][:, t, :].rearrange("p n d -> p (n d)"),
                                                   mean[:, t, 0:1].rearrange("p n o -> p (n o)"),
                                                   rstd[:, t, :].rearrange("p n o -> p (n o)"), ALU.subtract, ALU.mult)
                last.then_inc(xh_ready, 1)

            def read_q(x, j):
                dve.wait_ge(q_proj, x + 1)
                for h4 in range(RG):
                    last = nc.vector.tensor_scalar(qx[j][:, :, h4, :], batches_m, cols[:, C_QKV:C_QKV + 1],
                                                   qmask[:, h4:h4 + 1], ALU.add, ALU.mult)
                last.then_inc(q_read, 1)

            def shift(n, u):
                dve.wait_ge(scored, n + 1)
                sc = ps_s[u % 2][:].rearrange("p x r s -> p (x r) s")
                nc.vector.tensor_reduce(top[u % 2][:], sc, AX.X, ALU.max).then_inc(maxed, 1)
                dve.wait_ge(maxed, n + 1)
                nc.vector.tensor_tensor(prob[u][:].rearrange("p x r s -> p (x r) s"), sc,
                                        top[u % 2][:].unsqueeze(2).to_broadcast([P, 2 * UB * RG, S]),
                                        ALU.subtract).then_inc(shifted, 1)

            def divide(n, j, u):
                dve.wait_ge(mixed, n * UB + UB)
                for half in range(2):
                    rows = slice(half * S, (half + 1) * S)
                    last = nc.vector.reciprocal(rden[u % 2][rows, :], mix_slots[rows, :, half, HD])
                last.then_inc(inverted, 1)
                dve.wait_ge(inverted, n + 1)
                for half in range(2):
                    rows = slice(half * S, (half + 1) * S)
                    last = nc.vector.tensor_tensor(cx[j][rows, u * 16:u * 16 + 16, :], mix_slots[rows, :, half, 0:HD],
                                                   rden[u % 2][rows, :].unsqueeze(2).to_broadcast([S, UB * 8, HD]),
                                                   ALU.mult)
                last.then_inc(c_ready, 1)

            def residual(x, j):
                dve.wait_ge(x2_biased, x + 1)
                dve.wait_ge(summed, free2(x))
                dve.wait_ge(o_proj, x + 1)
                nc.vector.tensor_tensor(h[j][:], xb[j][:], tiles_m, ALU.add).then_inc(h_ready, 1)
                dve.wait_ge(h_ready, done(x))
                ln2.moments(dve, h[j], j, x)

            def normalise_h(x, j):
                ln2.normalise(dve, h[j], hh[j], j, x).then_inc(hh_ready, 1)

            def group(g, j):
                ahead, behind = not final(g), not first(g)
                for u in range(NU):
                    n = g * NU + u
                    if u == 0 and ahead:
                        normalise_x(g + 1, 1 - j)
                    if u in (1, 2):
                        divide(n - 1, j, u - 1)
                    elif u == 0 and behind:
                        divide(n - 1, 1 - j, NU - 1)
                    if u == 3 and behind:
                        normalise_h(g - 1, 1 - j)
                    if u < AHEAD or ahead:
                        shift(n + AHEAD, (u + AHEAD) % NU)
                    if u == 0 and ahead:
                        read_q(g + 1, 1 - j)
                    if u == 2:
                        divide(n, j, u)
                    if u == 2 and behind:
                        residual(g - 1, 1 - j)

            normalise_x(0, 0)
            read_q(0, 0)
            for u in range(AHEAD):
                shift(u, u)
            all_groups(dve, group)
            divide(G * NU - 1, 1, NU - 1)
            residual(G - 1, 1)
            normalise_h(G - 1, 1)


def moe_stage(nc, a, w, out, sem):
    NJ = NE * FC
    HB = 4
    GB_ = 2 * FC
    NT = NTOK // P
    w1_split, h2_high, h2_split = sem("mo_w1_split"), sem("mo_h2_high"), sem("mo_h2_split")
    b_in, b1_turned, b1_ready = sem("mo_b_in"), sem("mo_b1_turned"), sem("mo_b1_ready")
    stored = [sem("mo_stored0"), sem("mo_stored1")]
    (exped, route, ranked, share_ready, we_copied, we_turned, weT_ready, biased, hidden, gelued, used,
     combined, o_ready) = (sem("mo_" + n) for n in (
         "exped", "route", "ranked", "share_ready", "we_copied", "we_turned", "weT_ready", "biased",
         "hidden", "gelued", "used", "combined", "o_ready"))
    with ExitStack() as ctx:
        def mem(name, shape, n=2):
            return [ctx.enter_context(nc.sbuf_tensor(f"mo_{name}{i}", shape, F32)) for i in range(n)]

        def bank(name, shape, n):
            return [ctx.enter_context(nc.psum_tensor(f"mo_{name}{i}", shape, F32)) for i in range(n)]

        b1_rows, = mem("b1_rows", [NJ, P], 1)
        b1, = mem("b1", [P, NE, FC], 1)
        b2, = mem("b2", [NE, D], 1)
        def part(name, shape):
            return ctx.enter_context(nc.sbuf_tensor(f"mo_{name}", shape, F32R))

        w1_hi, w1_lo = part("w1_hi", [P, NE * FC, P]), part("w1_lo", [P, NE * FC, P])
        h2_hi, h2_lo = ([part(f"{n}{i}", [P, GT]) for i in range(2)] for n in ("h2_hi", "h2_lo"))
        share, = mem("share", [P, NT, NE], 1)
        first, second, cand, ps = mem("rt", [P, NT, NE], 4)
        m1, m2, r1, r2 = mem("rs", [P, NT], 4)
        rank, = mem("rank", [P, NE], 1)
        we = mem("we", [P, TILES, NE])
        weT = mem("weT", [NE, GT])
        gel = mem("gel", [P, GT], GB_)
        acc = mem("acc", [P, TILES, D])
        fin = mem("fin", [P, TILES, D])
        ps_h = bank("ps_h", [P, GT], HB)
        ps_y = bank("ps_y", [P, TILES, D], 2)
        ps_w_all, = bank("ps_w", [P, GT], 1)
        ps_w = ps_w_all[0:NE, :]
        ps_b, = bank("ps_b", [P, TILES, D], 1)
        ln = LayerNorm(nc, ctx, sem, w, "mo_ln")
        block = ctx.enter_context(nc.Block())
        outv = out.rearrange("b s d -> (b s) d")

        @block.sync
        def _(sp):
            sp.dma_start(b1_rows[:], a["L0_ffn_b1"].rearrange("e (c p) -> (e c) p", p=P)).then_inc(b_in, 16)
            sp.dma_start(b2[:], a["L0_ffn_b2"]).then_inc(b_in, 16)
            with sp.Fori(0, G // 2) as it:
                for j in range(2):
                    g = it * 2 + j
                    sp.wait_ge(o_ready, g + 1)
                    sp.dma_start(outv[bass.ds(g * GT, GT), :].rearrange("(n p) d -> p n d", p=P), fin[j][:]
                                 ).then_inc(stored[j], 16)
            for j in range(2):
                sp.wait_ge(stored[j], 16 * (1 + G // 2))

        @block.gpsimd
        def _(pool):
            for e in range(NE):
                nc.gpsimd.memset(rank[:, e:e + 1], float(NE - e)).then_inc(ranked, 1)
            for j in range(2):
                pool.sem_inc(stored[j], 16)

            def split_h2(x, j):
                if not isinstance(x, int) or x >= 2:
                    pool.wait_ge(hidden, (x - 1) * NJ)
                if not isinstance(x, int):
                    carry_pool(nc, w, j)
                nc.gpsimd.tensor_copy(h2_hi[j][:], group_cols(w["h2T"], x)).then_inc(h2_high, 1)
                pool.wait_ge(h2_high, x + 1)
                if not isinstance(x, int):
                    carry_pool(nc, w, 2 + j)
                nc.gpsimd.tensor_tensor(h2_lo[j][:], group_cols(w["h2T"], x), h2_hi[j][:].bitcast(F32), ALU.subtract
                                        ).then_inc(h2_split, 1)

            def split_w1(e):
                src = w["w1"][e // 4][:, e % 4 * FC:(e % 4 + 1) * FC, :]
                hi, lo = (t[:, e * FC:(e + 1) * FC, :] for t in (w1_hi, w1_lo))
                nc.gpsimd.tensor_copy(hi, src).then_inc(w1_split, 1)
                pool.wait_ge(w1_split, 2 * e + 1)
                nc.gpsimd.tensor_tensor(lo, src, hi.bitcast(F32), ALU.subtract).then_inc(w1_split, 1)

            split_h2(0, 0)
            for e in range(NE):
                split_w1(e)
            split_h2(1, 1)
            with pool.Fori(0, G // 2 - 1) as it:
                for j in range(2):
                    g = it * 2 + j
                    ln.root(pool, w["halfpow"], j, g)
                    split_h2(g + 2, j)
            ln.root(pool, w["halfpow"], 0, G - 2)
            ln.root(pool, w["halfpow"], 1, G - 1)

        @block.tensor
        def _(pe):
            pe.sem_inc(we_turned, CREDIT)
            pe.sem_inc(used, 2)
            pe.wait_ge(b_in, 32)
            nc.tensor.transpose(ps_w_all[:, 0:NJ], b1_rows[:], w["ident"][0:NJ, 0:NJ]).then_inc(b1_turned, 1)
            with pe.Fori(0, G // 2) as it:
                for j in range(2):
                    g = it * 2 + j
                    pe.wait_ge(h2_split, g + 1)

                    def up(e):
                        pe.wait_ge(w1_split, 2 * e + 2)
                        for c in range(FC):
                            m = e * FC + c
                            pe.wait_ge(gelued, g * NJ + (m + 1))
                            for n, (wt, x) in enumerate(((w1_hi, h2_hi), (w1_hi, h2_lo), (w1_lo, h2_hi))):
                                last = nc.tensor.matmul(ps_h[m % HB][:], wt[:, e * FC + c, :], x[j][:],
                                                        start=(n == 0), stop=(n == 2))
                            last.then_inc(hidden, 1)

                    def down(e):
                        pe.wait_ge(gelued, g * NJ + (e * FC + FC + HB))
                        pe.wait_ge(combined, g * NE + (e + 1))
                        for n in range(TILES):
                            for c in range(FC):
                                last = nc.tensor.matmul(ps_y[e % 2][:, n, :],
                                                        gel[(e * FC + c) % GB_][:, n * P:(n + 1) * P],
                                                        w["w2"][:, (e * FC + c) * D:(e * FC + c + 1) * D], start=(c == 0), stop=(c == FC - 1))
                        last.then_inc(used, 1)
                    up(0)
                    up(1)
                    pe.wait_ge(we_copied, g + 1)
                    pe.wait_ge(weT_ready, g + 1)
                    for n in range(TILES):
                        last = nc.tensor.transpose(ps_w[:, n * P:(n + 1) * P], we[j][:, n, :], w["ident"][:])
                    last.then_inc(we_turned, 1)
                    down(0)
                    up(2)
                    pe.wait_ge(weT_ready, g + 2)
                    pe.wait_ge(combined, g * NE + 2)
                    for n in range(TILES):
                        last = nc.tensor.matmul(ps_b[:, n, :], weT[j][:, n * P:(n + 1) * P], b2[:], start=True, stop=True)
                    last.then_inc(biased, 1)
                    for e in range(3, NE):
                        down(e - 2)
                        up(e)
                    down(NE - 2)
                    down(NE - 1)

        @block.scalar
        def _(act):
            act.sem_inc(gelued, HB)
            act.wait_ge(b1_turned, 1)
            nc.scalar.copy(b1[:].rearrange("p e c -> p (e c)"), ps_w_all[:, 0:NJ]).then_inc(b1_ready, 1)
            act.wait_ge(b1_ready, 1)
            act.sem_inc(weT_ready, 1)
            act.wait_ge(route, 2)
            nc.scalar.activation(ps[:], ps[:], ACT.Exp).then_inc(exped, 1)
            with act.Fori(0, G // 2) as it:
                for j in range(2):
                    g = it * 2 + j
                    for e in range(NE):
                        act.wait_ge(used, g * NE + (e + 1))
                        for c in range(FC):
                            m = e * FC + c
                            act.wait_ge(hidden, g * NJ + (m + 1))
                            nc.scalar.activation(gel[m % GB_][:], ps_h[m % HB][:], ACT.Gelu_apprx_tanh,
                                                 bias=b1[:, e, c:c + 1]).then_inc(gelued, 1)
                        if e == 1:
                            act.wait_ge(we_turned, done(g))
                            nc.scalar.copy(weT[j][:], ps_w).then_inc(weT_ready, 1)

        @block.vector
        def _(dve):
            count = [0]

            def link(ins):
                count[0] += 1
                ins.then_inc(route, 1)
                dve.wait_ge(route, count[0])

            lg = w["logits"]
            wide = [P, NT, NE]
            link(nc.vector.tensor_reduce(m1[:], lg[:], AX.X, ALU.max))
            link(nc.vector.tensor_tensor(ps[:], lg[:], m1[:].unsqueeze(2).to_broadcast(wide), ALU.subtract))
            dve.wait_ge(exped, 1)
            dve.wait_ge(ranked, NE)

            def pick(src, m, r, onehot):
                link(nc.vector.tensor_reduce(m[:], src[:], AX.X, ALU.max))
                link(nc.vector.tensor_tensor(cand[:], src[:], m[:].unsqueeze(2).to_broadcast(wide), ALU.is_equal))
                link(nc.vector.tensor_tensor(cand[:], cand[:], rank[:].unsqueeze(1).to_broadcast(wide), ALU.mult))
                link(nc.vector.tensor_reduce(r[:], cand[:], AX.X, ALU.max))
                link(nc.vector.tensor_tensor(onehot[:], cand[:], r[:].unsqueeze(2).to_broadcast(wide), ALU.is_equal))
            pick(ps, m1, r1, first)
            link(nc.vector.scalar_tensor_tensor(out=share[:], in0=first[:], scalar=-4.0, in1=ps[:], op0=ALU.mult, op1=ALU.add))
            pick(share, m2, r2, second)
            link(nc.vector.tensor_tensor(m1[:], m1[:], m2[:], ALU.add))
            link(nc.vector.reciprocal(m1[:], m1[:]))
            link(nc.vector.tensor_tensor(first[:], first[:], second[:], ALU.add))
            link(nc.vector.tensor_tensor(first[:], first[:], ps[:], ALU.mult))
            link(nc.vector.tensor_tensor(share[:], first[:], m1[:].unsqueeze(2).to_broadcast(wide), ALU.mult))
            dve.sem_inc(combined, 2)
            with dve.Fori(0, G // 2) as it:
                for j in range(2):
                    g = it * 2 + j
                    dve.wait_ge(we_turned, free2(g))
                    nc.vector.tensor_copy(we[j][:], group_tiles(share, g)).then_inc(we_copied, 1)
                    dve.wait_ge(we_copied, g + 1)
                    dve.wait_ge(biased, g + 1)
                    nc.vector.tensor_tensor(acc[j][:], group_tiles(w["x1"], g), ps_b[:], ALU.add).then_inc(share_ready, 1)
                    for e in range(NE):
                        dve.wait_ge(used, g * NE + (e + 3))
                        if e == 0:
                            dve.wait_ge(share_ready, g + 1)
                        else:
                            dve.wait_ge(combined, g * NE + (e + 2))
                        for n in range(TILES):
                            last = nc.vector.scalar_tensor_tensor(out=acc[j][:, n, :], in0=ps_y[e % 2][:, n, :],
                                                                  scalar=we[j][:, n, e:e + 1], in1=acc[j][:, n, :],
                                                                  op0=ALU.mult, op1=ALU.add)
                        last.then_inc(combined, 1)
                    dve.wait_ge(combined, g * NE + (NE + 2))
                    ln.moments(dve, acc[j], j, g)
                    dve.wait_ge(stored[j], it * 16 + 16)
                    ln.normalise(dve, acc[j], fin[j], j, g).then_inc(o_ready, 1)


_OUT_SHAPE = (64, 64, 128)


def kernel(**inputs):
    import numpy as _np
    import concourse.bacc as _bacc
    from concourse import mybir as _mybir
    from concourse.bass_utils import run_bass_kernel_spmd as _run

    nc = _bacc.Bacc("TRN2", target_bir_lowering=False, num_devices=1)
    arrays, args = {}, {}
    for name in inputs:
        v = _np.ascontiguousarray(inputs[name])
        arrays[f"in_{name}_dram"] = v
        args[name] = nc.dram_tensor(f"in_{name}_dram", v.shape, _mybir.dt.from_np(v.dtype), kind="ExternalInput").ap()
    out = nc.dram_tensor("out_0_dram", _OUT_SHAPE, F32, kind="ExternalOutput").ap()
    decoder_layer(nc, args, out)
    r = _run(nc, [arrays], core_ids=[0])
    return r.results[0]["out_0_dram"]
```
